# Optimizing a Trainium2 kernel written in Bass

```python
import numpy as np
import jax
import jax.numpy as jnp

def _softmax(x, axis=-1):
    return jax.nn.softmax(x, axis=axis)

def _gelu(x):
    return jax.nn.gelu(x, approximate=True)

def _silu(x):
    return jax.nn.silu(x)

def _sigmoid(x):
    return jax.nn.sigmoid(x)

def _layernorm(x, axis=-1, eps=1e-05):
    m = jnp.mean(x, axis=axis, keepdims=True)
    v = jnp.var(x, axis=axis, keepdims=True)
    return (x - m) / jnp.sqrt(v + eps)

def _scatter_add(tgt, idx, src, axis=0):
    return tgt.at[idx].add(src)

def _segment_sum(src, seg, n):
    return jax.ops.segment_sum(src, seg, n)
kernel_name = 'mk_gnn_ffn_d1_gnn_r8_20da40'

def setup_inputs(seed: int=0):
    np.random.seed(seed)
    _w = jnp.asarray

    def _rec_inputs():
        import jax
        import jax.numpy as jnp
        _gk = jax.random.key(seed)
        x = -6.415e-05 + 1 * jax.random.normal(jax.random.fold_in(_gk, 1), (1250, 512), jnp.float32)
        src = jax.random.randint(jax.random.fold_in(_gk, 2), (20000,), 0, 1250, jnp.int32)
        dst = jax.random.randint(jax.random.fold_in(_gk, 3), (20000,), 0, 1250, jnp.int32)
        _o = jnp.argsort(dst, stable=True)
        src = src[_o]
        dst = dst[_o]
        edge_weight1 = -0.00598325 + 0.997157 * jax.random.normal(jax.random.fold_in(_gk, 12), (20000, 1), jnp.float32)
        return (x, src, dst, edge_weight1)
    x, src, dst, edge_weight1 = _rec_inputs()

    def _L0_gnn_setup():
        import jax, jax.numpy as jnp
        import numpy as np
        N, D, E, L = (2500, 512, 20000, 4)
        BN_EPS = 1e-05

        def _gine_layer(x, src, dst, edge_attr, eps, We, be, W1, b1, gamma, beta, W2, b2):
            e = edge_attr @ We + be
            m = jax.nn.relu(x[src] + e)
            agg = jax.ops.segment_sum(m, dst, num_segments=x.shape[0])
            h = ((1.0 + eps) * x + agg) @ W1 + b1
            mu = jnp.mean(h, axis=0)
            var = jnp.mean(jnp.square(h - mu), axis=0)
            h = (h - mu) * jax.lax.rsqrt(var + BN_EPS) * gamma + beta
            h = jax.nn.relu(h)
            return jax.nn.relu(h @ W2 + b2)
        key = jax.random.key(seed)
        ks = jax.random.split(key, 10)
        x = jax.random.normal(ks[0], (N, D), dtype=jnp.float32)
        edge_index = jax.random.randint(ks[1], (2, E), 0, N, dtype=jnp.int64)
        edge_attr = jax.random.normal(ks[2], (E, 1), dtype=jnp.float32)
        s1 = 1.0 / np.sqrt(D)
        params = {'eps': jnp.zeros((L,), jnp.float32), 'We': jax.random.normal(ks[3], (L, 1, D), jnp.float32) * 1.0, 'be': jnp.zeros((L, D), jnp.float32), 'W1': jax.random.normal(ks[4], (L, D, D), jnp.float32) * s1, 'b1': jnp.zeros((L, D), jnp.float32), 'gamma': jnp.ones((L, D), jnp.float32), 'beta': jnp.zeros((L, D), jnp.float32), 'W2': jax.random.normal(ks[5], (L, D, D), jnp.float32) * s1, 'b2': jnp.zeros((L, D), jnp.float32)}
        return {'x': x, 'edge_index': edge_index, 'edge_attr': edge_attr, **params}
    _L0_gnn_all = _L0_gnn_setup()
    _L0_gnn_in = {k: v for k, v in _L0_gnn_all.items() if k in ('eps', 'We', 'be', 'W1', 'b1', 'gamma', 'beta', 'W2', 'b2')}
    del _L0_gnn_all

    def _L0_ffn_setup():
        import jax, jax.numpy as jnp
        import numpy as np
        E = 64
        K = 2
        D = 512
        H = 256
        NSH = 2
        ROUTE_SCALE = 2.5
        CAP = 1024
        STD = 0.02
        key = jax.random.key(seed)
        ks = jax.random.split(key, 8)
        x = jax.random.normal(ks[0], (4, 256, D), dtype=jnp.float32)
        gate_w = jax.random.normal(ks[1], (E, D), dtype=jnp.float32) * STD
        w1 = jax.random.normal(ks[2], (E, D, H), dtype=jnp.float32) * STD
        w3 = jax.random.normal(ks[3], (E, D, H), dtype=jnp.float32) * STD
        w2 = jax.random.normal(ks[4], (E, H, D), dtype=jnp.float32) * STD
        sw1 = jax.random.normal(ks[5], (D, H * NSH), dtype=jnp.float32) * STD
        sw3 = jax.random.normal(ks[6], (D, H * NSH), dtype=jnp.float32) * STD
        sw2 = jax.random.normal(ks[7], (H * NSH, D), dtype=jnp.float32) * STD
        return {'x': x, 'gate_w': gate_w, 'w1': w1, 'w3': w3, 'w2': w2, 'sw1': sw1, 'sw3': sw3, 'sw2': sw2}
    _L0_ffn_all = _L0_ffn_setup()
    _L0_ffn_in = {k: v for k, v in _L0_ffn_all.items() if k in ('gate_w', 'w1', 'w3', 'w2', 'sw1', 'sw3', 'sw2')}
    del _L0_ffn_all
    return {'x': x, 'src': src, 'dst': dst, 'edge_weight1': edge_weight1, 'L0_gnn_eps': _L0_gnn_in['eps'], 'L0_gnn_We': _L0_gnn_in['We'], 'L0_gnn_be': _L0_gnn_in['be'], 'L0_gnn_W1': _L0_gnn_in['W1'], 'L0_gnn_b1': _L0_gnn_in['b1'], 'L0_gnn_gamma': _L0_gnn_in['gamma'], 'L0_gnn_beta': _L0_gnn_in['beta'], 'L0_gnn_W2': _L0_gnn_in['W2'], 'L0_gnn_b2': _L0_gnn_in['b2'], 'L0_ffn_gate_w': _L0_ffn_in['gate_w'], 'L0_ffn_w1': _L0_ffn_in['w1'], 'L0_ffn_w3': _L0_ffn_in['w3'], 'L0_ffn_w2': _L0_ffn_in['w2'], 'L0_ffn_sw1': _L0_ffn_in['sw1'], 'L0_ffn_sw3': _L0_ffn_in['sw3'], 'L0_ffn_sw2': _L0_ffn_in['sw2']}

def reference(x, src, dst, edge_weight1, L0_gnn_eps, L0_gnn_We, L0_gnn_be, L0_gnn_W1, L0_gnn_b1, L0_gnn_gamma, L0_gnn_beta, L0_gnn_W2, L0_gnn_b2, L0_ffn_gate_w, L0_ffn_w1, L0_ffn_w3, L0_ffn_w2, L0_ffn_sw1, L0_ffn_sw3, L0_ffn_sw2):
    import jax
    import jax.numpy as jnp

    def _L0_gnn_ref(x, edge_index, edge_attr, eps, We, be, W1, b1, gamma, beta, W2, b2):
        import jax, jax.numpy as jnp
        import numpy as np
        N, D, E, L = (2500, 512, 20000, 4)
        BN_EPS = 1e-05

        def _gine_layer(x, src, dst, edge_attr, eps, We, be, W1, b1, gamma, beta, W2, b2):
            e = edge_attr @ We + be
            m = jax.nn.relu(x[src] + e)
            agg = jax.ops.segment_sum(m, dst, num_segments=x.shape[0])
            h = ((1.0 + eps) * x + agg) @ W1 + b1
            mu = jnp.mean(h, axis=0)
            var = jnp.mean(jnp.square(h - mu), axis=0)
            h = (h - mu) * jax.lax.rsqrt(var + BN_EPS) * gamma + beta
            h = jax.nn.relu(h)
            return jax.nn.relu(h @ W2 + b2)
        src, dst = (edge_index[0], edge_index[1])
        for l in range(L):
            x = _gine_layer(x, src, dst, edge_attr, eps[l], We[l], be[l], W1[l], b1[l], gamma[l], beta[l], W2[l], b2[l])
        return x

    def _L0_ffn_ref(x, gate_w, w1, w3, w2, sw1, sw3, sw2):
        import jax, jax.numpy as jnp
        import numpy as np
        E = 64
        K = 2
        D = 512
        H = 256
        NSH = 2
        ROUTE_SCALE = 2.5
        CAP = 1024
        STD = 0.02
        bs, slen, d = x.shape
        xf = x.reshape(-1, d)
        logits = xf @ gate_w.T
        scores = jax.nn.sigmoid(logits.astype(jnp.float32))
        top_scores, top_idx = jax.lax.top_k(scores, K)
        top_scores = top_scores / (top_scores.sum(-1, keepdims=True) + 1e-20)
        top_scores = top_scores * ROUTE_SCALE
        flat_e = top_idx.reshape(-1)
        x_pairs = jnp.repeat(xf, K, axis=0)
        oh = jax.nn.one_hot(flat_e, E, dtype=jnp.int32)
        pos = jnp.take_along_axis(jnp.cumsum(oh, axis=0), flat_e[:, None], axis=1)[:, 0] - 1
        buf = jnp.zeros((E, CAP, d), dtype=xf.dtype).at[flat_e, pos].set(x_pairs, mode='drop')
        h = jax.nn.silu(jnp.einsum('ecd,edh->ech', buf, w1)) * jnp.einsum('ecd,edh->ech', buf, w3)
        y = jnp.einsum('ech,ehd->ecd', h, w2)
        valid = (pos < CAP)[:, None]
        y_pairs = jnp.where(valid, y[flat_e, jnp.minimum(pos, CAP - 1)], 0.0)
        routed = (y_pairs.reshape(-1, K, d) * top_scores[..., None].astype(xf.dtype)).sum(axis=1)
        shared = jax.nn.silu(xf @ sw1) * (xf @ sw3) @ sw2
        return (shared + routed).reshape(bs, slen, d)
    edge_index = jnp.stack([src, dst])
    x = x + _L0_gnn_ref(_layernorm(x, axis=-1), edge_index, edge_weight1, L0_gnn_eps, L0_gnn_We, L0_gnn_be, L0_gnn_W1, L0_gnn_b1, L0_gnn_gamma, L0_gnn_beta, L0_gnn_W2, L0_gnn_b2)
    x = x + _L0_ffn_ref(_layernorm(x, axis=-1)[None], L0_ffn_gate_w, L0_ffn_w1, L0_ffn_w3, L0_ffn_w2, L0_ffn_sw1, L0_ffn_sw3, L0_ffn_sw2)[0]
    return x

_drawn_inputs = setup_inputs


def setup_inputs(seed=0):
    import zlib

    import numpy as np

    out = dict(_drawn_inputs(seed))
    spreads = {'L0_gnn_eps': (0.0, 0.8),
     'L0_gnn_be': (0.0, 0.1),
     'L0_gnn_b1': (0.0, 0.8),
     'L0_gnn_gamma': (1.0, 0.2),
     'L0_gnn_beta': (0.0, 0.1),
     'L0_gnn_b2': (0.0, 0.1)}
    factors = {}
    for name, (base, spread) in spreads.items():
        noise = np.random.default_rng([zlib.crc32(name.encode()), seed]).standard_normal(out[name].shape)
        drawn = base * np.exp(spread * noise) if base else spread * noise
        out[name] = jnp.asarray(drawn.astype(out[name].dtype))
    for name, factor in factors.items():
        out[name] = (out[name] * factor).astype(out[name].dtype)
    return out
```

```python
import concourse.bass as bass
from concourse import mybir
from contextlib import ExitStack

F32, BF16 = mybir.dt.float32, mybir.dt.bfloat16
I32, U32 = mybir.dt.int32, mybir.dt.uint32
ALU = mybir.AluOpType
ACT = mybir.ActivationFunctionType
AX = mybir.AxisListType

P = 128
N, D, E, L = 1250, 512, 20000, 4
NT = -(-N // P)
NP = NT * P
LAST = N - (NT - 1) * P
KC = D // P
EP = 125
EC = E // EP
BN_EPS = LN_EPS = 1e-5

HB = NT // 2
HALF_MAX = (E - 1) // P + 1 + HB - 1
MAIN = [-(-E * HB * P // N // P) + HB // 2 + 1 + 3, -(-E * (N - HB * P) // N // P) + HB // 2 + 3]
MT = sum(MAIN)
RING = 8
assert MT % RING == 0
OVER = [HALF_MAX - m for m in MAIN]
OV0 = [MT + RING, MT + RING + OVER[0]]
COLS = MT + RING + sum(OVER)
B_AT = 1024
ROWS = 160
RROWS = ROWS * NT + 16
NX, KX, HX = 64, 2, 256
CAP = 1024
SCALE = 2.5
XOVER = (N * KX - 1) // P
XT = NX + XOVER
XC = HX // P
WR = 4
REC = 4


class Chain:

    def __init__(self, engine, sem):
        self.engine, self.sem, self.base, self.n = engine, sem, 0, 0

    def __call__(self, instruction):
        self.mark(instruction)
        self.wait()

    def mark(self, instruction):
        instruction.then_inc(self.sem, 1)
        self.n += 1

    def count(self):
        return self.base + self.n

    def wait(self):
        self.engine.wait_ge(self.sem, self.count())

    def enter(self, i, per):
        self.before, self.per = self.base + self.n, per
        self.base, self.n = self.before + i * per, 0

    def leave(self, rounds):
        assert self.n == self.per, (self.n, self.per)
        self.base, self.n = self.before + rounds * self.per, 0


def at_least(engine, sem, value):
    if not isinstance(value, int) or value > 0:
        engine.wait_ge(sem, value)


def build(nc, x, src, dst, ew, eps, We, be, W1, b1, gamma, beta, W2, b2,
          gate_w, xw1, xw3, xw2, sw1, sw3, sw2, out, scratch):
    xb_dram, rec_dram, xn_dram, tok_dram, y_dram = scratch
    with ExitStack() as ctx:
        def sb(name, shape, dt=F32):
            return ctx.enter_context(nc.sbuf_tensor(name, shape, dt))

        def sem(name):
            return ctx.enter_context(nc.semaphore(name))

        def inside(buffer, layout):
            at, views = 0, []
            for parts, dims, dt in layout:
                n = 1
                for d in dims:
                    n *= d
                v = buffer[0:parts, at:at + n]
                at += n
                if dt is not F32:
                    v = v.bitcast(dt)
                if len(dims) > 1:
                    names = "abcd"[:len(dims)]
                    v = v.rearrange(f"p ({' '.join(names)}) -> p {' '.join(names)}", **dict(zip(names, dims)))
                views.append(v)
            return views

        turned = sb("turned", [P, KC * NP])
        hidden_ = sb("hidden_", [P, KC * NP])
        flight = sb("flight", [P, RING * D])
        rows = sb("rows", [P, 3 * D])
        mixed = sb("mixed", [P, KC * D])
        [hinT] = inside(turned, [(P, (KC, NP), F32)])
        [h1T] = inside(hidden_, [(P, (KC, NP), F32)])
        [ring] = inside(flight, [(P, (RING, D), F32)])
        web, beb, b2b = inside(rows, [(P, (D,), F32)] * 3)
        oneh, stage = inside(mixed, [(P, (RING, P), F32), (P, (2, D), F32)])
        [w3s] = inside(mixed, [(P, (KC, D), F32)])
        [cmpx] = inside(rows, [(P, (XOVER, NX), F32)])
        srcE, dstE, ewE, buckI, buckE, slotF, slotT, slotI, recE, memb, cumu = inside(
            turned, [(EP, (EC,), t) for t in (I32, I32, F32, I32, F32, F32, F32, U32)]
            + [(EP, (EC, REC), F32), (EP, (NT, EC), F32), (EP, (NT, EC), F32)])
        vrow, brow, rrow, tmpc, padrec = inside(
            hidden_, [(P, (COLS,), F32)] * 4 + [(P, (P, REC), F32)])
        [vrow0] = inside(rows, [(1, (COLS,), F32)])
        lg, both, run, pos, slotm, oh0 = inside(
            flight, [(P, (NT, NX), F32), (P, (NT, NX), F32), (P, (NT + 1, NX), F32)] + [(P, (NT, NX), F32)] * 3)
        oh = [oh0, sb("oh1", [P, NT, NX])]
        xeT, sg, hh, hT, ysb = inside(
            hidden_, [(P, (2, KC, P), F32), (P, (2, HX), F32), (P, (2, HX), F32), (P, (2, XC, P), F32), (P, (WR, D), F32)])
        ident = sb("ident", [P, P])
        below = sb("below", [P, P])
        ones = sb("ones", [P, P])
        zeros_h = sb("zeros_h", [P, D], BF16)
        lane = sb("lane", [P, P])
        vrows = sb("vrows", [3 * L * KC, P])
        vecs = sb("vecs", [P, 3, L, KC])
        zrow = sb("zrow", [P, EC])
        rowtot = sb("rowtot", [EP, NT])
        prior = sb("prior", [EP, NT])
        cnt = sb("cnt", [P, NT])
        cntI = sb("cntI", [P, NT], I32)
        tiles = sb("tiles", [P, NT])
        TS = sb("TS", [P, NT])
        Dd = sb("Dd", [P, NT + 1])
        DD = sb("DD", [P, NT])
        bankI = sb("bankI", [P, COLS], I32)
        NCH = -(-COLS // P)
        rowsel = sb("rowsel", [P, NCH], U32)
        idxT = sb("idxT", [P, COLS], U32)
        wT = sb("wT", [P, COLS])
        dloc = sb("dloc", [P, COLS])
        rec4 = sb("rec4", [EP, 4, REC])
        idx4 = sb("idx4", [EP, 4], U32)
        xs = sb("xs", [P, NT, D])
        hin = sb("hin", [P, NT, D])
        w1s = sb("w1s", [P, KC, D])
        w2s = sb("w2s", [P, KC, D])
        vec = sb("vec", [P, 3, KC])
        epsb = sb("epsb", [P, L])
        cur = sb("cur", [P, RING], U32)
        st = sb("st", [P, NT, 6])
        mv = sb("mv", [P, NT, 2])
        t0 = sb("t0", [P, NT])
        t1 = sb("t1", [P, NT])
        t2 = sb("t2", [P, NT])
        bst = sb("bst", [P, KC, 4, 6])
        bmv = sb("bmv", [P, KC, 2])
        bve = sb("bve", [P, KC])
        bsq = sb("bsq", [P, KC])
        brs = sb("brs", [P, KC])
        bt = sb("bt", [P, KC])
        bscale = sb("bscale", [P, KC])
        bshift = sb("bshift", [P, KC])
        ovx = sb("ovx", [P, D])
        ovh = sb("ovh", [P, P])
        ovi = sb("ovi", [P, 1], U32)
        flagI = sb("flagI", [1, 2], I32)

        gw = sb("gw", [NX, D])
        gT = sb("gT", [P, KC, NX])
        valid = sb("valid", [P, 1])
        m8 = sb("m8", [P, NT, 8])
        i8 = sb("i8", [P, NT, 8], U32)
        i8f = sb("i8f", [P, NT, 8])
        cntx = sb("cntx", [P, NX])
        ovn = sb("ovn", [P, NX])
        ovnI = sb("ovnI", [P, NX], I32)
        ovs = sb("ovs", [P, NX])
        b128 = sb("b128", [P, NX])
        bdif = sb("bdif", [P, NX])
        sel = sb("sel", [P, KX, NT])
        selp = sb("selp", [P, KX, NT])
        selI = sb("selI", [P, KX, NT], I32)
        hiI = sb("hiI", [P, KX, NT], I32)
        slotx = sb("slotx", [P, KX, NT], U32)
        tabx = sb("tabx", [P, KX, NT], U32)
        tokid = sb("tokid", [P, NT], I32)
        tokT = sb("tokT", [P, XT], I32)
        ztab = sb("ztab", [P, XT], I32)
        sgm = sb("sgm", [P, NT, KX])
        gden = sb("gden", [P, NT])
        gate = sb("gate", [P, KX, NT])
        eovF = sb("eovF", [P, XOVER])
        eovI = sb("eovI", [P, XOVER], I32)
        nov = sb("nov", [P, 1], I32)
        shsig = sb("shsig", [P, 2, 320])
        w13 = sb("w13", [P, WR, KC, 2, HX])
        w2e = sb("w2e", [P, WR, XC, D])
        icur = sb("icur", [P, WR], I32)
        xe = ring[:, 0:WR, :]

        ps = ctx.enter_context(nc.psum_tensor("ps", [P, 8, D], F32))

        s_idle = sem("idle")
        s_const = sem("constants")
        s_zro = sem("zero_bf16")
        s_ldx = sem("x_loaded")
        s_lde = sem("edges_loaded")
        s_padm = sem("pad_records_made")
        s_padw = sem("pad_records_stored")
        s_slot = sem("slots_known")
        s_rot = sem("row_totals_known")
        s_cntp = sem("counts_summed")
        s_rowp = sem("row_numbers_known")
        s_rowt = sem("row_numbers_turned")
        s_rsel = sem("row_numbers_ready")
        s_c4 = sem("pool_copies")
        s_scat = sem("records_scattered")
        s_rowg = sem("record_rows_gathered")
        s_plane = sem("record_planes_turned")
        s_tab = sem("tile_tables_ready")
        s_dve = sem("dve_chain")
        s_act = sem("act_chain")
        s_ln = sem("layernorm_sums")
        s_lnq = sem("layernorm_roots")
        s_wl = sem("layer_weights_loaded")
        s_ldv = sem("vectors_loaded")
        s_vt = sem("vectors_turned")
        s_vec = sem("layer_vectors_ready")
        s_sg = sem("staged")
        s_sw = [sem("stage_stored0"), sem("stage_stored1")]
        s_first = sem("first_indices")
        s_g = [sem(f"gathered{k}") for k in range(RING)]
        s_y = sem("messages_summed")
        s_m = sem("messages_ready")
        s_free = sem("ring_slots_free")
        s_zero = sem("acc_zeroed")
        s_hin = sem("aggregate_read")
        s_tr = sem("bank_filled")
        s_ra = sem("bank_read_by_act")
        s_rd = sem("bank_read_by_dve")
        s_var = sem("bn_variance")
        s_root = sem("bn_root")
        s_bn = sem("bn_ready")
        s_gt = sem("hidden_ready")
        s_xs = sem("x_relu")
        s_og = [sem(f"over_gathered{h}") for h in range(2)]
        s_oi = [sem(f"over_index{h}") for h in range(2)]
        s_oy = [sem(f"over_summed{h}") for h in range(2)]
        s_om = [sem(f"over_message{h}") for h in range(2)]
        s_ou = [sem(f"over_used{h}") for h in range(2)]
        s_gw = sem("gate_loaded")
        s_gt4 = sem("gate_turned")
        s_gT = sem("gate_ready")
        s_ztab = sem("token_table_zero")
        s_ztw = sem("token_table_cleared")
        s_swl = sem("shared_weights_loaded")
        s_xn = sem("tokens_normed")
        s_xnw = sem("tokens_stored")
        s_tr2 = sem("tokens_turned")
        s_ra2 = sem("turned_tokens_read")
        s_lg = sem("logits")
        s_gat = sem("top_scores")
        s_sgm = sem("top_sigmoids")
        s_run = sem("expert_members")
        s_pos = sem("expert_ranks")
        s_tabx = sem("token_slots")
        s_scx = sem("tokens_scattered")
        s_tok = sem("token_table_loaded")
        s_xrt = sem("expert_tables_ready")
        s_sp = sem("shared_products")
        s_ssg = sem("shared_sigmoids")
        s_shh = sem("shared_hidden")
        s_so = sem("shared_out")
        s_sod = sem("shared_added")
        s_ic = sem("expert_indices")
        s_w = [sem(f"expert_weights{k}") for k in range(WR)]
        s_xg = [sem(f"tokens_gathered{k}") for k in range(WR)]
        s_tx = sem("x_turned")
        s_xt = sem("xT_ready")
        s_g1 = sem("up_products")
        s_sig = sem("sigmoids")
        s_hh = sem("hidden")
        s_hm = sem("hidden_half")
        s_th = sem("hidden_turned")
        s_ht = sem("hiddenT_ready")
        s_g2 = sem("down_products")
        s_yc = sem("y_copied")
        s_ys = [sem(f"y_stored{k}") for k in range(WR)]
        s_yz = sem("over_rows_cleared")
        s_vw = sem("over_weights")
        s_vg = sem("over_tokens")
        s_vi = sem("over_token_index")
        s_vp = sem("over_pe")
        s_va = sem("over_act")
        s_vd = sem("over_dve")
        s_vs = sem("over_y_stored")
        s_yg = [sem(f"y_gathered{k}") for k in range(RING)]
        s_fa = sem("combined")
        s_fa2 = sem("y_added")
        s_out = sem("out_stored")
        s_fin = sem("final_sum")

        def hold(engine, s, value):
            engine.wait_ge(s, value)
            engine.sem_inc(s_idle, 1)

        def halves(l):
            return [(h, sum(MAIN[:h]), MAIN[h] // RING, MAIN[h] % RING) for h in range(2)]

        block = ctx.enter_context(nc.Block())

        @block.sync
        def _(sp):
            xr = x[0:(NT - 1) * P, :].rearrange("(t p) d -> p t d", p=P)
            sp.dma_start(dstE[:, :], dst.rearrange("(p c) -> p c", p=EP)).then_inc(s_lde, 16)
            sp.dma_start(srcE[:, :], src.rearrange("(p c) -> p c", p=EP)).then_inc(s_lde, 16)
            sp.dma_start(ewE[:, :], ew.rearrange("(p c) o -> p (c o)", p=EP)).then_inc(s_lde, 16)
            for v, a in enumerate((b1, gamma, beta)):
                sp.dma_start(vrows[v * L * KC:(v + 1) * L * KC, :], a.rearrange("l (c p) -> (l c) p", p=P)).then_inc(s_ldv, 16)
            sp.wait_ge(s_const, 1)
            sp.dma_start(hin[:, 0:NT - 1, :], xr).then_inc(s_ldx, 16)
            sp.dma_start(hin[0:LAST, NT - 1, :], x[(NT - 1) * P:N, :]).then_inc(s_ldx, 16)
            sp.dma_start(epsb[:, :], eps.partition_broadcast(P)).then_inc(s_ldx, 16)
            sp.wait_ge(s_padm, 1)
            full = RROWS // P
            sp.dma_start(rec_dram[0:full * P, :].rearrange("(r p) c -> p r c", p=P),
                         padrec[:, :, :].rearrange("p a b -> p (a b)").unsqueeze(1).broadcast_to([P, full, P * REC])
                         ).then_inc(s_padw, 16)
            sp.dma_start(rec_dram[full * P:RROWS, :],
                         padrec[0:RROWS - full * P, :, :].rearrange("p a b -> p (a b)")).then_inc(s_padw, 16)
            sp.dma_start(gw[:, :], gate_w).then_inc(s_gw, 16)
            sp.wait_ge(s_ztab, 1)
            sp.dma_start(tok_dram.rearrange("(p j) o -> p (j o)", p=P), ztab[:, :]).then_inc(s_ztw, 16)

            def load_expert(e, k, done):
                sp.dma_start(w13[:, k, :, 0, :], xw1[bass.ds(e, 1), :, :].rearrange("o (p k) n -> (o p) k n", k=KC)).then_inc(done, 16)
                sp.dma_start(w13[:, k, :, 1, :], xw3[bass.ds(e, 1), :, :].rearrange("o (p k) n -> (o p) k n", k=KC)).then_inc(done, 16)
                sp.dma_start(w2e[:, k, :, :], xw2[bass.ds(e, 1), :, :].rearrange("o (p k) n -> (o p) k n", k=XC)).then_inc(done, 16)

            sp.wait_ge(s_zro, 1)
            sp.dma_start(y_dram[NX * P:XT * P, :].rearrange("(p t) (a c) -> p (t a) c", p=P, a=2),
                         zeros_h[:, :].bitcast(F32).unsqueeze(1).broadcast_to([P, XOVER * 2, D // 2])).then_inc(s_yz, 16)
            for e in range(WR):
                load_expert(e, e, s_w[e])
            with sp.Fori(0, L) as l:
                hold(sp, s_rd, 10 + l * NT)
                sp.dma_start(w1s[:, :, :], W1[bass.ds(l, 1), :, :].rearrange("o (p k) n -> (o p) k n", k=KC)).then_inc(s_wl, 16)
                sp.dma_start(w2s[:, :, :], W2[bass.ds(l, 1), :, :].rearrange("o (k p) n -> p (o k) n", p=P)).then_inc(s_wl, 16)
                sp.dma_start(web[:, :], We[bass.ds(l, 1), 0, :].rearrange("o d -> (o d)").partition_broadcast(P)).then_inc(s_wl, 16)
                sp.dma_start(beb[:, :], be[bass.ds(l, 1), :].rearrange("o d -> (o d)").partition_broadcast(P)).then_inc(s_wl, 16)
                sp.dma_start(b2b[:, :], b2[bass.ds(l, 1), :].rearrange("o d -> (o d)").partition_broadcast(P)).then_inc(s_wl, 16)
                for t in range(NT):
                    hold(sp, s_sg, l * NT + t + 1)
                    sp.dma_start(xb_dram[t * P:(t + 1) * P, :], stage[:, t % 2, :]).then_inc(s_sw[t % 2], 16)
            sp.wait_ge(s_rd, 10 + L * NT)
            sp.dma_start(hin[:, 0:NT - 1, :], xr).then_inc(s_ldx, 16)
            sp.dma_start(hin[0:LAST, NT - 1, :], x[(NT - 1) * P:N, :]).then_inc(s_ldx, 16)
            sp.dma_start(w1s[:, :, :], sw1.rearrange("(p k) n -> p k n", k=KC)).then_inc(s_swl, 16)
            sp.dma_start(w3s[:, :, :], sw3.rearrange("(p k) n -> p k n", k=KC)).then_inc(s_swl, 16)
            sp.dma_start(w2s[:, :, :], sw2.rearrange("(k p) n -> p k n", p=P)).then_inc(s_swl, 16)
            for t in range(NT):
                sp.wait_ge(s_xn, t + 1)
                sp.dma_start(xn_dram[t * P:(t + 1) * P, :], hin[:, t, :]).then_inc(s_xnw, 16)
            sp.wait_ge(s_scx, 16 * KX * NT)
            sp.dma_start(tokT[:, :], tok_dram.rearrange("(p j) o -> p (j o)", p=P)).then_inc(s_tok, 16)

            def store_y(j, k):
                at_least(sp, s_yc, j + 1)
                sp.dma_start(y_dram[bass.ds(j * P, P), :], ysb[:, k, :]).then_inc(s_ys[k], 16)

            def expert_traffic(j, k):
                sp.wait_ge(s_g2, j - WR + 1)
                load_expert(j, k, s_w[k])
                if not isinstance(j, int) or j > WR:
                    store_y(j - WR - 1, (k - 1) % WR)

            for k in range(WR):
                expert_traffic(WR + k, k)
            with sp.Fori(2, NX // WR) as g:
                for k in range(WR):
                    expert_traffic(g * WR + k, k)
            for j in range(NX - WR - 1, NX):
                store_y(j, j % WR)
            sp.wait_ge(s_xrt, 1)
            sp.wait_ge(s_yz, 16)
            over = sp.value_load(nov[0:1, 0:1], min_val=0, max_val=XOVER)
            with sp.If(over > 0):
                def traffic(o):
                    at_least(sp, s_va, o * 3)
                    e = sp.value_load(eovI[0:1, bass.ds(o, 1)], min_val=0, max_val=NX - 1)
                    load_expert(e, 0, s_vw)
                    sp.wait_ge(s_va, o * 3 + 3)
                    sp.dma_start(y_dram[bass.ds((o + NX) * P, P), :], ysb[:, 0, :]).then_inc(s_vs, 16)

                traffic(0)
                with sp.Fori(1, XOVER) as o:
                    traffic(o)
            for t in range(NT):
                sp.wait_ge(s_fa, t + 1)
                n = min(P, N - t * P)
                sp.dma_start(out[t * P:t * P + n, :], xs[0:n, t, :]).then_inc(s_out, 16)
            sp.wait_ge(s_out, 16 * NT)

        @block.gpsimd
        def _(pool):
            nc.gpsimd.memset(hin[:, NT - 1, :], 0.0).then_inc(s_const, 1)
            nc.gpsimd.memset(padrec[:, :, :], 0.0).then_inc(s_c4, 1)
            pool.wait_ge(s_c4, 1)
            nc.gpsimd.memset(padrec[:, :, 1], 65536.0).then_inc(s_padm, 1)
            nc.gpsimd.memset(ones[:, :], 1.0).then_inc(s_c4, 1)
            nc.gpsimd.memset(ident[:, :], 0.0).then_inc(s_c4, 1)
            pool.wait_ge(s_c4, 3)
            nc.gpsimd.affine_select(out=below[:, :], in_=ones[:, :], compare_op=ALU.is_gt, fill=0.0, base=0,
                                    pattern=[[1, P]], channel_multiplier=-1).then_inc(s_const, 1)
            nc.gpsimd.affine_select(out=ident[:, :], in_=ident[:, :], compare_op=ALU.not_equal, fill=1.0, base=0,
                                    pattern=[[-1, P]], channel_multiplier=1).then_inc(s_const, 1)
            nc.gpsimd.iota(lane[:, :], [[1, P]], base=0, channel_multiplier=0,
                           allow_small_or_imprecise_dtypes=True).then_inc(s_const, 1)
            for a, n, v in ((0, MAIN[0], 0), (MAIN[0], MAIN[1], B_AT), (MT, RING, 0),
                            (OV0[0], OVER[0], MAIN[0]), (OV0[1], OVER[1], B_AT + MAIN[1])):
                nc.gpsimd.iota(vrow[:, a:a + n], [[1, n]], base=v, channel_multiplier=0,
                               allow_small_or_imprecise_dtypes=True).then_inc(s_const, 1)
            nc.gpsimd.affine_select(out=valid[:, :], in_=ones[:, 0:1], compare_op=ALU.is_gt, fill=0.0, base=LAST,
                                    pattern=[[0, 1]], channel_multiplier=-1).then_inc(s_const, 1)
            nc.gpsimd.iota(tokid[:, :], [[P, NT]], base=0, channel_multiplier=1).then_inc(s_const, 1)
            pool.wait_ge(s_slot, 1)
            pool.wait_ge(s_padw, 32)
            recs = rec_dram.rearrange("r (e c) -> (r e) c", c=REC)

            def scatter(i):
                nc.gpsimd.tensor_copy(rec4[:, :, :], recE[:, bass.ds(i * 4, 4), :]).then_inc(s_c4, 1)
                nc.gpsimd.tensor_copy(idx4[:, :], slotI[:, bass.ds(i * 4, 4)]).then_inc(s_c4, 1)
                hold(pool, s_c4, i * 2 + 5)
                for k in range(4):
                    pool.indirect_dma_start(recs, bass.IndirectOffsetOnAxis(ap=idx4[:, k:k + 1], axis=0),
                                            rec4[:, k, :], None).then_inc(s_scat, 16)

            scatter(0)
            with pool.Fori(1, EC // 4) as i:
                hold(pool, s_scat, 64 * i)
                scatter(i)
            pool.wait_ge(s_rsel, NCH)
            pool.wait_ge(s_scat, 64 * (EC // 4))
            for c in range(NCH):
                n = min(P, COLS - c * P)
                pool.indirect_dma_start(ring[0:n, c, :], None, rec_dram,
                                        bass.IndirectOffsetOnAxis(ap=rowsel[0:n, c:c + 1], axis=0)).then_inc(s_rowg, 16)
            pool.wait_ge(s_tab, 1)
            needed = [pool.value_load(flagI[0:1, h:h + 1], min_val=0, max_val=HALF_MAX) for h in range(2)]
            with pool.Fori(0, L) as l:
                hold(pool, s_sw[0], (l + 1) * (NT // 2) * 16)
                hold(pool, s_sw[1], (l + 1) * (NT // 2) * 16)

                def gather(t, k):
                    hold(pool, s_free, l * MT + t + 1)
                    pool.indirect_dma_start(ring[:, k, :], None, xb_dram,
                                            bass.IndirectOffsetOnAxis(ap=cur[:, k:k + 1], axis=0)).then_inc(s_g[k], 16)

                for h, first, groups, rest in halves(l):
                    with pool.Fori(0, groups) as g:
                        for k in range(RING):
                            gather(first + g * RING + k, (first + k) % RING)
                    for k in range(rest):
                        gather(first + groups * RING + k, (first + k) % RING)
                    with pool.If(needed[h] > MAIN[h]):
                        with pool.Fori(0, OVER[h]) as o:
                            hold(pool, s_ou[h], l * OVER[h] + o + 1)
                            nc.gpsimd.tensor_copy(ovi[:, :], idxT[:, bass.ds(o + OV0[h], 1)]).then_inc(s_oi[h], 1)
                            hold(pool, s_oi[h], l * OVER[h] + o + 1)
                            pool.indirect_dma_start(ovx[:, :], None, xb_dram,
                                                    bass.IndirectOffsetOnAxis(ap=ovi[:, :], axis=0)).then_inc(s_og[h], 16)
            pool.wait_ge(s_ztw, 16)
            pool.wait_ge(s_tabx, 1)
            for k in range(KX):
                for t in range(NT):
                    n = min(P, N - t * P)
                    pool.indirect_dma_start(tok_dram, bass.IndirectOffsetOnAxis(ap=tabx[0:n, k, t:t + 1], axis=0),
                                            tokid[0:n, t:t + 1], None).then_inc(s_scx, 16)
            pool.wait_ge(s_tok, 16)
            pool.wait_ge(s_xnw, 16 * NT)

            def tokens(g):
                if not isinstance(g, int):
                    hold(pool, s_tx, g * WR)
                nc.gpsimd.tensor_copy(icur[:, :], tokT[:, bass.ds(g * WR, WR)]).then_inc(s_ic, 1)
                hold(pool, s_ic, g + 1)
                for k in range(WR):
                    pool.indirect_dma_start(xe[:, k, :], None, xn_dram,
                                            bass.IndirectOffsetOnAxis(ap=icur[:, k:k + 1], axis=0)).then_inc(s_xg[k], 16)

            tokens(0)
            with pool.Fori(1, NX // WR) as g:
                tokens(g)
            pool.wait_ge(s_xrt, 1)
            over = pool.value_load(nov[0:1, 0:1], min_val=0, max_val=XOVER)
            with pool.If(over > 0):
                pool.wait_ge(s_tx, NX)

                def over_tokens(o):
                    if not isinstance(o, int):
                        hold(pool, s_vp, o * 4)
                    nc.gpsimd.tensor_copy(icur[:, 0:1], tokT[:, bass.ds(o + NX, 1)]).then_inc(s_vi, 1)
                    hold(pool, s_vi, o + 1)
                    pool.indirect_dma_start(xe[:, 0, :], None, xn_dram,
                                            bass.IndirectOffsetOnAxis(ap=icur[:, 0:1], axis=0)).then_inc(s_vg, 16)

                over_tokens(0)
                with pool.Fori(1, XOVER) as o:
                    over_tokens(o)
                pool.wait_ge(s_vs, 16 * XOVER)
            pool.wait_ge(s_tx, NX)
            for k in range(WR):
                pool.wait_ge(s_ys[k], 16 * (NX // WR))
            for u in range(KX * NT):
                at_least(pool, s_fa2, u - RING + 1)
                n = min(P, N - u // KX * P)
                pool.indirect_dma_start(ring[0:n, u % RING, :], None, y_dram,
                                        bass.IndirectOffsetOnAxis(ap=slotx[0:n, u % KX, u // KX:u // KX + 1], axis=0)
                                        ).then_inc(s_yg[u % RING], 16)

        @block.scalar
        def _(act):
            chain = Chain(act, s_act)
            act.wait_ge(s_ln, 1)
            nc.scalar.activation(t1[:, :], t0[:, :], ACT.Sqrt).then_inc(s_lnq, 1)
            act.wait_ge(s_tab, 3)
            nc.scalar.copy(cur[:, :], idxT[:, 0:RING]).then_inc(s_first, 1)
            act.wait_ge(s_first, 1)
            act.sem_inc(s_free, RING)
            needed = [act.value_load(flagI[0:1, h:h + 1], min_val=0, max_val=HALF_MAX) for h in range(2)]
            with act.Fori(0, L) as l:
                def message(t, k):
                    act.wait_ge(s_y, (l * MT + t + 1) * 2)
                    nc.scalar.activation(ring[:, k, :], ring[:, k, :], ACT.Relu).then_inc(s_m, 1)
                    nc.scalar.copy(cur[:, k:k + 1], idxT[:, bass.ds(t + RING, 1)]).then_inc(s_m, 1)

                use = 0
                for h, first, groups, rest in halves(l):
                    with act.Fori(0, groups) as g:
                        for k in range(RING):
                            message(first + g * RING + k, (first + k) % RING)
                    for k in range(rest):
                        message(first + groups * RING + k, (first + k) % RING)
                    with act.If(needed[h] > MAIN[h]):
                        with act.Fori(0, OVER[h]) as o:
                            act.wait_ge(s_oy[h], (l * OVER[h] + o + 1) * 2)
                            nc.scalar.activation(ovx[:, :], ovx[:, :], ACT.Relu).then_inc(s_om[h], 1)
                    for t in range(HB):
                        act.wait_ge(s_tr, l * 36 + use + 1)
                        nc.scalar.copy(hinT[:, :, (h * HB + t) * P:(h * HB + t + 1) * P],
                                       ps[:, 5 + use % 3, :].rearrange("p (k n) -> p k n", k=KC)).then_inc(s_ra, 1)
                        use += 1
                    if h == 0:
                        hold(act, s_vec, l + 1)
                    for q in range(2):
                        for c in range(KC):
                            act.wait_ge(s_tr, l * 36 + use + 1)
                            a = h * HB * P + q * 320
                            nc.scalar.activation(h1T[:, c, a:a + 320], ps[:, 5 + use % 3, 0:320], ACT.Identity,
                                                 bias=vec[:, 0, c:c + 1]).then_inc(s_ra, 1)
                            use += 1
                act.wait_ge(s_var, l + 1)
                nc.scalar.activation(bsq[:, :], bve[:, :], ACT.Sqrt).then_inc(s_root, 1)
                act.wait_ge(s_bn, l + 1)
                for q in range(4):
                    for c in range(KC):
                        v = h1T[:, c, q * 320:(q + 1) * 320]
                        nc.scalar.activation(v, v, ACT.Relu, bias=bshift[:, c:c + 1],
                                             scale=bscale[:, c:c + 1]).then_inc(s_gt, 1)
                for t in range(NT):
                    act.wait_ge(s_rd, 10 + l * NT + t + 1)
                    nc.scalar.activation(xs[:, t, :], xs[:, t, :], ACT.Relu).then_inc(s_xs, 1)
            act.wait_ge(s_ln, 2)
            nc.scalar.activation(t1[:, :], t0[:, :], ACT.Sqrt).then_inc(s_lnq, 1)
            for t in range(NT):
                act.wait_ge(s_tr2, t + 1)
                nc.scalar.copy(hinT[:, :, t * P:(t + 1) * P],
                               ps[:, 5 + t % 3, :].rearrange("p (k n) -> p k n", k=KC)).then_inc(s_ra2, 1)
            act.wait_ge(s_gat, 1)
            nc.scalar.activation(sgm[:, :, :], m8[:, :, 0:KX], ACT.Sigmoid).then_inc(s_sgm, 1)
            for u in range(16):
                act.wait_ge(s_sp, u + 1)
                at_least(act, s_shh, u - 1)
                nc.scalar.activation(shsig[:, u % 2, :], ps[:, 4 + u % 2 * 2, 0:320], ACT.Sigmoid).then_inc(s_ssg, 1)

            def turned(j, k):
                act.wait_ge(s_tx, j + 1)
                at_least(act, s_g1, j - 1)
                nc.scalar.copy(xeT[:, k % 2, :, :].rearrange("p k n -> p (k n)"), ps[:, k % 2, :]).then_inc(s_xt, 1)

            def sigmoid(j, k):
                act.wait_ge(s_g1, j + 1)
                at_least(act, s_hh, j - 1)
                nc.scalar.activation(sg[:, k % 2, :], ps[:, 2 + k % 2, 0:HX], ACT.Sigmoid).then_inc(s_sig, 1)

            def result(j, k, turn):
                act.wait_ge(s_g2, j + 1)
                at_least(act, s_ys[k], turn * 16)
                nc.scalar.copy(ysb[:, k, :], ps[:, 6 + k % 2, :]).then_inc(s_yc, 1)

            def step(g, k):
                j = g * WR + k
                static = isinstance(j, int)
                if not static or j < NX:
                    sigmoid(j, k)
                if not static or j >= 2:
                    result(j - 2, (k - 2) % WR, g + (k - 2) // WR)
                if not static or j + 1 < NX:
                    turned(j + 1, (k + 1) % WR)

            turned(0, 0)
            for k in range(WR):
                step(0, k)
            with act.Fori(1, NX // WR - 1) as g:
                for k in range(WR):
                    step(g, k)
            for k in range(WR + 2):
                step(NX // WR - 1 + k // WR, k % WR)
            act.wait_ge(s_xrt, 1)
            over = act.value_load(nov[0:1, 0:1], min_val=0, max_val=XOVER)
            with act.If(over > 0):
                act.wait_ge(s_ys[0], 16 * (NX // WR))

                def over_act(o):
                    act.wait_ge(s_vp, o * 4 + 1)
                    nc.scalar.copy(xeT[:, 0, :, :].rearrange("p k n -> p (k n)"), ps[:, 0, :]).then_inc(s_va, 1)
                    act.wait_ge(s_vp, o * 4 + 2)
                    nc.scalar.activation(sg[:, 0, :], ps[:, 2, 0:HX], ACT.Sigmoid).then_inc(s_va, 1)
                    act.wait_ge(s_vp, o * 4 + 4)
                    at_least(act, s_vs, o * 16)
                    nc.scalar.copy(ysb[:, 0, :], ps[:, 6, :]).then_inc(s_va, 1)

                over_act(0)
                with act.Fori(1, XOVER) as o:
                    over_act(o)

        @block.vector
        def _(dve):
            chain = Chain(dve, s_dve)
            V = nc.vector

            def rsqrt_step():
                chain(V.reciprocal(t1[:, :], t1[:, :]))
                chain(V.tensor_tensor(t2[:, :], t1[:, :], t1[:, :], ALU.mult))
                chain(V.tensor_tensor(t2[:, :], t2[:, :], t0[:, :], ALU.mult))
                chain(V.tensor_scalar(t2[:, :], t2[:, :], -0.5, 1.5, ALU.mult, ALU.add))
                chain(V.tensor_tensor(t1[:, :], t1[:, :], t2[:, :], ALU.mult))

            V.memset(zeros_h[:, :], 0.0).then_inc(s_zro, 1)
            V.memset(ztab[:, :], 0).then_inc(s_ztab, 1)
            chain(V.memset(zrow[:, :], 0.0))
            dve.wait_ge(s_lde, 48)
            chain.mark(V.memset(recE[:, :, 3], 0.0))
            chain.mark(V.tensor_copy(recE[:, :, 0], srcE[:, :]))
            chain.mark(V.tensor_copy(recE[:, :, 1], dstE[:, :]))
            chain.mark(V.tensor_copy(recE[:, :, 2], ewE[:, :]))
            chain(V.tensor_scalar(buckI[:, :], dstE[:, :], 7, None, ALU.arith_shift_right))
            chain(V.tensor_copy(buckE[:, :], buckI[:, :]))
            for b in range(NT):
                chain(V.tensor_scalar(memb[:, b, :], buckE[:, :], float(b), None, ALU.is_equal))
                chain(V.tensor_tensor_scan(cumu[:, b, :], memb[:, b, :], zrow[0:EP, :], 0.0, ALU.add, ALU.add))
            V.tensor_copy(rowtot[:, :], cumu[:, :, EC - 1]).then_inc(s_rot, 1)
            dve.wait_ge(s_cntp, 2)
            chain(V.tensor_copy(prior[:, :], ps[0:EP, 0, 0:NT]))
            chain(V.tensor_copy(cnt[:, :], ps[:, 1, 0:NT]))
            for b in range(NT):
                chain(V.tensor_scalar(slotT[:, :], cumu[:, b, :], prior[:, b:b + 1], float(b * ROWS * P - 1), ALU.add, ALU.add))
                chain(V.tensor_tensor(slotT[:, :], slotT[:, :], memb[:, b, :], ALU.mult))
                if b == 0:
                    chain(V.tensor_copy(slotF[:, :], slotT[:, :]))
                else:
                    chain(V.tensor_tensor(slotF[:, :], slotF[:, :], slotT[:, :], ALU.add))
            V.tensor_copy(slotI[:, :], slotF[:, :]).then_inc(s_slot, 1)
            chain(V.tensor_scalar(tiles[:, :], cnt[:, :], float(P - 1), None, ALU.add))
            chain(V.tensor_copy(cntI[:, :], tiles[:, :]))
            chain(V.tensor_scalar(cntI[:, :], cntI[:, :], 7, None, ALU.arith_shift_right))
            chain(V.tensor_copy(tiles[:, :], cntI[:, :]))
            for h in range(2):
                s = slice(h * HB, (h + 1) * HB)
                chain(V.tensor_tensor_scan(TS[:, s], tiles[:, s], zrow[:, 0:HB], float(h * B_AT), ALU.add, ALU.add))
            chain(V.tensor_scalar(flagI[0:1, 0:1], TS[0:1, HB - 1:HB], 0.0, None, ALU.add))
            chain(V.tensor_scalar(flagI[0:1, 1:2], TS[0:1, NT - 1:NT], float(-B_AT), None, ALU.add))
            chain(V.tensor_tensor(TS[:, :], TS[:, :], tiles[:, :], ALU.subtract))
            chain(V.memset(Dd[:, 0:1], 0.0))
            dve.wait_ge(s_const, 9)
            chain(V.scalar_tensor_tensor(Dd[:, 1:NT + 1], lane[:, 0:NT], float(ROWS), TS[:, :], ALU.mult, ALU.subtract))
            chain(V.tensor_tensor(DD[:, :], Dd[:, 1:NT + 1], Dd[:, 0:NT], ALU.subtract))
            chain(V.tensor_scalar(brow[:, :], vrow[:, :], 0.0, -1.0, ALU.mult, ALU.add))
            chain(V.tensor_copy(rrow[:, :], vrow[:, :]))
            for b in range(NT):
                chain(V.scalar_tensor_tensor(brow[:, :], vrow[:, :], TS[:, b:b + 1], brow[:, :], ALU.is_ge, ALU.add))
                chain(V.tensor_scalar(tmpc[:, :], vrow[:, :], TS[:, b:b + 1], DD[:, b:b + 1], ALU.is_ge, ALU.mult))
                chain(V.tensor_tensor(rrow[:, :], rrow[:, :], tmpc[:, :], ALU.add))
            V.tensor_copy(vrow0[:, :], rrow[0:1, :]).then_inc(s_rowp, 1)
            dve.wait_ge(s_rowt, 1)
            for c in range(NCH):
                n = min(P, COLS - c * P)
                V.tensor_copy(rowsel[0:n, c:c + 1], ps[0:n, 2, c:c + 1]).then_inc(s_rsel, 1)
            chain(V.tensor_scalar(tmpc[:, :], vrow[:, :], float(B_AT), float(-HB), ALU.is_ge, ALU.mult))
            chain(V.tensor_tensor(tmpc[:, :], tmpc[:, :], brow[:, :], ALU.add))
            V.tensor_copy(bankI[:, :], tmpc[:, :]).then_inc(s_tab, 1)
            dve.wait_ge(s_ldx, 48)
            for t in range(NT):
                chain(V.bn_stats(st[:, t, :], hin[:, t, :]))
                chain(V.bn_aggr(mv[:, t, :], st[:, t, :]))
            V.tensor_scalar(t0[:, :], mv[:, :, 1], LN_EPS, None, ALU.add).then_inc(s_ln, 1)
            dve.wait_ge(s_lnq, 1)
            rsqrt_step()
            for t in range(NT):
                chain(V.tensor_scalar(xs[:, t, :], hin[:, t, :], mv[:, t, 0:1], t1[:, t:t + 1], ALU.subtract, ALU.mult))
            chain(V.tensor_scalar(epsb[:, :], epsb[:, :], 1.0, None, ALU.add))
            dve.wait_ge(s_plane, 1)
            V.tensor_copy(idxT[:, :], ps[:, 0, 0:COLS]).then_inc(s_tab, 1)
            chain(V.tensor_copy(wT[:, :], ps[:, 2, 0:COLS]))
            V.scalar_tensor_tensor(dloc[:, :], brow[:, :], float(-P), ps[:, 1, 0:COLS], ALU.mult, ALU.add).then_inc(s_tab, 1)
            dve.wait_ge(s_tab, 3)
            dve.wait_ge(s_vt, 1)
            chain(V.tensor_copy(vecs[:, :, :, :].rearrange("p v l c -> p (v l c)"), ps[:, 7, 0:3 * L * KC]))
            dve.wait_ge(s_gt4, 1)
            chain(V.tensor_copy(gT[:, :, :].rearrange("p k e -> p (k e)"), ps[:, 6, 0:KC * NX]))
            dve.sem_inc(s_rd, 10)
            needed = [dve.value_load(flagI[0:1, h:h + 1], min_val=0, max_val=HALF_MAX) for h in range(2)]
            with dve.Fori(0, L) as l:
                chain.enter(l, CH_LAYER)
                hold(dve, s_wl, (l + 1) * 80)
                V.tensor_copy(vec[:, :, :], vecs[:, :, bass.ds(l, 1), :].rearrange("p v o c -> p v (o c)")).then_inc(s_vec, 1)
                for t in range(NT):
                    if t >= 2:
                        dve.wait_ge(s_sw[t % 2], (l * (NT // 2) + t // 2) * 16)
                    V.tensor_tensor(stage[:, t % 2, :], xs[:, t, :], beb[:, :], ALU.add).then_inc(s_sg, 1)

                def edges(t, k, turn):
                    dve.wait_ge(s_g[k], (l * (MT // RING) + turn + 1) * 16)
                    V.tensor_scalar(oneh[:, k, :], lane[:, :], dloc[:, bass.ds(t, 1)], None, ALU.is_equal).then_inc(s_y, 1)
                    V.scalar_tensor_tensor(ring[:, k, :], web[:, :], wT[:, bass.ds(t, 1)], ring[:, k, :],
                                           ALU.mult, ALU.add).then_inc(s_y, 1)

                for h, first, groups, rest in halves(l):
                    with dve.Fori(0, groups) as g:
                        for k in range(RING):
                            edges(first + g * RING + k, (first + k) % RING, g + (first + k) // RING)
                    for k in range(rest):
                        edges(first + groups * RING + k, (first + k) % RING, groups + (first + k) // RING)
                    with dve.If(needed[h] > MAIN[h]):
                        with dve.Fori(0, OVER[h]) as o:
                            dve.wait_ge(s_og[h], (l * OVER[h] + o + 1) * 16)
                            V.tensor_scalar(ovh[:, :], lane[:, :], dloc[:, bass.ds(o + OV0[h], 1)], None,
                                            ALU.is_equal).then_inc(s_oy[h], 1)
                            V.scalar_tensor_tensor(ovx[:, :], web[:, :], wT[:, bass.ds(o + OV0[h], 1)], ovx[:, :],
                                                   ALU.mult, ALU.add).then_inc(s_oy[h], 1)
                        hold(dve, s_ou[h], (l + 1) * OVER[h] + 1)
                    dve.wait_ge(s_free, RING + l * MT + first + MAIN[h])
                    for b in range(HB):
                        t = h * HB + b
                        V.scalar_tensor_tensor(hin[:, t, :], xs[:, t, :], epsb[:, bass.ds(l, 1)], ps[:, b, :],
                                               ALU.mult, ALU.add).then_inc(s_hin, 1)
                    for q in range(2):
                        for c in range(KC):
                            a = h * HB * P + q * 320
                            n = min(320, N - a)
                            dve.wait_ge(s_ra, l * 26 + h * 13 + HB + q * KC + c + 1)
                            chain.mark(V.bn_stats(bst[:, c, h * 2 + q, :], h1T[:, c, a:a + n]))
                hold(dve, s_dve, chain.count())
                for c in range(KC):
                    chain.mark(V.bn_aggr(bmv[:, c, :], bst[:, c, :, :].rearrange("p a b -> p (a b)")))
                chain.wait()
                V.tensor_scalar(bve[:, :], bmv[:, :, 1], BN_EPS, None, ALU.add).then_inc(s_var, 1)
                dve.wait_ge(s_root, l + 1)
                chain(V.reciprocal(brs[:, :], bsq[:, :]))
                chain(V.tensor_tensor(bt[:, :], brs[:, :], brs[:, :], ALU.mult))
                chain(V.tensor_tensor(bt[:, :], bt[:, :], bve[:, :], ALU.mult))
                chain(V.tensor_scalar(bt[:, :], bt[:, :], -0.5, 1.5, ALU.mult, ALU.add))
                chain(V.tensor_tensor(brs[:, :], brs[:, :], bt[:, :], ALU.mult))
                dve.wait_ge(s_vec, l + 1)
                chain(V.tensor_tensor(bscale[:, :], brs[:, :], vec[:, 1, :], ALU.mult))
                chain(V.tensor_tensor(bt[:, :], bmv[:, :, 0], bscale[:, :], ALU.mult))
                V.tensor_tensor(bshift[:, :], vec[:, 2, :], bt[:, :], ALU.subtract).then_inc(s_bn, 1)
                for t in range(NT):
                    dve.wait_ge(s_tr, l * 36 + 26 + t + 1)
                    V.tensor_tensor(xs[:, t, :], ps[:, 5 + (26 + t) % 3, :], b2b[:, :], ALU.add).then_inc(s_rd, 1)
                hold(dve, s_xs, (l + 1) * NT)
                chain.leave(L)
            dve.wait_ge(s_ldx, 80)
            for t in range(NT):
                chain(V.tensor_tensor(xs[:, t, :], hin[:, t, :], xs[:, t, :], ALU.add))
                chain(V.bn_stats(st[:, t, :], xs[:, t, :]))
                chain(V.bn_aggr(mv[:, t, :], st[:, t, :]))
            V.tensor_scalar(t0[:, :], mv[:, :, 1], LN_EPS, None, ALU.add).then_inc(s_ln, 1)
            dve.wait_ge(s_lnq, 2)
            rsqrt_step()
            for t in range(NT):
                V.tensor_scalar(hin[:, t, :], xs[:, t, :], mv[:, t, 0:1], t1[:, t:t + 1], ALU.subtract, ALU.mult).then_inc(s_xn, 1)
            dve.wait_ge(s_lg, 1)
            chain(V.tensor_copy(lg[:, :, :].rearrange("p t e -> p (t e)")[:, 0:D], ps[:, 0, :]))
            chain(V.tensor_copy(lg[:, :, :].rearrange("p t e -> p (t e)")[:, D:NT * NX], ps[:, 1, 0:NT * NX - D]))
            for t in range(NT):
                chain.mark(V.max(m8[:, t, :], lg[:, t, :]))
            chain.wait()
            dve.sem_inc(s_gat, 1)
            for t in range(NT):
                chain.mark(V.max_index(i8[:, t, :], m8[:, t, :], lg[:, t, :]))
            chain.wait()
            chain(V.tensor_copy(i8f[:, :, :], i8[:, :, :]))
            every = [P, NT, NX]
            for k in range(KX):
                chain(V.tensor_tensor(oh[k][:, :, :], lane[:, 0:NX].unsqueeze(1).broadcast_to(every),
                                      i8f[:, :, k:k + 1].broadcast_to(every), ALU.is_equal))
                chain(V.tensor_scalar(oh[k][:, NT - 1, :], oh[k][:, NT - 1, :], valid[:, :], None, ALU.mult))
            chain(V.tensor_tensor(both[:, :, :], oh[0][:, :, :], oh[1][:, :, :], ALU.add))
            chain(V.memset(run[:, 0, :], 0.0))
            for t in range(NT):
                chain(V.tensor_tensor(run[:, t + 1, :], run[:, t, :], both[:, t, :], ALU.add))
            V.tensor_scalar(b128[:, :], lane[:, 0:NX], float(P), None, ALU.mult).then_inc(s_run, 1)

            def shared(u):
                q, c = divmod(u, KC)
                v = h1T[:, c, q * 320:(q + 1) * 320]
                dve.wait_ge(s_ssg, u + 1)
                chain(V.tensor_tensor(v, shsig[:, u % 2, :], ps[:, 4 + u % 2 * 2, 0:320], ALU.mult))
                V.tensor_tensor(v, v, ps[:, 5 + u % 2 * 2, 0:320], ALU.mult).then_inc(s_shh, 1)

            shared(0)
            shared(1)
            dve.wait_ge(s_pos, 1)
            flat = pos[:, :, :].rearrange("p t e -> p (t e)")
            chain.mark(V.tensor_copy(flat[:, 0:D], ps[:, 2, :]))
            chain.mark(V.tensor_copy(flat[:, D:NT * NX], ps[:, 3, 0:NT * NX - D]))
            chain(V.tensor_copy(cntx[:, :], ps[:, 3, 256:256 + NX]))
            chain(V.tensor_scalar(ovn[:, :], cntx[:, :], float(P - 1), None, ALU.add))
            chain(V.tensor_copy(ovnI[:, :], ovn[:, :]))
            chain(V.tensor_scalar(ovnI[:, :], ovnI[:, :], 7, None, ALU.arith_shift_right))
            chain(V.tensor_copy(ovn[:, :], ovnI[:, :]))
            chain(V.tensor_scalar(ovn[:, :], ovn[:, :], -1.0, 0.0, ALU.add, ALU.max))
            chain(V.tensor_tensor_scan(ovs[:, :], ovn[:, :], zrow[:, 0:NX], 0.0, ALU.add, ALU.add))
            chain(V.tensor_copy(nov[:, :], ovs[:, NX - 1:NX]))
            chain(V.tensor_tensor(bdif[:, :], ovs[:, :], ovn[:, :], ALU.subtract))
            chain(V.tensor_scalar(bdif[:, :], bdif[:, :], float(NX - 1), float(P), ALU.add, ALU.mult))
            chain(V.tensor_tensor(bdif[:, :], bdif[:, :], b128[:, :], ALU.subtract))
            chain(V.tensor_scalar(slotm[:, :, :], pos[:, :, :], float(P), None, ALU.is_ge))
            chain(V.tensor_tensor(slotm[:, :, :], slotm[:, :, :], bdif[:, :].unsqueeze(1).broadcast_to(every), ALU.mult))
            chain(V.tensor_tensor(slotm[:, :, :], slotm[:, :, :], b128[:, :].unsqueeze(1).broadcast_to(every), ALU.add))
            chain(V.tensor_tensor(slotm[:, :, :], slotm[:, :, :], pos[:, :, :], ALU.add))
            for k in range(KX):
                chain(V.tensor_tensor(lg[:, :, :], oh[k][:, :, :], slotm[:, :, :], ALU.mult))
                chain(V.tensor_reduce(sel[:, k, :], lg[:, :, :], AX.X, ALU.add))
                chain(V.tensor_tensor(lg[:, :, :], oh[k][:, :, :], pos[:, :, :], ALU.mult))
                chain(V.tensor_reduce(selp[:, k, :], lg[:, :, :], AX.X, ALU.add))
            chain.mark(V.tensor_copy(slotx[:, :, :], sel[:, :, :]))
            chain(V.tensor_copy(selI[:, :, :], sel[:, :, :]))
            chain(V.tensor_scalar(hiI[:, :, :], selI[:, :, :], 7, None, ALU.arith_shift_right))
            chain(V.tensor_scalar(selI[:, :, :], selI[:, :, :], P - 1, None, ALU.bitwise_and))
            V.scalar_tensor_tensor(tabx[:, :, :], selI[:, :, :], float(XT), hiI[:, :, :], ALU.mult, ALU.add).then_inc(s_tabx, 1)
            dve.wait_ge(s_sgm, 1)
            chain(V.tensor_tensor(gden[:, :], sgm[:, :, 0], sgm[:, :, 1], ALU.add))
            chain(V.tensor_scalar(gden[:, :], gden[:, :], 1e-20, None, ALU.add))
            chain(V.reciprocal(gden[:, :], gden[:, :]))
            chain(V.tensor_scalar(selp[:, :, :], selp[:, :, :], float(CAP), SCALE, ALU.is_lt, ALU.mult))
            for k in range(KX):
                chain(V.tensor_tensor(gate[:, k, :], sgm[:, :, k], gden[:, :], ALU.mult))
                chain(V.tensor_tensor(gate[:, k, :], gate[:, k, :], selp[:, k, :], ALU.mult))
            ovall = [P, XOVER, NX]
            chain(V.tensor_tensor(cmpx[:, :, :], lane[:, 0:XOVER].unsqueeze(2).broadcast_to(ovall),
                                  ovs[:, :].unsqueeze(1).broadcast_to(ovall), ALU.is_ge))
            chain(V.tensor_reduce(eovF[:, :], cmpx[:, :, :], AX.X, ALU.add))
            chain(V.tensor_scalar(eovF[:, :], eovF[:, :], float(NX - 1), None, ALU.min))
            V.tensor_copy(eovI[:, :], eovF[:, :]).then_inc(s_xrt, 1)
            for u in range(2, 16):
                shared(u)
            for t in range(NT):
                dve.wait_ge(s_so, t + 1)
                V.tensor_tensor(xs[:, t, :], xs[:, t, :], ps[:, t % 2, :], ALU.add).then_inc(s_sod, 1)

            def hidden(j, k):
                dve.wait_ge(s_sig, j + 1)
                at_least(dve, s_th, j - 1)
                V.tensor_tensor(hh[:, k % 2, :], sg[:, k % 2, :], ps[:, 2 + k % 2, 0:HX], ALU.mult).then_inc(s_hm, 1)
                dve.wait_ge(s_hm, j + 1)
                V.tensor_tensor(hh[:, k % 2, :], hh[:, k % 2, :], ps[:, 2 + k % 2, HX:2 * HX], ALU.mult).then_inc(s_hh, 1)

            def hidden_turned(j, k):
                dve.wait_ge(s_th, j + 1)
                at_least(dve, s_g2, j - 1)
                hold(dve, s_th, j + 1)
                V.tensor_copy(hT[:, k % 2, :, :].rearrange("p k n -> p (k n)"), ps[:, 4 + k % 2, 0:XC * P]).then_inc(s_ht, 1)

            def step(g, k):
                j = g * WR + k
                static = isinstance(j, int)
                if not static or j < NX:
                    hidden(j, k)
                if not static or 1 <= j <= NX:
                    hidden_turned(j - 1, (k - 1) % WR)

            for k in range(WR):
                step(0, k)
            with dve.Fori(1, NX // WR - 1) as g:
                for k in range(WR):
                    step(g, k)
            for k in range(WR + 1):
                step(NX // WR - 1 + k // WR, k % WR)
            over = dve.value_load(nov[0:1, 0:1], min_val=0, max_val=XOVER)
            with dve.If(over > 0):
                with dve.Fori(0, XOVER) as o:
                    dve.wait_ge(s_va, o * 3 + 2)
                    V.tensor_tensor(hh[:, 0, :], sg[:, 0, :], ps[:, 2, 0:HX], ALU.mult).then_inc(s_vd, 1)
                    dve.wait_ge(s_vd, o * 3 + 1)
                    V.tensor_tensor(hh[:, 0, :], hh[:, 0, :], ps[:, 2, HX:2 * HX], ALU.mult).then_inc(s_vd, 1)
                    hold(dve, s_vp, o * 4 + 3)
                    V.tensor_copy(hT[:, 0, :, :].rearrange("p k n -> p (k n)"), ps[:, 4, 0:XC * P]).then_inc(s_vd, 1)
            for u in range(KX * NT):
                t, k = u // KX, u % KX
                n = min(P, N - t * P)
                dve.wait_ge(s_yg[u % RING], 16 * (u // RING + 1))
                if k:
                    dve.wait_ge(s_fa2, u)
                last = V.scalar_tensor_tensor(xs[0:n, t, :], ring[0:n, u % RING, :], gate[0:n, k, t:t + 1], xs[0:n, t, :],
                                              ALU.mult, ALU.add)
                last.then_inc(s_fa2, 1)
                if k:
                    dve.wait_ge(s_fa2, u + 1)
                    dve.sem_inc(s_fa, 1)

        @block.tensor
        def _(pe):
            T = nc.tensor
            pe.wait_ge(s_rot, 1)
            pe.wait_ge(s_const, 4)
            T.matmul(ps[0:EP, 0, 0:NT], below[0:EP, 0:EP], rowtot[:, :], start=True, stop=True).then_inc(s_cntp, 1)
            T.matmul(ps[:, 1, 0:NT], ones[0:EP, :], rowtot[:, :], start=True, stop=True).then_inc(s_cntp, 1)
            pe.wait_ge(s_rowp, 1)
            for c in range(NCH):
                n = min(P, COLS - c * P)
                last = T.matmul(ps[0:n, 2, c:c + 1], vrow0[0:1, c * P:c * P + n], ones[0:1, 0:1], start=True, stop=True)
            last.then_inc(s_rowt, 1)
            pe.wait_ge(s_rowg, 16 * NCH)
            pe.wait_ge(s_rsel, NCH)
            for f in range(3):
                for c in range(NCH):
                    n = min(P, COLS - c * P)
                    last = T.transpose(ps[:, f, c * P:c * P + n], ring[0:n, c, :].rearrange("p (e f) -> p f e", f=REC)[:, f, :],
                                       ident[0:n, 0:n])
            last.then_inc(s_plane, 1)
            pe.wait_ge(s_ldv, 48)
            T.transpose(ps[:, 7, 0:3 * L * KC], vrows[:, :], ident[0:3 * L * KC, 0:3 * L * KC]).then_inc(s_vt, 1)
            pe.wait_ge(s_gw, 16)
            for k in range(KC):
                last = T.transpose(ps[:, 6, k * NX:(k + 1) * NX], gw[:, :].rearrange("e (p k) -> e k p", k=KC)[:, k, :], ident[0:NX, 0:NX])
            last.then_inc(s_gt4, 1)
            pe.wait_ge(s_tab, 3)
            pe.wait_ge(s_zro, 1)
            pe.sem_inc(s_ou[0], 1)
            pe.sem_inc(s_ou[1], 1)
            needed = [pe.value_load(flagI[0:1, h:h + 1], min_val=0, max_val=HALF_MAX) for h in range(2)]
            with pe.Fori(0, L) as l:
                def clear(h):
                    for b in range(HB):
                        if h == 1:
                            pe.wait_ge(s_hin, l * NT + b + 1)
                        T.matmul(ps[:, b, :], zeros_h[:, 0:P], zeros_h[:, :], start=True, stop=False, skip_group_check=True)

                def add(t, k):
                    bank = pe.value_load(bankI[0:1, bass.ds(t, 1)], min_val=0, max_val=HB - 1)
                    pe.wait_ge(s_m, (l * MT + t + 1) * 2)
                    T.matmul(ps[:, bass.ds(bank, 1), :], oneh[:, k, :], ring[:, k, :], start=False, stop=False,
                             skip_group_check=True).then_inc(s_free, 1)

                use = 0

                def freed(u):
                    if u < 3:
                        pe.wait_ge(s_rd, 10 + (l * NT) + (u - 3 + 1 + 0) + 0)
                    elif u - 3 < 26:
                        pe.wait_ge(s_ra, l * 26 + u - 3 + 1)
                    else:
                        pe.wait_ge(s_rd, 10 + l * NT + u - 3 - 26 + 1)

                for h, first, groups, rest in halves(l):
                    clear(h)
                    with pe.Fori(0, groups) as g:
                        for k in range(RING):
                            add(first + g * RING + k, (first + k) % RING)
                    for k in range(rest):
                        add(first + groups * RING + k, (first + k) % RING)
                    with pe.If(needed[h] > MAIN[h]):
                        with pe.Fori(0, OVER[h]) as o:
                            bank = pe.value_load(bankI[0:1, bass.ds(o + OV0[h], 1)], min_val=0, max_val=HB - 1)
                            pe.wait_ge(s_om[h], l * OVER[h] + o + 1)
                            T.matmul(ps[:, bass.ds(bank, 1), :], ovh[:, :], ovx[:, :], start=False, stop=False,
                                     skip_group_check=True).then_inc(s_ou[h], 1)
                    for b in range(HB):
                        pe.wait_ge(s_hin, l * NT + h * HB + b + 1)
                        freed(use)
                        for k in range(KC):
                            last = T.transpose(ps[:, 5 + use % 3, k * P:(k + 1) * P],
                                               hin[:, h * HB + b, :].rearrange("p (d k) -> p k d", k=KC)[:, k, :], ident[:, :])
                        last.then_inc(s_tr, 1)
                        use += 1
                    pe.wait_ge(s_ra, l * 26 + h * 13 + HB)
                    if h == 0:
                        pe.wait_ge(s_wl, (l + 1) * 80)
                    for q in range(2):
                        for c in range(KC):
                            freed(use)
                            a = h * HB * P + q * 320
                            for k in range(KC):
                                last = T.matmul(ps[:, 5 + use % 3, 0:320], w1s[:, k, c * P:(c + 1) * P], hinT[:, k, a:a + 320],
                                                start=k == 0, stop=k == KC - 1)
                            last.then_inc(s_tr, 1)
                            use += 1
                for t in range(NT):
                    pe.wait_ge(s_gt, l * 16 + KC * (((t + 1) * P - 1) // 320 + 1))
                    freed(use)
                    for k in range(KC):
                        last = T.matmul(ps[:, 5 + use % 3, :], h1T[:, k, t * P:(t + 1) * P], w2s[:, k, :],
                                        start=k == 0, stop=k == KC - 1)
                    last.then_inc(s_tr, 1)
                    use += 1
            for t in range(NT):
                pe.wait_ge(s_xn, t + 1)
                at_least(pe, s_ra2, t - 2)
                for k in range(KC):
                    last = T.transpose(ps[:, 5 + t % 3, k * P:(k + 1) * P],
                                       hin[:, t, :].rearrange("p (d k) -> p k d", k=KC)[:, k, :], ident[:, :])
                last.then_inc(s_tr2, 1)
            for t in range(NT):
                pe.wait_ge(s_ra2, t + 1)
                for k in range(KC):
                    last = T.matmul(ps[:, t // 8, t % 8 * NX:(t % 8 + 1) * NX], hinT[:, k, t * P:(t + 1) * P], gT[:, k, :],
                                    start=k == 0, stop=k == KC - 1)
            last.then_inc(s_lg, 1)
            pe.wait_ge(s_swl, 48)

            def shared_up(u):
                q, c = divmod(u, KC)
                at_least(pe, s_shh, u - 1)
                for v, w in ((4, w1s), (5, w3s)):
                    for k in range(KC):
                        last = T.matmul(ps[:, v + u % 2 * 2, 0:320], w[:, k, c * P:(c + 1) * P], hinT[:, k, q * 320:(q + 1) * 320],
                                        start=k == 0, stop=k == KC - 1)
                last.then_inc(s_sp, 1)

            shared_up(0)
            shared_up(1)
            pe.wait_ge(s_run, 1)
            for t in range(NT):
                o = ps[:, 2 + t // 8, t % 8 * NX:(t % 8 + 1) * NX]
                T.matmul(o, below[:, :], both[:, t, :], start=True, stop=False)
                T.matmul(o, ones[:, :], run[:, t, :], start=False, stop=True)
            T.matmul(ps[:, 3, 256:256 + NX], ones[:, :], run[:, NT, :], start=True, stop=True).then_inc(s_pos, 1)
            for u in range(2, 16):
                shared_up(u)
            for t in range(NT):
                pe.wait_ge(s_shh, KC * (((t + 1) * P - 1) // 320 + 1))
                at_least(pe, s_sod, t - 1)
                for k in range(KC):
                    last = T.matmul(ps[:, t % 2, :], h1T[:, k, t * P:(t + 1) * P], w2s[:, k, :], start=k == 0, stop=k == KC - 1)
                last.then_inc(s_so, 1)
            pe.wait_ge(s_sod, NT)

            def turn_x(k):
                for c in range(KC):
                    last = T.transpose(ps[:, k % 2, c * P:(c + 1) * P],
                                       xe[:, k, :].rearrange("p (d k) -> p k d", k=KC)[:, c, :], ident[:, :])
                return last

            def up(k):
                for c in range(KC):
                    last = T.matmul(ps[:, 2 + k % 2, :], xeT[:, k % 2, c, :], w13[:, k, c, :, :].rearrange("p a n -> p (a n)"),
                                    start=c == 0, stop=c == KC - 1)
                return last

            def turn_h(k):
                for c in range(XC):
                    last = T.transpose(ps[:, 4 + k % 2, c * P:(c + 1) * P],
                                       hh[:, k % 2, :].rearrange("p (d k) -> p k d", k=XC)[:, c, :], ident[:, :])
                return last

            def down(k):
                for c in range(XC):
                    last = T.matmul(ps[:, 6 + k % 2, :], hT[:, k % 2, c, :], w2e[:, k, c, :], start=c == 0, stop=c == XC - 1)
                return last

            def turned(j, k, turn):
                pe.wait_ge(s_xg[k], (turn + 1) * 16)
                at_least(pe, s_xt, j - 1)
                turn_x(k).then_inc(s_tx, 1)

            def step(g, k):
                j = g * WR + k
                static = isinstance(j, int)
                if not static or j < NX:
                    pe.wait_ge(s_xt, j + 1)
                    pe.wait_ge(s_w[k], (g + 1) * 48)
                    at_least(pe, s_hh, j - 1)
                    up(k).then_inc(s_g1, 1)
                if not static or 1 <= j <= NX:
                    at_least(pe, s_hh, j)
                    at_least(pe, s_ht, j - 2)
                    turn_h((k - 1) % WR).then_inc(s_th, 1)
                if not static or j >= 2:
                    at_least(pe, s_ht, j - 1)
                    at_least(pe, s_yc, j - 3)
                    down((k - 2) % WR).then_inc(s_g2, 1)
                if not static or j + 1 < NX:
                    turned(j + 1, (k + 1) % WR, g + (k + 1) // WR)

            turned(0, 0, 0)
            for k in range(WR):
                step(0, k)
            with pe.Fori(1, NX // WR - 1) as g:
                for k in range(WR):
                    step(g, k)
            for k in range(WR + 2):
                step(NX // WR - 1 + k // WR, k % WR)
            pe.wait_ge(s_xrt, 1)
            over = pe.value_load(nov[0:1, 0:1], min_val=0, max_val=XOVER)
            with pe.If(over > 0):
                with pe.Fori(0, XOVER) as o:
                    pe.wait_ge(s_vg, o * 16 + 16)
                    turn_x(0).then_inc(s_vp, 1)
                    pe.wait_ge(s_va, o * 3 + 1)
                    pe.wait_ge(s_vw, o * 48 + 48)
                    up(0).then_inc(s_vp, 1)
                    pe.wait_ge(s_vd, o * 3 + 2)
                    turn_h(0).then_inc(s_vp, 1)
                    pe.wait_ge(s_vd, o * 3 + 3)
                    down(0).then_inc(s_vp, 1)


CH_LAYER = 16 + 4 + 7

_INS = ["x", "src", "dst", "edge_weight1", "L0_gnn_eps", "L0_gnn_We", "L0_gnn_be", "L0_gnn_W1", "L0_gnn_b1",
        "L0_gnn_gamma", "L0_gnn_beta", "L0_gnn_W2", "L0_gnn_b2", "L0_ffn_gate_w", "L0_ffn_w1", "L0_ffn_w3",
        "L0_ffn_w2", "L0_ffn_sw1", "L0_ffn_sw3", "L0_ffn_sw2"]


def kernel(**inputs):
    import numpy as np
    import concourse.bacc as bacc
    from concourse.bass_utils import run_bass_kernel_spmd as run

    nc = bacc.Bacc("TRN2", target_bir_lowering=False, num_devices=1)
    arrays, args = {}, []
    for name in _INS:
        a = np.ascontiguousarray(inputs[name])
        arrays[f"in_{name}"] = a
        args.append(nc.dram_tensor(f"in_{name}", a.shape, mybir.dt.from_np(a.dtype), kind="ExternalInput").ap())
    out = nc.dram_tensor("out", (N, D), F32, kind="ExternalOutput").ap()
    scratch = [nc.dram_tensor("x_rows", (NP, D), F32).ap(), nc.dram_tensor("records", (RROWS, P * REC), F32).ap(),
               nc.dram_tensor("token_rows", (NP, D), F32).ap(), nc.dram_tensor("token_table", (P * XT, 1), I32).ap(),
               nc.dram_tensor("expert_rows", (XT * P, D), F32).ap()]
    build(nc, *args, out, scratch)
    return run(nc, [arrays], core_ids=[0]).results[0]["out"]
```

```python
import concourse.bass as bass
from concourse import mybir
from contextlib import ExitStack

F32, BF16 = mybir.dt.float32, mybir.dt.bfloat16
I32, U32 = mybir.dt.int32, mybir.dt.uint32
ALU = mybir.AluOpType
ACT = mybir.ActivationFunctionType
AX = mybir.AxisListType

P = 128
N, D, E, L = 1250, 512, 20000, 4
NT = -(-N // P)
NP = NT * P
LAST = N - (NT - 1) * P
KC = D // P
EP = 125
EC = E // EP
BN_EPS = LN_EPS = 1e-5

HB = NT // 2
HALF_MAX = (E - 1) // P + 1 + HB - 1
MAIN = [-(-E * HB * P // N // P) + HB // 2 + 1 + 3, -(-E * (N - HB * P) // N // P) + HB // 2 + 3]
MT = sum(MAIN)
RING = 8
assert MT % RING == 0
PRE = 2 * RING
BODY = 2 * KC * RING
assert PRE + BODY <= MAIN[1]
OVER = [HALF_MAX - m for m in MAIN]
OV0 = [MT + RING, MT + RING + OVER[0]]
COLS = MT + RING + sum(OVER)
B_AT = 1024
FULL = -(-E // P)
RROWS = FULL + 1
PADP = 32
PADS = RROWS * P - E
assert PADS % PADP == 0
NX, KX, HX = 64, 2, 256
CAP = 1024
SCALE = 2.5
XOVER = (N * KX - 1) // P
XT = NX + XOVER
XC = HX // P
WR = 4
REC = 4


class Chain:

    def __init__(self, engine, sem):
        self.engine, self.sem, self.base, self.n = engine, sem, 0, 0

    def __call__(self, instruction):
        self.mark(instruction)
        self.wait()

    def mark(self, instruction):
        instruction.then_inc(self.sem, 1)
        self.n += 1

    def count(self):
        return self.base + self.n

    def wait(self):
        self.engine.wait_ge(self.sem, self.count())

    def enter(self, i, per):
        self.before, self.per = self.base + self.n, per
        self.base, self.n = self.before + i * per, 0

    def leave(self, rounds):
        assert self.n == self.per, (self.n, self.per)
        self.base, self.n = self.before + rounds * self.per, 0


def at_least(engine, sem, value):
    if not isinstance(value, int) or value > 0:
        engine.wait_ge(sem, value)


def build(nc, x, src, dst, ew, eps, We, be, W1, b1, gamma, beta, W2, b2,
          gate_w, xw1, xw3, xw2, sw1, sw3, sw2, out, scratch):
    xb_dram, rec_dram, xn_dram, tok_dram, y_dram = scratch
    with ExitStack() as ctx:
        def sb(name, shape, dt=F32):
            return ctx.enter_context(nc.sbuf_tensor(name, shape, dt))

        def sem(name):
            return ctx.enter_context(nc.semaphore(name))

        def inside(buffer, layout):
            at, views = 0, []
            for parts, dims, dt in layout:
                n = 1
                for d in dims:
                    n *= d
                v = buffer[0:parts, at:at + n]
                at += n
                if dt is not F32:
                    v = v.bitcast(dt)
                if len(dims) > 1:
                    names = "abcd"[:len(dims)]
                    v = v.rearrange(f"p ({' '.join(names)}) -> p {' '.join(names)}", **dict(zip(names, dims)))
                views.append(v)
            return views

        turned = sb("turned", [P, KC * NP])
        hidden_ = sb("hidden_", [P, KC * NP])
        flight = sb("flight", [P, RING * D])
        rows = sb("rows", [P, 3 * D])
        mixed = sb("mixed", [P, KC * D])
        [hinT] = inside(turned, [(P, (KC, NP), F32)])
        [h1T] = inside(hidden_, [(P, (KC, NP), F32)])
        [ring] = inside(flight, [(P, (RING, D), F32)])
        web, beb, b2b = inside(rows, [(P, (D,), F32)] * 3)
        [oneh] = inside(mixed, [(P, (RING, P), F32)])
        [xres] = inside(turned, [(P, (NT, D), F32)])
        [w3s] = inside(mixed, [(P, (KC, D), F32)])
        [cmpx] = inside(rows, [(P, (XOVER, NX), F32)])
        srcE, ewE, slotF, slotT, slotI, recE, memb, cumu = inside(
            turned, [(EP, (EC,), t) for t in (I32, F32, F32, F32, U32)]
            + [(EP, (EC, REC), F32), (EP, (NT + 1, EC), F32), (EP, (NT, EC), F32)])
        vrow, brow, tmpc, padrec = inside(
            hidden_, [(P, (COLS,), F32)] * 3 + [(PADP, (PADS // PADP, REC), F32)])
        dstE, buckI, buckE = inside(rows, [(EP, (EC + 1,), t) for t in (I32, I32, F32)])
        lg, both, run, pos, slotm, oh0 = inside(
            flight, [(P, (NT, NX), F32), (P, (NT, NX), F32), (P, (NT + 1, NX), F32)] + [(P, (NT, NX), F32)] * 3)
        oh = [oh0, sb("oh1", [P, NT, NX])]
        xeT, sg, hh, hT, ysb = inside(
            hidden_, [(P, (2, KC, P), F32), (P, (2, HX), F32), (P, (2, HX), F32), (P, (2, XC, P), F32), (P, (WR, D), F32)])
        ident = sb("ident", [P, P])
        below = sb("below", [P, P])
        ones = sb("ones", [P, P])
        zeros_h = sb("zeros_h", [P, D], BF16)
        lane = sb("lane", [P, P])
        vrows = sb("vrows", [3 * L * KC, P])
        vecs = sb("vecs", [P, 3, L, KC])
        zrow = sb("zrow", [P, EC])
        rowtot = sb("rowtot", [EP, NT + 1])
        prior = sb("prior", [EP, NT])
        cnt = sb("cnt", [P, NT + 1])
        upto = sb("upto", [P, NT])
        start = sb("start", [P, NT])
        rowI = sb("rowI", [P, 2, NT], I32)
        row01 = sb("row01", [P, 2, NT])
        unsI = sb("unsI", [1, 1], I32)
        tiles = sb("tiles", [P, NT])
        TS = sb("TS", [P, NT])
        Dd = sb("Dd", [P, NT + 1])
        DD = sb("DD", [P, NT])
        bankI = sb("bankI", [P, COLS], I32)
        NCH = -(-COLS // P)
        rowsel = sb("rowsel", [P, NCH], U32)
        colid = sb("colid", [P, NCH])
        vcol = sb("vcol", [P, NCH])
        tcol = sb("tcol", [P, NCH])
        ccol = sb("ccol", [P, NCH, NT])
        idxT = sb("idxT", [P, COLS], U32)
        wT = sb("wT", [P, COLS])
        dloc = sb("dloc", [P, COLS])
        rec4 = sb("rec4", [EP, 4, REC])
        idx4 = sb("idx4", [EP, 4], U32)
        xs = sb("xs", [P, NT, D])
        hin = sb("hin", [P, NT, D])
        w1s = sb("w1s", [P, KC, D])
        w2s = sb("w2s", [P, KC, D])
        vec = sb("vec", [P, 3, KC])
        epsb = sb("epsb", [P, L])
        cur = sb("cur", [P, RING], U32)
        st = sb("st", [P, NT, 6])
        mv = sb("mv", [P, NT, 2])
        t0 = sb("t0", [P, NT])
        t1 = sb("t1", [P, NT])
        t2 = sb("t2", [P, NT])
        bst = sb("bst", [P, KC, 4, 6])
        bmv = sb("bmv", [P, KC, 2])
        bve = sb("bve", [P, KC])
        bsq = sb("bsq", [P, KC])
        brs = sb("brs", [P, KC])
        bt = sb("bt", [P, KC])
        bscale = sb("bscale", [P, KC])
        bshift = sb("bshift", [P, KC])
        ovx = sb("ovx", [P, D])
        ovh = sb("ovh", [P, P])
        ovi = sb("ovi", [P, 1], U32)
        flagI = sb("flagI", [1, 2], I32)

        gw = sb("gw", [NX, D])
        gT = sb("gT", [P, KC, NX])
        valid = sb("valid", [P, 1])
        m8 = sb("m8", [P, NT, 8])
        i8 = sb("i8", [P, NT, 8], U32)
        i8f = sb("i8f", [P, NT, 8])
        cntx = sb("cntx", [P, NX])
        ovn = sb("ovn", [P, NX])
        ovnI = sb("ovnI", [P, NX], I32)
        ovs = sb("ovs", [P, NX])
        b128 = sb("b128", [P, NX])
        bdif = sb("bdif", [P, NX])
        sel = sb("sel", [P, KX, NT])
        selp = sb("selp", [P, KX, NT])
        selI = sb("selI", [P, KX, NT], I32)
        hiI = sb("hiI", [P, KX, NT], I32)
        slotx = sb("slotx", [P, KX, NT], U32)
        tabx = sb("tabx", [P, KX, NT], U32)
        tokid = sb("tokid", [P, NT], I32)
        tokT = sb("tokT", [P, XT], I32)
        ztab = sb("ztab", [P, XT], I32)
        sgm = sb("sgm", [P, NT, KX])
        gden = sb("gden", [P, NT])
        gate = sb("gate", [P, KX, NT])
        eovF = sb("eovF", [P, XOVER])
        eovI = sb("eovI", [P, XOVER], I32)
        nov = sb("nov", [P, 1], I32)
        shsig = sb("shsig", [P, 2, 320])
        w13 = sb("w13", [P, WR, KC, 2, HX])
        w2e = sb("w2e", [P, WR, XC, D])
        icur = sb("icur", [P, WR], I32)
        xe = ring[:, 0:WR, :]

        ps = ctx.enter_context(nc.psum_tensor("ps", [P, 8, D], F32))

        s_idle = sem("idle")
        s_const = sem("constants")
        s_colid = sem("column_numbers")
        s_zro = sem("zero_bf16")
        s_ldx = sem("x_loaded")
        s_ldd = sem("destinations_loaded")
        s_lde = sem("edges_loaded")
        s_padm = sem("pad_records_made")
        s_rec = sem("records_made")
        s_recw = sem("records_stored")
        s_slot = sem("slots_known")
        s_rot = sem("row_totals_known")
        s_cntp = sem("counts_summed")
        s_uns = sem("order_known")
        s_rsel = sem("row_numbers_ready")
        s_pc = sem("pool_constants")
        s_c4 = sem("pool_copies")
        s_gen = sem("dve_slots_chain")
        s_scat = sem("records_scattered")
        s_rowg = sem("record_rows_gathered")
        s_plane = sem("record_planes_turned")
        s_idx = sem("sources_ready")
        s_tab = sem("tile_tables_ready")
        s_dve = sem("dve_chain")
        s_act = sem("act_chain")
        s_ln = sem("layernorm_sums")
        s_lnq = sem("layernorm_roots")
        s_lwe = sem("We_loaded")
        s_lw1 = sem("W1_loaded")
        s_lw2 = sem("W2_b2_loaded")
        s_lbe = sem("be_loaded")
        s_ldv = sem("vectors_loaded")
        s_vt = sem("vectors_turned")
        s_vec = sem("layer_vectors_ready")
        s_sg = sem("staged")
        s_st = sem("x_be_stored")
        s_first = sem("first_indices")
        s_g = [sem(f"gathered{k}") for k in range(RING)]
        s_y = sem("messages_summed")
        s_m = sem("messages_ready")
        s_free = sem("ring_slots_free")
        s_zero = sem("acc_zeroed")
        s_hin = sem("aggregate_read")
        s_tr = sem("bank_filled")
        s_ra = sem("bank_read_by_act")
        s_rd = sem("bank_read_by_dve")
        s_var = sem("bn_variance")
        s_root = sem("bn_root")
        s_bn = sem("bn_ready")
        s_gt = sem("hidden_ready")
        s_xs = sem("x_relu")
        s_og = [sem(f"over_gathered{h}") for h in range(2)]
        s_oi = [sem(f"over_index{h}") for h in range(2)]
        s_oy = [sem(f"over_summed{h}") for h in range(2)]
        s_om = [sem(f"over_message{h}") for h in range(2)]
        s_ou = [sem(f"over_used{h}") for h in range(2)]
        s_gw = sem("gate_loaded")
        s_gt4 = sem("gate_turned")
        s_gT = sem("gate_ready")
        s_ztab = sem("token_table_zero")
        s_ztw = sem("token_table_cleared")
        s_swl = sem("shared_weights_loaded")
        s_xn = sem("tokens_normed")
        s_xnw = sem("tokens_stored")
        s_tr2 = sem("tokens_turned")
        s_ra2 = sem("turned_tokens_read")
        s_lg = sem("logits")
        s_gat = sem("top_scores")
        s_sgm = sem("top_sigmoids")
        s_run = sem("expert_members")
        s_pos = sem("expert_ranks")
        s_tabx = sem("token_slots")
        s_scx = sem("tokens_scattered")
        s_tok = sem("token_table_loaded")
        s_xrt = sem("expert_tables_ready")
        s_sp = sem("shared_products")
        s_ssg = sem("shared_sigmoids")
        s_shh = sem("shared_hidden")
        s_so = sem("shared_out")
        s_sod = sem("shared_added")
        s_ic = sem("expert_indices")
        s_w = [sem(f"expert_weights{k}") for k in range(WR)]
        s_xg = [sem(f"tokens_gathered{k}") for k in range(WR)]
        s_tx = sem("x_turned")
        s_xt = sem("xT_ready")
        s_g1 = sem("up_products")
        s_sig = sem("sigmoids")
        s_hh = sem("hidden")
        s_hm = sem("hidden_half")
        s_th = sem("hidden_turned")
        s_ht = sem("hiddenT_ready")
        s_g2 = sem("down_products")
        s_yc = sem("y_copied")
        s_ys = [sem(f"y_stored{k}") for k in range(WR)]
        s_yz = sem("over_rows_cleared")
        s_vw = sem("over_weights")
        s_vg = sem("over_tokens")
        s_vi = sem("over_token_index")
        s_vp = sem("over_pe")
        s_va = sem("over_act")
        s_vd = sem("over_dve")
        s_vs = sem("over_y_stored")
        s_yg = [sem(f"y_gathered{k}") for k in range(RING)]
        s_fa = sem("combined")
        s_fa2 = sem("y_added")
        s_out = sem("out_stored")
        s_fin = sem("final_sum")

        def hold(engine, s, value):
            engine.wait_ge(s, value)
            engine.sem_inc(s_idle, 1)

        def halves(l):
            return [(h, sum(MAIN[:h]), MAIN[h] // RING, MAIN[h] % RING) for h in range(2)]

        block = ctx.enter_context(nc.Block())

        @block.sync
        def _(sp):
            xr = x[0:(NT - 1) * P, :].rearrange("(t p) d -> p t d", p=P)
            sp.dma_start(dstE[:, 0:EC], dst.rearrange("(p c) -> p c", p=EP)).then_inc(s_ldd, 16)
            sp.wait_ge(s_const, 1)
            sp.dma_start(dstE[0:EP - 1, EC:EC + 1], dst.rearrange("(p c) -> p c", p=EP)[1:EP, 0:1],
                         allow_slow_non_contiguous=True).then_inc(s_ldd, 16)
            sp.dma_start(srcE[:, :], src.rearrange("(p c) -> p c", p=EP)).then_inc(s_lde, 16)
            sp.dma_start(ewE[:, :], ew.rearrange("(p c) o -> p (c o)", p=EP)).then_inc(s_lde, 16)
            sp.wait_ge(s_const, 2)
            sp.dma_start(hin[:, 0:NT - 1, :], xr).then_inc(s_ldx, 16)
            sp.dma_start(hin[0:LAST, NT - 1, :], x[(NT - 1) * P:N, :]).then_inc(s_ldx, 16)
            sp.dma_start(epsb[:, :], eps.partition_broadcast(P)).then_inc(s_ldx, 16)
            sp.dma_start(beb[:, :], be[0, :].partition_broadcast(P)).then_inc(s_lbe, 16)
            flat = rec_dram.rearrange("r c -> (r c)")
            sp.wait_ge(s_padm, 1)
            sp.dma_start(flat[E * REC:RROWS * P * REC].rearrange("(p c) -> p c", p=PADP),
                         padrec[:, :, :].rearrange("p a b -> p (a b)")).then_inc(s_recw, 16)
            sp.wait_ge(s_rec, 4)
            sp.dma_start(flat[0:E * REC].rearrange("(p c) -> p c", p=EP),
                         recE[:, :, :].rearrange("p a b -> p (a b)")).then_inc(s_recw, 16)
            for v, a in enumerate((b1, gamma, beta)):
                sp.dma_start(vrows[v * L * KC:(v + 1) * L * KC, :], a.rearrange("l (c p) -> (l c) p", p=P)).then_inc(s_ldv, 16)
            sp.dma_start(gw[:, :], gate_w).then_inc(s_gw, 16)
            sp.wait_ge(s_ztab, 1)
            sp.dma_start(tok_dram.rearrange("(p j) o -> p (j o)", p=P), ztab[:, :]).then_inc(s_ztw, 16)

            def load_expert(e, k, done):
                sp.dma_start(w13[:, k, :, 0, :], xw1[bass.ds(e, 1), :, :].rearrange("o (p k) n -> (o p) k n", k=KC)).then_inc(done, 16)
                sp.dma_start(w13[:, k, :, 1, :], xw3[bass.ds(e, 1), :, :].rearrange("o (p k) n -> (o p) k n", k=KC)).then_inc(done, 16)
                sp.dma_start(w2e[:, k, :, :], xw2[bass.ds(e, 1), :, :].rearrange("o (p k) n -> (o p) k n", k=XC)).then_inc(done, 16)

            sp.wait_ge(s_rot, 1)
            with sp.Fori(0, L) as l:
                hold(sp, s_hin, 1 + l * NT)
                sp.dma_start(web[:, :], We[bass.ds(l, 1), 0, :].rearrange("o d -> (o d)").partition_broadcast(P)).then_inc(s_lwe, 16)
                hold(sp, s_var, 1 + l)
                sp.dma_start(w1s[:, :, :], W1[bass.ds(l, 1), :, :].rearrange("o (p k) n -> (o p) k n", k=KC)).then_inc(s_lw1, 16)
                for t in range(NT):
                    hold(sp, s_sg, l * NT + t + 1)
                    sp.dma_start(xb_dram[t * P:(t + 1) * P, :], hin[:, t, :]).then_inc(s_st, 16)
                hold(sp, s_rd, 10 + l * NT)
                sp.dma_start(w2s[:, :, :], W2[bass.ds(l, 1), :, :].rearrange("o (k p) n -> p (o k) n", p=P)).then_inc(s_lw2, 16)
                sp.dma_start(b2b[:, :], b2[bass.ds(l, 1), :].rearrange("o d -> (o d)").partition_broadcast(P)).then_inc(s_lw2, 16)
                with sp.If(l < L - 1):
                    after = nc.s_assert_within(l + 1, 1, L - 1, skip_runtime_bounds_check_because="l < L - 1 here")
                    sp.dma_start(beb[:, :], be[bass.ds(after, 1), :].rearrange("o d -> (o d)").partition_broadcast(P)).then_inc(s_lbe, 16)
            sp.wait_ge(s_var, 1 + L)
            sp.dma_start(xres[:, 0:NT - 1, :], xr).then_inc(s_ldx, 16)
            sp.dma_start(xres[0:LAST, NT - 1, :], x[(NT - 1) * P:N, :]).then_inc(s_ldx, 16)
            sp.wait_ge(s_rd, 10 + L * NT)
            sp.dma_start(w1s[:, :, :], sw1.rearrange("(p k) n -> p k n", k=KC)).then_inc(s_swl, 16)
            sp.dma_start(w3s[:, :, :], sw3.rearrange("(p k) n -> p k n", k=KC)).then_inc(s_swl, 16)
            sp.dma_start(w2s[:, :, :], sw2.rearrange("(k p) n -> p k n", p=P)).then_inc(s_swl, 16)
            for t in range(NT):
                sp.wait_ge(s_xn, t + 1)
                sp.dma_start(xn_dram[t * P:(t + 1) * P, :], hin[:, t, :]).then_inc(s_xnw, 16)
            for e in range(WR):
                load_expert(e, e, s_w[e])
            sp.wait_ge(s_zro, 1)
            sp.dma_start(y_dram[NX * P:XT * P, :].rearrange("(p t) (a c) -> p (t a) c", p=P, a=2),
                         zeros_h[:, :].bitcast(F32).unsqueeze(1).broadcast_to([P, XOVER * 2, D // 2])).then_inc(s_yz, 16)
            sp.wait_ge(s_scx, 16 * KX * NT)
            sp.dma_start(tokT[:, :], tok_dram.rearrange("(p j) o -> p (j o)", p=P)).then_inc(s_tok, 16)

            def store_y(j, k):
                at_least(sp, s_yc, j + 1)
                sp.dma_start(y_dram[bass.ds(j * P, P), :], ysb[:, k, :]).then_inc(s_ys[k], 16)

            def expert_traffic(j, k):
                sp.wait_ge(s_g2, j - WR + 1)
                load_expert(j, k, s_w[k])
                if not isinstance(j, int) or j > WR:
                    store_y(j - WR - 1, (k - 1) % WR)

            for k in range(WR):
                expert_traffic(WR + k, k)
            with sp.Fori(2, NX // WR) as g:
                for k in range(WR):
                    expert_traffic(g * WR + k, k)
            for j in range(NX - WR - 1, NX):
                store_y(j, j % WR)
            sp.wait_ge(s_xrt, 1)
            sp.wait_ge(s_yz, 16)
            over = sp.value_load(nov[0:1, 0:1], min_val=0, max_val=XOVER)
            with sp.If(over > 0):
                def traffic(o):
                    at_least(sp, s_va, o * 3)
                    e = sp.value_load(eovI[0:1, bass.ds(o, 1)], min_val=0, max_val=NX - 1)
                    load_expert(e, 0, s_vw)
                    sp.wait_ge(s_va, o * 3 + 3)
                    sp.dma_start(y_dram[bass.ds((o + NX) * P, P), :], ysb[:, 0, :]).then_inc(s_vs, 16)

                traffic(0)
                with sp.Fori(1, XOVER) as o:
                    traffic(o)
            for t in range(NT):
                sp.wait_ge(s_fa, t + 1)
                n = min(P, N - t * P)
                sp.dma_start(out[t * P:t * P + n, :], xs[0:n, t, :]).then_inc(s_out, 16)
            sp.wait_ge(s_out, 16 * NT)

        @block.gpsimd
        def _(pool):
            nc.gpsimd.memset(dstE[:, EC:EC + 1], 1 << 20).then_inc(s_const, 1)
            nc.gpsimd.memset(hin[:, NT - 1, :], 0.0).then_inc(s_const, 1)
            nc.gpsimd.memset(padrec[:, :, :], 0.0).then_inc(s_pc, 1)
            nc.gpsimd.memset(recE[:, :, 3], 0.0).then_inc(s_rec, 1)
            nc.gpsimd.memset(ones[:, :], 1.0).then_inc(s_pc, 1)
            nc.gpsimd.memset(ident[:, :], 0.0).then_inc(s_pc, 1)
            pool.wait_ge(s_pc, 3)
            nc.gpsimd.memset(padrec[:, :, 1], 65536.0).then_inc(s_padm, 1)
            nc.gpsimd.iota(colid[:, :], [[P, NCH]], base=0, channel_multiplier=1,
                           allow_small_or_imprecise_dtypes=True).then_inc(s_colid, 1)
            nc.gpsimd.affine_select(out=below[:, :], in_=ones[:, :], compare_op=ALU.is_gt, fill=0.0, base=0,
                                    pattern=[[1, P]], channel_multiplier=-1).then_inc(s_const, 1)
            nc.gpsimd.affine_select(out=ident[:, :], in_=ident[:, :], compare_op=ALU.not_equal, fill=1.0, base=0,
                                    pattern=[[-1, P]], channel_multiplier=1).then_inc(s_const, 1)
            nc.gpsimd.iota(lane[:, :], [[1, P]], base=0, channel_multiplier=0,
                           allow_small_or_imprecise_dtypes=True).then_inc(s_const, 1)
            for a, n, v in ((0, MAIN[0], 0), (MAIN[0], MAIN[1], B_AT), (MT, RING, 0),
                            (OV0[0], OVER[0], MAIN[0]), (OV0[1], OVER[1], B_AT + MAIN[1])):
                nc.gpsimd.iota(vrow[:, a:a + n], [[1, n]], base=v, channel_multiplier=0,
                               allow_small_or_imprecise_dtypes=True).then_inc(s_const, 1)
            nc.gpsimd.affine_select(out=valid[:, :], in_=ones[:, 0:1], compare_op=ALU.is_gt, fill=0.0, base=LAST,
                                    pattern=[[0, 1]], channel_multiplier=-1).then_inc(s_const, 1)
            nc.gpsimd.iota(tokid[:, :], [[P, NT]], base=0, channel_multiplier=1).then_inc(s_const, 1)
            pool.wait_ge(s_uns, 1)
            pool.wait_ge(s_recw, 32)
            recs = rec_dram.rearrange("r (e c) -> (r e) c", c=REC)
            unsorted = pool.value_load(unsI[0:1, 0:1], min_val=0, max_val=E)

            def scatter(i):
                nc.gpsimd.tensor_copy(rec4[:, :, :], recE[:, bass.ds(i * 4, 4), :]).then_inc(s_c4, 1)
                nc.gpsimd.tensor_copy(idx4[:, :], slotI[:, bass.ds(i * 4, 4)]).then_inc(s_c4, 1)
                hold(pool, s_c4, i * 2 + 2)
                for k in range(4):
                    pool.indirect_dma_start(recs, bass.IndirectOffsetOnAxis(ap=idx4[:, k:k + 1], axis=0),
                                            rec4[:, k, :], None).then_inc(s_scat, 16)

            with pool.If(unsorted > 0):
                pool.wait_ge(s_slot, 1)
                scatter(0)
                with pool.Fori(1, EC // 4) as i:
                    hold(pool, s_scat, 64 * i)
                    scatter(i)
                pool.wait_ge(s_scat, 64 * (EC // 4))
            pool.wait_ge(s_rsel, 1)
            for c in range(NCH):
                n = min(P, COLS - c * P)
                pool.indirect_dma_start(ring[0:n, c, :], None, rec_dram,
                                        bass.IndirectOffsetOnAxis(ap=rowsel[0:n, c:c + 1], axis=0)).then_inc(s_rowg, 16)
            needed = [pool.value_load(flagI[0:1, h:h + 1], min_val=0, max_val=HALF_MAX) for h in range(2)]
            with pool.Fori(0, L) as l:
                hold(pool, s_st, (l + 1) * NT * 16)

                def gather(t, k):
                    hold(pool, s_free, l * MT + t + 1)
                    pool.indirect_dma_start(ring[:, k, :], None, xb_dram,
                                            bass.IndirectOffsetOnAxis(ap=cur[:, k:k + 1], axis=0)).then_inc(s_g[k], 16)

                for h, first, groups, rest in halves(l):
                    with pool.Fori(0, groups) as g:
                        for k in range(RING):
                            gather(first + g * RING + k, (first + k) % RING)
                    for k in range(rest):
                        gather(first + groups * RING + k, (first + k) % RING)
                    with pool.If(needed[h] > MAIN[h]):
                        with pool.Fori(0, OVER[h]) as o:
                            hold(pool, s_ou[h], l * OVER[h] + o + 1)
                            nc.gpsimd.tensor_copy(ovi[:, :], idxT[:, bass.ds(o + OV0[h], 1)]).then_inc(s_oi[h], 1)
                            hold(pool, s_oi[h], l * OVER[h] + o + 1)
                            pool.indirect_dma_start(ovx[:, :], None, xb_dram,
                                                    bass.IndirectOffsetOnAxis(ap=ovi[:, :], axis=0)).then_inc(s_og[h], 16)
            pool.wait_ge(s_const, 12)
            pool.wait_ge(s_ztw, 16)
            pool.wait_ge(s_tabx, 1)
            for k in range(KX):
                for t in range(NT):
                    n = min(P, N - t * P)
                    pool.indirect_dma_start(tok_dram, bass.IndirectOffsetOnAxis(ap=tabx[0:n, k, t:t + 1], axis=0),
                                            tokid[0:n, t:t + 1], None).then_inc(s_scx, 16)
            pool.wait_ge(s_tok, 16)
            pool.wait_ge(s_xnw, 16 * NT)

            def tokens(g):
                if not isinstance(g, int):
                    hold(pool, s_tx, g * WR)
                nc.gpsimd.tensor_copy(icur[:, :], tokT[:, bass.ds(g * WR, WR)]).then_inc(s_ic, 1)
                hold(pool, s_ic, g + 1)
                for k in range(WR):
                    pool.indirect_dma_start(xe[:, k, :], None, xn_dram,
                                            bass.IndirectOffsetOnAxis(ap=icur[:, k:k + 1], axis=0)).then_inc(s_xg[k], 16)

            tokens(0)
            with pool.Fori(1, NX // WR) as g:
                tokens(g)
            pool.wait_ge(s_xrt, 1)
            over = pool.value_load(nov[0:1, 0:1], min_val=0, max_val=XOVER)
            with pool.If(over > 0):
                pool.wait_ge(s_tx, NX)

                def over_tokens(o):
                    if not isinstance(o, int):
                        hold(pool, s_vp, o * 4)
                    nc.gpsimd.tensor_copy(icur[:, 0:1], tokT[:, bass.ds(o + NX, 1)]).then_inc(s_vi, 1)
                    hold(pool, s_vi, o + 1)
                    pool.indirect_dma_start(xe[:, 0, :], None, xn_dram,
                                            bass.IndirectOffsetOnAxis(ap=icur[:, 0:1], axis=0)).then_inc(s_vg, 16)

                over_tokens(0)
                with pool.Fori(1, XOVER) as o:
                    over_tokens(o)
                pool.wait_ge(s_vs, 16 * XOVER)
            pool.wait_ge(s_tx, NX)
            for k in range(WR):
                pool.wait_ge(s_ys[k], 16 * (NX // WR))
            for u in range(KX * NT):
                at_least(pool, s_fa2, u - RING + 1)
                n = min(P, N - u // KX * P)
                pool.indirect_dma_start(ring[0:n, u % RING, :], None, y_dram,
                                        bass.IndirectOffsetOnAxis(ap=slotx[0:n, u % KX, u // KX:u // KX + 1], axis=0)
                                        ).then_inc(s_yg[u % RING], 16)

        @block.scalar
        def _(act):
            chain = Chain(act, s_act)
            act.wait_ge(s_ldd, 32)
            nc.scalar.copy(recE[:, :, 1], dstE[:, 0:EC]).then_inc(s_rec, 1)
            act.wait_ge(s_lde, 32)
            nc.scalar.copy(recE[:, :, 0], srcE[:, :]).then_inc(s_rec, 1)
            nc.scalar.copy(recE[:, :, 2], ewE[:, :]).then_inc(s_rec, 1)
            act.wait_ge(s_ln, 1)
            nc.scalar.activation(t1[:, :], t0[:, :], ACT.Sqrt).then_inc(s_lnq, 1)
            act.wait_ge(s_idx, 1)
            nc.scalar.copy(cur[:, :], idxT[:, 0:RING]).then_inc(s_first, 1)
            act.wait_ge(s_first, 1)
            act.sem_inc(s_free, RING)
            needed = [act.value_load(flagI[0:1, h:h + 1], min_val=0, max_val=HALF_MAX) for h in range(2)]
            with act.Fori(0, L) as l:
                def message(t, k):
                    act.wait_ge(s_y, (l * MT + t + 1) * 2)
                    nc.scalar.activation(ring[:, k, :], ring[:, k, :], ACT.Relu).then_inc(s_m, 1)
                    nc.scalar.copy(cur[:, k:k + 1], idxT[:, bass.ds(t + RING, 1)]).then_inc(s_m, 1)

                def turned_in(t, bank):
                    act.wait_ge(s_tr, l * 36 + (t if t < HB else t - HB + 13) + 1)
                    nc.scalar.copy(hinT[:, :, t * P:(t + 1) * P],
                                   ps[:, bank, :].rearrange("p (k n) -> p k n", k=KC)).then_inc(s_ra, 1)

                def product(h, q, c, bank):
                    act.wait_ge(s_tr, l * 36 + h * 13 + HB + q * KC + c + 1)
                    nc.scalar.activation(h1T[:, c, bass.ds(q * 320 + h * HB * P, 320)], ps[:, bank, 0:320], ACT.Identity,
                                         bias=vec[:, 0, c:c + 1]).then_inc(s_ra, 1)

                with act.Fori(0, MAIN[0] // RING) as g:
                    for k in range(RING):
                        message(g * RING + k, k)
                for t in range(MAIN[0] // RING * RING, MAIN[0]):
                    message(t, t % RING)

                def overflow(h):
                    with act.If(needed[h] > MAIN[h]):
                        with act.Fori(0, OVER[h]) as o:
                            act.wait_ge(s_oy[h], (l * OVER[h] + o + 1) * 2)
                            nc.scalar.activation(ovx[:, :], ovx[:, :], ACT.Relu).then_inc(s_om[h], 1)

                overflow(0)
                hold(act, s_vec, l + 1)
                for t in range(PRE):
                    message(MAIN[0] + t, (MAIN[0] + t) % RING)
                    if t % RING == RING - 1:
                        for b in range(3) if t < RING else range(3, HB):
                            turned_in(b, 5 + b % 3)
                with act.Fori(0, 2) as q:
                    for c in range(KC):
                        for k in range(RING):
                            message(MAIN[0] + PRE + (q * KC + c) * RING + k, (MAIN[0] + k) % RING)
                        product(0, q, c, 6 + c % 2)
                for t in range(MAIN[0] + PRE + BODY, MT):
                    message(t, t % RING)
                overflow(1)
                for b in range(HB):
                    turned_in(HB + b, 5 + (13 + b) % 3)
                for q in range(2):
                    for c in range(KC):
                        product(1, q, c, 5 + (13 + HB + q * KC + c) % 3)
                act.wait_ge(s_var, 1 + l + 1)
                nc.scalar.activation(bsq[:, :], bve[:, :], ACT.Sqrt).then_inc(s_root, 1)
                act.wait_ge(s_bn, l + 1)
                for q in range(4):
                    for c in range(KC):
                        v = h1T[:, c, q * 320:(q + 1) * 320]
                        nc.scalar.activation(v, v, ACT.Relu, bias=bshift[:, c:c + 1],
                                             scale=bscale[:, c:c + 1]).then_inc(s_gt, 1)
                for t in range(NT):
                    act.wait_ge(s_rd, 10 + l * NT + t + 1)
                    nc.scalar.activation(xs[:, t, :], xs[:, t, :], ACT.Relu).then_inc(s_xs, 1)
            act.wait_ge(s_ln, 2)
            nc.scalar.activation(t1[:, :], t0[:, :], ACT.Sqrt).then_inc(s_lnq, 1)
            for t in range(NT):
                act.wait_ge(s_tr2, t + 1)
                nc.scalar.copy(hinT[:, :, t * P:(t + 1) * P],
                               ps[:, 5 + t % 3, :].rearrange("p (k n) -> p k n", k=KC)).then_inc(s_ra2, 1)
            act.wait_ge(s_gat, 1)
            nc.scalar.activation(sgm[:, :, :], m8[:, :, 0:KX], ACT.Sigmoid).then_inc(s_sgm, 1)
            for u in range(16):
                act.wait_ge(s_sp, u + 1)
                at_least(act, s_shh, u - 1)
                nc.scalar.activation(shsig[:, u % 2, :], ps[:, 4 + u % 2 * 2, 0:320], ACT.Sigmoid).then_inc(s_ssg, 1)

            def turned(j, k):
                act.wait_ge(s_tx, j + 1)
                at_least(act, s_g1, j - 1)
                nc.scalar.copy(xeT[:, k % 2, :, :].rearrange("p k n -> p (k n)"), ps[:, k % 2, :]).then_inc(s_xt, 1)

            def sigmoid(j, k):
                act.wait_ge(s_g1, j + 1)
                at_least(act, s_hh, j - 1)
                nc.scalar.activation(sg[:, k % 2, :], ps[:, 2 + k % 2, 0:HX], ACT.Sigmoid).then_inc(s_sig, 1)

            def result(j, k, turn):
                act.wait_ge(s_g2, j + 1)
                at_least(act, s_ys[k], turn * 16)
                nc.scalar.copy(ysb[:, k, :], ps[:, 6 + k % 2, :]).then_inc(s_yc, 1)

            def step(g, k):
                j = g * WR + k
                static = isinstance(j, int)
                if not static or j < NX:
                    sigmoid(j, k)
                if not static or j + 1 < NX:
                    turned(j + 1, (k + 1) % WR)
                if not static or j >= 2:
                    result(j - 2, (k - 2) % WR, g + (k - 2) // WR)

            turned(0, 0)
            for k in range(WR):
                step(0, k)
            with act.Fori(1, NX // WR - 1) as g:
                for k in range(WR):
                    step(g, k)
            for k in range(WR + 2):
                step(NX // WR - 1 + k // WR, k % WR)
            act.wait_ge(s_xrt, 1)
            over = act.value_load(nov[0:1, 0:1], min_val=0, max_val=XOVER)
            with act.If(over > 0):
                act.wait_ge(s_ys[0], 16 * (NX // WR))

                def over_act(o):
                    act.wait_ge(s_vp, o * 4 + 1)
                    nc.scalar.copy(xeT[:, 0, :, :].rearrange("p k n -> p (k n)"), ps[:, 0, :]).then_inc(s_va, 1)
                    act.wait_ge(s_vp, o * 4 + 2)
                    nc.scalar.activation(sg[:, 0, :], ps[:, 2, 0:HX], ACT.Sigmoid).then_inc(s_va, 1)
                    act.wait_ge(s_vp, o * 4 + 4)
                    at_least(act, s_vs, o * 16)
                    nc.scalar.copy(ysb[:, 0, :], ps[:, 6, :]).then_inc(s_va, 1)

                over_act(0)
                with act.Fori(1, XOVER) as o:
                    over_act(o)

        @block.vector
        def _(dve):
            chain = Chain(dve, s_dve)
            V = nc.vector

            def rsqrt_step():
                chain(V.reciprocal(t1[:, :], t1[:, :]))
                chain(V.tensor_tensor(t2[:, :], t1[:, :], t1[:, :], ALU.mult))
                chain(V.tensor_tensor(t2[:, :], t2[:, :], t0[:, :], ALU.mult))
                chain(V.tensor_scalar(t2[:, :], t2[:, :], -0.5, 1.5, ALU.mult, ALU.add))
                chain(V.tensor_tensor(t1[:, :], t1[:, :], t2[:, :], ALU.mult))

            dve.sem_inc(s_hin, 1)
            dve.sem_inc(s_var, 1)
            V.memset(zeros_h[:, :], 0.0).then_inc(s_zro, 1)
            V.memset(ztab[:, :], 0).then_inc(s_ztab, 1)
            chain(V.memset(zrow[:, :], 0.0))
            dve.wait_ge(s_colid, 1)
            chain(V.tensor_copy(vcol[:, :], colid[:, :]))
            shift = 0
            for a, v in ((MAIN[0], B_AT), (MT, 0), (OV0[0], MAIN[0]), (OV0[1], B_AT + MAIN[1])):
                chain(V.tensor_scalar(tcol[:, :], colid[:, :], float(a), float(v - a - shift), ALU.is_ge, ALU.mult))
                chain(V.tensor_tensor(vcol[:, :], vcol[:, :], tcol[:, :], ALU.add))
                shift = v - a
            dve.wait_ge(s_ldd, 32)
            chain(V.tensor_scalar(buckI[:, :], dstE[:, :], 7, None, ALU.arith_shift_right))
            chain(V.tensor_copy(buckE[:, :], buckI[:, :]))
            for b in range(NT):
                chain.mark(V.tensor_scalar(memb[:, b, :], buckE[:, 0:EC], float(b), None, ALU.is_equal))
            chain(V.tensor_tensor(memb[:, NT, :], buckE[:, 0:EC], buckE[:, 1:EC + 1], ALU.is_gt))
            V.tensor_reduce(rowtot[:, :], memb[:, :, :], AX.X, ALU.add).then_inc(s_rot, 1)
            dve.wait_ge(s_cntp, 2)
            chain(V.tensor_copy(cnt[:, :], ps[:, 1, 0:NT + 1]))
            V.tensor_copy(unsI[:, :], cnt[0:1, NT:NT + 1]).then_inc(s_uns, 1)
            chain(V.tensor_tensor_scan(upto[:, :], cnt[:, 0:NT], zrow[:, 0:NT], 0.0, ALU.add, ALU.add))
            chain(V.tensor_tensor(start[:, :], upto[:, :], cnt[:, 0:NT], ALU.subtract))
            chain.mark(V.tensor_copy(rowI[:, 0, :], start[:, :]))
            chain(V.tensor_scalar(rowI[:, 1, :], upto[:, :], -1.0, None, ALU.add))
            chain(V.tensor_scalar(rowI[:, :, :], rowI[:, :, :], 7, None, ALU.arith_shift_right))
            chain(V.tensor_copy(row01[:, :, :], rowI[:, :, :]))
            chain(V.scalar_tensor_tensor(tiles[:, :], row01[:, 1, :], 1.0, row01[:, 0, :], ALU.add, ALU.subtract))
            for h in range(2):
                s = slice(h * HB, (h + 1) * HB)
                chain(V.tensor_tensor_scan(TS[:, s], tiles[:, s], zrow[:, 0:HB], float(h * B_AT), ALU.add, ALU.add))
            chain.mark(V.tensor_scalar(flagI[0:1, 0:1], TS[0:1, HB - 1:HB], 0.0, None, ALU.add))
            chain(V.tensor_scalar(flagI[0:1, 1:2], TS[0:1, NT - 1:NT], float(-B_AT), None, ALU.add))
            chain.mark(V.memset(Dd[:, 0:1], 0.0))
            chain(V.tensor_tensor(TS[:, :], TS[:, :], tiles[:, :], ALU.subtract))
            chain(V.tensor_tensor(Dd[:, 1:NT + 1], row01[:, 0, :], TS[:, :], ALU.subtract))
            chain(V.tensor_tensor(DD[:, :], Dd[:, 1:NT + 1], Dd[:, 0:NT], ALU.subtract))
            cols = [P, NCH, NT]
            chain(V.tensor_tensor(ccol[:, :, :], vcol[:, :].unsqueeze(2).broadcast_to(cols),
                                  TS[:, :].unsqueeze(1).broadcast_to(cols), ALU.is_ge))
            chain(V.tensor_tensor(ccol[:, :, :], ccol[:, :, :], DD[:, :].unsqueeze(1).broadcast_to(cols), ALU.mult))
            chain(V.tensor_reduce(tcol[:, :], ccol[:, :, :], AX.X, ALU.add))
            chain(V.tensor_tensor(tcol[:, :], tcol[:, :], vcol[:, :], ALU.add))
            V.tensor_scalar(rowsel[:, :], tcol[:, :], float(FULL), None, ALU.min).then_inc(s_rsel, 1)
            unsorted = dve.value_load(unsI[0:1, 0:1], min_val=0, max_val=E)
            with dve.If(unsorted > 0):
                slots = Chain(dve, s_gen)
                slots(V.tensor_tensor(prior[:, :], ps[0:EP, 0, 0:NT], start[0:EP, :], ALU.add))
                for b in range(NT):
                    slots(V.tensor_tensor_scan(cumu[:, b, :], memb[:, b, :], zrow[0:EP, :], 0.0, ALU.add, ALU.add))
                    slots(V.tensor_scalar(slotT[:, :], cumu[:, b, :], prior[:, b:b + 1], -1.0, ALU.add, ALU.add))
                    slots(V.tensor_tensor(slotT[:, :], slotT[:, :], memb[:, b, :], ALU.mult))
                    if b == 0:
                        slots(V.tensor_copy(slotF[:, :], slotT[:, :]))
                    else:
                        slots(V.tensor_tensor(slotF[:, :], slotF[:, :], slotT[:, :], ALU.add))
                V.tensor_copy(slotI[:, :], slotF[:, :]).then_inc(s_slot, 1)
            dve.wait_ge(s_ldx, 48)
            for t in range(NT):
                chain(V.bn_stats(st[:, t, :], hin[:, t, :]))
                chain(V.bn_aggr(mv[:, t, :], st[:, t, :]))
            V.tensor_scalar(t0[:, :], mv[:, :, 1], LN_EPS, None, ALU.add).then_inc(s_ln, 1)
            dve.wait_ge(s_lnq, 1)
            rsqrt_step()
            dve.wait_ge(s_lbe, 16)
            for t in range(NT):
                chain(V.tensor_scalar(xs[:, t, :], hin[:, t, :], mv[:, t, 0:1], t1[:, t:t + 1], ALU.subtract, ALU.mult))
                V.tensor_tensor(hin[:, t, :], xs[:, t, :], beb[:, :], ALU.add).then_inc(s_sg, 1)
            dve.wait_ge(s_plane, 1)
            V.tensor_copy(idxT[:, :], ps[:, 0, 0:COLS]).then_inc(s_idx, 1)
            chain(V.tensor_copy(wT[:, :], ps[:, 2, 0:COLS]))
            chain(V.tensor_scalar(epsb[:, :], epsb[:, :], 1.0, None, ALU.add))
            dve.wait_ge(s_const, 11)
            chain(V.tensor_scalar(brow[:, :], vrow[:, :], 0.0, -1.0, ALU.mult, ALU.add))
            for b in range(NT):
                chain(V.scalar_tensor_tensor(brow[:, :], vrow[:, :], TS[:, b:b + 1], brow[:, :], ALU.is_ge, ALU.add))
            chain(V.scalar_tensor_tensor(dloc[:, :], brow[:, :], float(-P), ps[:, 1, 0:COLS], ALU.mult, ALU.add))
            chain(V.tensor_scalar(tmpc[:, :], vrow[:, :], float(B_AT), float(-HB), ALU.is_ge, ALU.mult))
            chain(V.tensor_tensor(tmpc[:, :], tmpc[:, :], brow[:, :], ALU.add))
            V.tensor_copy(bankI[:, :], tmpc[:, :]).then_inc(s_tab, 1)
            dve.wait_ge(s_vt, 1)
            chain(V.tensor_copy(vecs[:, :, :, :].rearrange("p v l c -> p (v l c)"), ps[:, 7, 0:3 * L * KC]))
            dve.wait_ge(s_gt4, 1)
            chain(V.tensor_copy(gT[:, :, :].rearrange("p k e -> p (k e)"), ps[:, 6, 0:KC * NX]))
            dve.sem_inc(s_rd, 10)
            needed = [dve.value_load(flagI[0:1, h:h + 1], min_val=0, max_val=HALF_MAX) for h in range(2)]
            with dve.Fori(0, L) as l:
                chain.enter(l, CH_LAYER)
                V.tensor_copy(vec[:, :, :], vecs[:, :, bass.ds(l, 1), :].rearrange("p v o c -> p v (o c)")).then_inc(s_vec, 1)
                hold(dve, s_lwe, (l + 1) * 16)

                def edges(t, k, turn):
                    dve.wait_ge(s_g[k], (l * (MT // RING) + turn + 1) * 16)
                    V.tensor_scalar(oneh[:, k, :], lane[:, :], dloc[:, bass.ds(t, 1)], None, ALU.is_equal).then_inc(s_y, 1)
                    V.scalar_tensor_tensor(ring[:, k, :], web[:, :], wT[:, bass.ds(t, 1)], ring[:, k, :],
                                           ALU.mult, ALU.add).then_inc(s_y, 1)

                for h, first, groups, rest in halves(l):
                    with dve.Fori(0, groups) as g:
                        for k in range(RING):
                            edges(first + g * RING + k, (first + k) % RING, g + (first + k) // RING)
                    for k in range(rest):
                        edges(first + groups * RING + k, (first + k) % RING, groups + (first + k) // RING)
                    with dve.If(needed[h] > MAIN[h]):
                        with dve.Fori(0, OVER[h]) as o:
                            dve.wait_ge(s_og[h], (l * OVER[h] + o + 1) * 16)
                            V.tensor_scalar(ovh[:, :], lane[:, :], dloc[:, bass.ds(o + OV0[h], 1)], None,
                                            ALU.is_equal).then_inc(s_oy[h], 1)
                            V.scalar_tensor_tensor(ovx[:, :], web[:, :], wT[:, bass.ds(o + OV0[h], 1)], ovx[:, :],
                                                   ALU.mult, ALU.add).then_inc(s_oy[h], 1)
                        hold(dve, s_ou[h], (l + 1) * OVER[h] + 1)
                    dve.wait_ge(s_free, RING + l * MT + first + MAIN[h])
                    for b in range(HB):
                        t = h * HB + b
                        V.scalar_tensor_tensor(hin[:, t, :], xs[:, t, :], epsb[:, bass.ds(l, 1)], ps[:, b, :],
                                               ALU.mult, ALU.add).then_inc(s_hin, 1)
                for h in range(2):
                    for q in range(2):
                        for c in range(KC):
                            a = h * HB * P + q * 320
                            n = min(320, N - a)
                            dve.wait_ge(s_ra, l * 26 + h * 13 + HB + q * KC + c + 1)
                            chain.mark(V.bn_stats(bst[:, c, h * 2 + q, :], h1T[:, c, a:a + n]))
                hold(dve, s_dve, chain.count())
                for c in range(KC):
                    chain.mark(V.bn_aggr(bmv[:, c, :], bst[:, c, :, :].rearrange("p a b -> p (a b)")))
                chain.wait()
                V.tensor_scalar(bve[:, :], bmv[:, :, 1], BN_EPS, None, ALU.add).then_inc(s_var, 1)
                dve.wait_ge(s_root, l + 1)
                chain(V.reciprocal(brs[:, :], bsq[:, :]))
                chain(V.tensor_tensor(bt[:, :], brs[:, :], brs[:, :], ALU.mult))
                chain(V.tensor_tensor(bt[:, :], bt[:, :], bve[:, :], ALU.mult))
                chain(V.tensor_scalar(bt[:, :], bt[:, :], -0.5, 1.5, ALU.mult, ALU.add))
                chain(V.tensor_tensor(brs[:, :], brs[:, :], bt[:, :], ALU.mult))
                dve.wait_ge(s_vec, l + 1)
                chain(V.tensor_tensor(bscale[:, :], brs[:, :], vec[:, 1, :], ALU.mult))
                chain(V.tensor_tensor(bt[:, :], bmv[:, :, 0], bscale[:, :], ALU.mult))
                V.tensor_tensor(bshift[:, :], vec[:, 2, :], bt[:, :], ALU.subtract).then_inc(s_bn, 1)
                hold(dve, s_lw2, (l + 1) * 32)
                with dve.If(l < L - 1):
                    hold(dve, s_lbe, (l + 2) * 16)
                for t in range(NT + 1):
                    if t < NT:
                        dve.wait_ge(s_tr, l * 36 + 26 + t + 1)
                        V.tensor_tensor(xs[:, t, :], ps[:, 5 + (26 + t) % 3, :], b2b[:, :], ALU.add).then_inc(s_rd, 1)
                    if t >= 1:
                        dve.wait_ge(s_xs, l * NT + t)
                        V.tensor_tensor(hin[:, t - 1, :], xs[:, t - 1, :], beb[:, :], ALU.add).then_inc(s_sg, 1)
                chain.leave(L)
            dve.wait_ge(s_ldx, 80)
            for t in range(NT):
                chain(V.tensor_tensor(xs[:, t, :], xres[:, t, :], xs[:, t, :], ALU.add))
                chain(V.bn_stats(st[:, t, :], xs[:, t, :]))
                chain(V.bn_aggr(mv[:, t, :], st[:, t, :]))
            V.tensor_scalar(t0[:, :], mv[:, :, 1], LN_EPS, None, ALU.add).then_inc(s_ln, 1)
            dve.wait_ge(s_lnq, 2)
            rsqrt_step()
            for t in range(NT):
                V.tensor_scalar(hin[:, t, :], xs[:, t, :], mv[:, t, 0:1], t1[:, t:t + 1], ALU.subtract, ALU.mult).then_inc(s_xn, 1)
            dve.wait_ge(s_lg, 1)
            chain(V.tensor_copy(lg[:, :, :].rearrange("p t e -> p (t e)")[:, 0:D], ps[:, 0, :]))
            chain(V.tensor_copy(lg[:, :, :].rearrange("p t e -> p (t e)")[:, D:NT * NX], ps[:, 1, 0:NT * NX - D]))
            for t in range(NT):
                chain.mark(V.max(m8[:, t, :], lg[:, t, :]))
            chain.wait()
            dve.sem_inc(s_gat, 1)
            for t in range(NT):
                chain.mark(V.max_index(i8[:, t, :], m8[:, t, :], lg[:, t, :]))
            chain.wait()
            chain(V.tensor_copy(i8f[:, :, :], i8[:, :, :]))
            every = [P, NT, NX]
            for k in range(KX):
                chain(V.tensor_tensor(oh[k][:, :, :], lane[:, 0:NX].unsqueeze(1).broadcast_to(every),
                                      i8f[:, :, k:k + 1].broadcast_to(every), ALU.is_equal))
                chain(V.tensor_scalar(oh[k][:, NT - 1, :], oh[k][:, NT - 1, :], valid[:, :], None, ALU.mult))
            chain(V.tensor_tensor(both[:, :, :], oh[0][:, :, :], oh[1][:, :, :], ALU.add))
            chain(V.memset(run[:, 0, :], 0.0))
            for t in range(NT):
                chain(V.tensor_tensor(run[:, t + 1, :], run[:, t, :], both[:, t, :], ALU.add))
            V.tensor_scalar(b128[:, :], lane[:, 0:NX], float(P), None, ALU.mult).then_inc(s_run, 1)

            def shared(u):
                q, c = divmod(u, KC)
                v = h1T[:, c, q * 320:(q + 1) * 320]
                dve.wait_ge(s_ssg, u + 1)
                chain(V.tensor_tensor(v, shsig[:, u % 2, :], ps[:, 4 + u % 2 * 2, 0:320], ALU.mult))
                V.tensor_tensor(v, v, ps[:, 5 + u % 2 * 2, 0:320], ALU.mult).then_inc(s_shh, 1)

            shared(0)
            shared(1)
            dve.wait_ge(s_pos, 1)
            flat = pos[:, :, :].rearrange("p t e -> p (t e)")
            chain.mark(V.tensor_copy(flat[:, 0:D], ps[:, 2, :]))
            chain.mark(V.tensor_copy(flat[:, D:NT * NX], ps[:, 3, 0:NT * NX - D]))
            chain(V.tensor_copy(cntx[:, :], ps[:, 3, 256:256 + NX]))
            chain(V.tensor_scalar(ovn[:, :], cntx[:, :], float(P - 1), None, ALU.add))
            chain(V.tensor_copy(ovnI[:, :], ovn[:, :]))
            chain(V.tensor_scalar(ovnI[:, :], ovnI[:, :], 7, None, ALU.arith_shift_right))
            chain(V.tensor_copy(ovn[:, :], ovnI[:, :]))
            chain(V.tensor_scalar(ovn[:, :], ovn[:, :], -1.0, 0.0, ALU.add, ALU.max))
            chain(V.tensor_tensor_scan(ovs[:, :], ovn[:, :], zrow[:, 0:NX], 0.0, ALU.add, ALU.add))
            chain(V.tensor_copy(nov[:, :], ovs[:, NX - 1:NX]))
            chain(V.tensor_tensor(bdif[:, :], ovs[:, :], ovn[:, :], ALU.subtract))
            chain(V.tensor_scalar(bdif[:, :], bdif[:, :], float(NX - 1), float(P), ALU.add, ALU.mult))
            chain(V.tensor_tensor(bdif[:, :], bdif[:, :], b128[:, :], ALU.subtract))
            chain(V.tensor_scalar(slotm[:, :, :], pos[:, :, :], float(P), None, ALU.is_ge))
            chain(V.tensor_tensor(slotm[:, :, :], slotm[:, :, :], bdif[:, :].unsqueeze(1).broadcast_to(every), ALU.mult))
            chain(V.tensor_tensor(slotm[:, :, :], slotm[:, :, :], b128[:, :].unsqueeze(1).broadcast_to(every), ALU.add))
            chain(V.tensor_tensor(slotm[:, :, :], slotm[:, :, :], pos[:, :, :], ALU.add))
            for k in range(KX):
                chain(V.tensor_tensor(lg[:, :, :], oh[k][:, :, :], slotm[:, :, :], ALU.mult))
                chain(V.tensor_reduce(sel[:, k, :], lg[:, :, :], AX.X, ALU.add))
                chain(V.tensor_tensor(lg[:, :, :], oh[k][:, :, :], pos[:, :, :], ALU.mult))
                chain(V.tensor_reduce(selp[:, k, :], lg[:, :, :], AX.X, ALU.add))
            chain.mark(V.tensor_copy(slotx[:, :, :], sel[:, :, :]))
            chain(V.tensor_copy(selI[:, :, :], sel[:, :, :]))
            chain(V.tensor_scalar(hiI[:, :, :], selI[:, :, :], 7, None, ALU.arith_shift_right))
            chain(V.tensor_scalar(selI[:, :, :], selI[:, :, :], P - 1, None, ALU.bitwise_and))
            V.scalar_tensor_tensor(tabx[:, :, :], selI[:, :, :], float(XT), hiI[:, :, :], ALU.mult, ALU.add).then_inc(s_tabx, 1)
            dve.wait_ge(s_sgm, 1)
            chain(V.tensor_tensor(gden[:, :], sgm[:, :, 0], sgm[:, :, 1], ALU.add))
            chain(V.tensor_scalar(gden[:, :], gden[:, :], 1e-20, None, ALU.add))
            chain(V.reciprocal(gden[:, :], gden[:, :]))
            chain(V.tensor_scalar(selp[:, :, :], selp[:, :, :], float(CAP), SCALE, ALU.is_lt, ALU.mult))
            for k in range(KX):
                chain(V.tensor_tensor(gate[:, k, :], sgm[:, :, k], gden[:, :], ALU.mult))
                chain(V.tensor_tensor(gate[:, k, :], gate[:, k, :], selp[:, k, :], ALU.mult))
            ovall = [P, XOVER, NX]
            chain(V.tensor_tensor(cmpx[:, :, :], lane[:, 0:XOVER].unsqueeze(2).broadcast_to(ovall),
                                  ovs[:, :].unsqueeze(1).broadcast_to(ovall), ALU.is_ge))
            chain(V.tensor_reduce(eovF[:, :], cmpx[:, :, :], AX.X, ALU.add))
            chain(V.tensor_scalar(eovF[:, :], eovF[:, :], float(NX - 1), None, ALU.min))
            V.tensor_copy(eovI[:, :], eovF[:, :]).then_inc(s_xrt, 1)
            for u in range(2, 16):
                shared(u)
            for t in range(NT):
                dve.wait_ge(s_so, t + 1)
                V.tensor_tensor(xs[:, t, :], xs[:, t, :], ps[:, t % 2, :], ALU.add).then_inc(s_sod, 1)

            def hidden(j, k):
                dve.wait_ge(s_sig, j + 1)
                at_least(dve, s_th, j - 1)
                V.tensor_tensor(hh[:, k % 2, :], sg[:, k % 2, :], ps[:, 2 + k % 2, 0:HX], ALU.mult).then_inc(s_hm, 1)
                dve.wait_ge(s_hm, j + 1)
                V.tensor_tensor(hh[:, k % 2, :], hh[:, k % 2, :], ps[:, 2 + k % 2, HX:2 * HX], ALU.mult).then_inc(s_hh, 1)

            def hidden_turned(j, k):
                dve.wait_ge(s_th, j + 1)
                at_least(dve, s_g2, j - 1)
                hold(dve, s_th, j + 1)
                V.tensor_copy(hT[:, k % 2, :, :].rearrange("p k n -> p (k n)"), ps[:, 4 + k % 2, 0:XC * P]).then_inc(s_ht, 1)

            def step(g, k):
                j = g * WR + k
                static = isinstance(j, int)
                if not static or j < NX:
                    hidden(j, k)
                if not static or 1 <= j <= NX:
                    hidden_turned(j - 1, (k - 1) % WR)

            for k in range(WR):
                step(0, k)
            with dve.Fori(1, NX // WR - 1) as g:
                for k in range(WR):
                    step(g, k)
            for k in range(WR + 1):
                step(NX // WR - 1 + k // WR, k % WR)
            over = dve.value_load(nov[0:1, 0:1], min_val=0, max_val=XOVER)
            with dve.If(over > 0):
                with dve.Fori(0, XOVER) as o:
                    dve.wait_ge(s_va, o * 3 + 2)
                    V.tensor_tensor(hh[:, 0, :], sg[:, 0, :], ps[:, 2, 0:HX], ALU.mult).then_inc(s_vd, 1)
                    dve.wait_ge(s_vd, o * 3 + 1)
                    V.tensor_tensor(hh[:, 0, :], hh[:, 0, :], ps[:, 2, HX:2 * HX], ALU.mult).then_inc(s_vd, 1)
                    hold(dve, s_vp, o * 4 + 3)
                    V.tensor_copy(hT[:, 0, :, :].rearrange("p k n -> p (k n)"), ps[:, 4, 0:XC * P]).then_inc(s_vd, 1)
            for u in range(KX * NT):
                t, k = u // KX, u % KX
                n = min(P, N - t * P)
                dve.wait_ge(s_yg[u % RING], 16 * (u // RING + 1))
                if k:
                    dve.wait_ge(s_fa2, u)
                last = V.scalar_tensor_tensor(xs[0:n, t, :], ring[0:n, u % RING, :], gate[0:n, k, t:t + 1], xs[0:n, t, :],
                                              ALU.mult, ALU.add)
                last.then_inc(s_fa2, 1)
                if k:
                    dve.wait_ge(s_fa2, u + 1)
                    dve.sem_inc(s_fa, 1)

        @block.tensor
        def _(pe):
            T = nc.tensor
            pe.wait_ge(s_rot, 1)
            pe.wait_ge(s_const, 5)
            T.matmul(ps[0:EP, 0, 0:NT], below[0:EP, 0:EP], rowtot[:, 0:NT], start=True, stop=True).then_inc(s_cntp, 1)
            T.matmul(ps[:, 1, 0:NT + 1], ones[0:EP, :], rowtot[:, :], start=True, stop=True).then_inc(s_cntp, 1)
            pe.wait_ge(s_rowg, 16 * NCH)
            for f in range(3):
                for c in range(NCH):
                    n = min(P, COLS - c * P)
                    last = T.transpose(ps[:, f, c * P:c * P + n], ring[0:n, c, :].rearrange("p (e f) -> p f e", f=REC)[:, f, :],
                                       ident[0:n, 0:n])
            last.then_inc(s_plane, 1)
            pe.wait_ge(s_ldv, 48)
            T.transpose(ps[:, 7, 0:3 * L * KC], vrows[:, :], ident[0:3 * L * KC, 0:3 * L * KC]).then_inc(s_vt, 1)
            pe.wait_ge(s_gw, 16)
            for k in range(KC):
                last = T.transpose(ps[:, 6, k * NX:(k + 1) * NX], gw[:, :].rearrange("e (p k) -> e k p", k=KC)[:, k, :], ident[0:NX, 0:NX])
            last.then_inc(s_gt4, 1)
            pe.wait_ge(s_tab, 1)
            pe.wait_ge(s_zro, 1)
            pe.sem_inc(s_ou[0], 1)
            pe.sem_inc(s_ou[1], 1)
            needed = [pe.value_load(flagI[0:1, h:h + 1], min_val=0, max_val=HALF_MAX) for h in range(2)]
            with pe.Fori(0, L) as l:
                def clear(h):
                    for b in range(HB):
                        if h == 1:
                            pe.wait_ge(s_hin, 1 + l * NT + b + 1)
                        T.matmul(ps[:, b, :], zeros_h[:, 0:P], zeros_h[:, :], start=True, stop=False, skip_group_check=True)

                def add(t, k):
                    bank = pe.value_load(bankI[0:1, bass.ds(t, 1)], min_val=0, max_val=HB - 1)
                    pe.wait_ge(s_m, (l * MT + t + 1) * 2)
                    T.matmul(ps[:, bass.ds(bank, 1), :], oneh[:, k, :], ring[:, k, :], start=False, stop=False,
                             skip_group_check=True).then_inc(s_free, 1)

                def freed(u):
                    if u < 3:
                        pe.wait_ge(s_rd, 10 + (l * NT) + (u - 3 + 1 + 0) + 0)
                    elif u - 3 < 26:
                        pe.wait_ge(s_ra, l * 26 + u - 3 + 1)
                    else:
                        pe.wait_ge(s_rd, 10 + l * NT + u - 3 - 26 + 1)

                def overflow(h):
                    with pe.If(needed[h] > MAIN[h]):
                        with pe.Fori(0, OVER[h]) as o:
                            bank = pe.value_load(bankI[0:1, bass.ds(o + OV0[h], 1)], min_val=0, max_val=HB - 1)
                            pe.wait_ge(s_om[h], l * OVER[h] + o + 1)
                            T.matmul(ps[:, bass.ds(bank, 1), :], ovh[:, :], ovx[:, :], start=False, stop=False,
                                     skip_group_check=True).then_inc(s_ou[h], 1)

                def turn_in(t, use):
                    pe.wait_ge(s_hin, 1 + l * NT + t + 1)
                    freed(use)
                    for k in range(KC):
                        last = T.transpose(ps[:, 5 + use % 3, k * P:(k + 1) * P],
                                           hin[:, t, :].rearrange("p (d k) -> p k d", k=KC)[:, k, :], ident[:, :])
                    last.then_inc(s_tr, 1)

                def product(h, q, c, bank):
                    for k in range(KC):
                        last = T.matmul(ps[:, bank, 0:320], w1s[:, k, c * P:(c + 1) * P],
                                        hinT[:, k, bass.ds(q * 320 + h * HB * P, 320)], start=k == 0, stop=k == KC - 1)
                    last.then_inc(s_tr, 1)

                clear(0)
                with pe.Fori(0, MAIN[0] // RING) as g:
                    for k in range(RING):
                        add(g * RING + k, k)
                for t in range(MAIN[0] // RING * RING, MAIN[0]):
                    add(t, t % RING)
                overflow(0)
                clear(1)
                for t in range(PRE):
                    add(MAIN[0] + t, (MAIN[0] + t) % RING)
                    if t == RING // 2 - 1:
                        for b in range(3):
                            turn_in(b, b)
                    if t == RING // 2 + RING - 1:
                        for b in range(3, HB):
                            turn_in(b, b)
                hold(pe, s_lw1, (l + 1) * 16)
                with pe.Fori(0, 2) as q:
                    for c in range(KC):
                        for k in range(RING):
                            add(MAIN[0] + PRE + (q * KC + c) * RING + k, (MAIN[0] + k) % RING)
                            if k == RING // 2 - 1:
                                pe.wait_ge(s_ra, l * 26 + q * KC + c + HB + (0 if c < 1 else -1))
                                product(0, q, c, 6 + c % 2)
                for t in range(MAIN[0] + PRE + BODY, MT):
                    add(t, t % RING)
                overflow(1)
                pe.wait_ge(s_ra, l * 26 + 13)
                for b in range(HB):
                    turn_in(HB + b, 13 + b)
                pe.wait_ge(s_ra, l * 26 + 13 + HB)
                for q in range(2):
                    for c in range(KC):
                        use = 13 + HB + q * KC + c
                        freed(use)
                        product(1, q, c, 5 + use % 3)
                use = 26
                pe.wait_ge(s_lw2, (l + 1) * 32)
                for t in range(NT):
                    pe.wait_ge(s_gt, l * 16 + KC * (((t + 1) * P - 1) // 320 + 1))
                    freed(use)
                    for k in range(KC):
                        last = T.matmul(ps[:, 5 + use % 3, :], h1T[:, k, t * P:(t + 1) * P], w2s[:, k, :],
                                        start=k == 0, stop=k == KC - 1)
                    last.then_inc(s_tr, 1)
                    use += 1
            for t in range(NT):
                pe.wait_ge(s_xn, t + 1)
                at_least(pe, s_ra2, t - 2)
                for k in range(KC):
                    last = T.transpose(ps[:, 5 + t % 3, k * P:(k + 1) * P],
                                       hin[:, t, :].rearrange("p (d k) -> p k d", k=KC)[:, k, :], ident[:, :])
                last.then_inc(s_tr2, 1)
            for t in range(NT):
                pe.wait_ge(s_ra2, t + 1)
                for k in range(KC):
                    last = T.matmul(ps[:, t // 8, t % 8 * NX:(t % 8 + 1) * NX], hinT[:, k, t * P:(t + 1) * P], gT[:, k, :],
                                    start=k == 0, stop=k == KC - 1)
            last.then_inc(s_lg, 1)
            pe.wait_ge(s_swl, 48)

            def shared_up(u):
                q, c = divmod(u, KC)
                at_least(pe, s_shh, u - 1)
                for v, w in ((4, w1s), (5, w3s)):
                    for k in range(KC):
                        last = T.matmul(ps[:, v + u % 2 * 2, 0:320], w[:, k, c * P:(c + 1) * P], hinT[:, k, q * 320:(q + 1) * 320],
                                        start=k == 0, stop=k == KC - 1)
                last.then_inc(s_sp, 1)

            shared_up(0)
            shared_up(1)
            pe.wait_ge(s_run, 1)
            for t in range(NT):
                o = ps[:, 2 + t // 8, t % 8 * NX:(t % 8 + 1) * NX]
                T.matmul(o, below[:, :], both[:, t, :], start=True, stop=False)
                T.matmul(o, ones[:, :], run[:, t, :], start=False, stop=True)
            T.matmul(ps[:, 3, 256:256 + NX], ones[:, :], run[:, NT, :], start=True, stop=True).then_inc(s_pos, 1)
            for u in range(2, 16):
                shared_up(u)
            for t in range(NT):
                pe.wait_ge(s_shh, KC * (((t + 1) * P - 1) // 320 + 1))
                at_least(pe, s_sod, t - 1)
                for k in range(KC):
                    last = T.matmul(ps[:, t % 2, :], h1T[:, k, t * P:(t + 1) * P], w2s[:, k, :], start=k == 0, stop=k == KC - 1)
                last.then_inc(s_so, 1)
            pe.wait_ge(s_sod, NT)

            def turn_x(k):
                for c in range(KC):
                    last = T.transpose(ps[:, k % 2, c * P:(c + 1) * P],
                                       xe[:, k, :].rearrange("p (d k) -> p k d", k=KC)[:, c, :], ident[:, :])
                return last

            def up(k):
                for c in range(KC):
                    last = T.matmul(ps[:, 2 + k % 2, :], xeT[:, k % 2, c, :], w13[:, k, c, :, :].rearrange("p a n -> p (a n)"),
                                    start=c == 0, stop=c == KC - 1)
                return last

            def turn_h(k):
                for c in range(XC):
                    last = T.transpose(ps[:, 4 + k % 2, c * P:(c + 1) * P],
                                       hh[:, k % 2, :].rearrange("p (d k) -> p k d", k=XC)[:, c, :], ident[:, :])
                return last

            def down(k):
                for c in range(XC):
                    last = T.matmul(ps[:, 6 + k % 2, :], hT[:, k % 2, c, :], w2e[:, k, c, :], start=c == 0, stop=c == XC - 1)
                return last

            def turned(j, k, turn):
                pe.wait_ge(s_xg[k], (turn + 1) * 16)
                at_least(pe, s_xt, j - 1)
                turn_x(k).then_inc(s_tx, 1)

            def step(g, k):
                j = g * WR + k
                static = isinstance(j, int)
                if not static or j < NX:
                    pe.wait_ge(s_xt, j + 1)
                    pe.wait_ge(s_w[k], (g + 1) * 48)
                    at_least(pe, s_hh, j - 1)
                    up(k).then_inc(s_g1, 1)
                if not static or j + 1 < NX:
                    turned(j + 1, (k + 1) % WR, g + (k + 1) // WR)
                if not static or 1 <= j <= NX:
                    at_least(pe, s_hh, j)
                    at_least(pe, s_ht, j - 2)
                    turn_h((k - 1) % WR).then_inc(s_th, 1)
                if not static or j >= 2:
                    at_least(pe, s_ht, j - 1)
                    at_least(pe, s_yc, j - 3)
                    down((k - 2) % WR).then_inc(s_g2, 1)

            turned(0, 0, 0)
            for k in range(WR):
                step(0, k)
            with pe.Fori(1, NX // WR - 1) as g:
                for k in range(WR):
                    step(g, k)
            for k in range(WR + 2):
                step(NX // WR - 1 + k // WR, k % WR)
            pe.wait_ge(s_xrt, 1)
            over = pe.value_load(nov[0:1, 0:1], min_val=0, max_val=XOVER)
            with pe.If(over > 0):
                with pe.Fori(0, XOVER) as o:
                    pe.wait_ge(s_vg, o * 16 + 16)
                    turn_x(0).then_inc(s_vp, 1)
                    pe.wait_ge(s_va, o * 3 + 1)
                    pe.wait_ge(s_vw, o * 48 + 48)
                    up(0).then_inc(s_vp, 1)
                    pe.wait_ge(s_vd, o * 3 + 2)
                    turn_h(0).then_inc(s_vp, 1)
                    pe.wait_ge(s_vd, o * 3 + 3)
                    down(0).then_inc(s_vp, 1)


CH_LAYER = 16 + 4 + 7

_INS = ["x", "src", "dst", "edge_weight1", "L0_gnn_eps", "L0_gnn_We", "L0_gnn_be", "L0_gnn_W1", "L0_gnn_b1",
        "L0_gnn_gamma", "L0_gnn_beta", "L0_gnn_W2", "L0_gnn_b2", "L0_ffn_gate_w", "L0_ffn_w1", "L0_ffn_w3",
        "L0_ffn_w2", "L0_ffn_sw1", "L0_ffn_sw3", "L0_ffn_sw2"]


def kernel(**inputs):
    import numpy as np
    import concourse.bacc as bacc
    from concourse.bass_utils import run_bass_kernel_spmd as run

    nc = bacc.Bacc("TRN2", target_bir_lowering=False, num_devices=1)
    arrays, args = {}, []
    for name in _INS:
        a = np.ascontiguousarray(inputs[name])
        arrays[f"in_{name}"] = a
        args.append(nc.dram_tensor(f"in_{name}", a.shape, mybir.dt.from_np(a.dtype), kind="ExternalInput").ap())
    out = nc.dram_tensor("out", (N, D), F32, kind="ExternalOutput").ap()
    scratch = [nc.dram_tensor("x_rows", (NP, D), F32).ap(), nc.dram_tensor("records", (RROWS, P * REC), F32).ap(),
               nc.dram_tensor("token_rows", (NP, D), F32).ap(), nc.dram_tensor("token_table", (P * XT, 1), I32).ap(),
               nc.dram_tensor("expert_rows", (XT * P, D), F32).ap()]
    build(nc, *args, out, scratch)
    return run(nc, [arrays], core_ids=[0]).results[0]["out"]
```

```python
import concourse.bass as bass
from concourse import mybir
from contextlib import ExitStack

F32, BF16 = mybir.dt.float32, mybir.dt.bfloat16
I32, U32 = mybir.dt.int32, mybir.dt.uint32
ALU = mybir.AluOpType
ACT = mybir.ActivationFunctionType
AX = mybir.AxisListType

P = 128
N, D, E, L = 1250, 512, 20000, 4
NT = -(-N // P)
NP = NT * P
LAST = N - (NT - 1) * P
KC = D // P
EP = 125
EC = E // EP
BN_EPS = LN_EPS = 1e-5

HB = NT // 2
HALF_MAX = (E - 1) // P + 1 + HB - 1
RING = 8
MAIN = [-(-E * HB * P // N // P) + HB]
MAIN.append(-(-(MAIN[0] - (-E * (N - HB * P) // N // P) + HB) // RING) * RING - MAIN[0])
MT = sum(MAIN)
PARTS = [0, P, 3 * P, 6 * P, N]
QN = NP // 4
FILL_HALF = HB + 2 * KC
FILL_ACT = 2 * FILL_HALF
FILLS = FILL_ACT + NT
PRE = 2 * RING
BODY = 2 * KC * RING
assert PRE + BODY <= MAIN[1]
OVER = [HALF_MAX - m for m in MAIN]
OV0 = [MT + RING, MT + RING + OVER[0]]
COLS = MT + RING + sum(OVER)
B_AT = 1024
FULL = -(-E // P)
RROWS = FULL + 1
PADP = 32
PADS = RROWS * P - E
assert PADS % PADP == 0
NX, KX, HX = 64, 2, 256
CAP = 1024
SCALE = 2.5
XOVER = (N * KX - 1) // P
XT = NX + XOVER
XC = HX // P
WR = 4
WARM = 22
LEAD = 3
EARLY = 4
REC = 4


class Chain:

    def __init__(self, engine, sem):
        self.engine, self.sem, self.base, self.n = engine, sem, 0, 0

    def __call__(self, instruction):
        self.mark(instruction)
        self.wait()

    def mark(self, instruction):
        instruction.then_inc(self.sem, 1)
        self.n += 1

    def count(self):
        return self.base + self.n

    def wait(self):
        self.engine.wait_ge(self.sem, self.count())

    def enter(self, i, per):
        self.before, self.per = self.base + self.n, per
        self.base, self.n = self.before + i * per, 0

    def leave(self, rounds):
        assert self.n == self.per, (self.n, self.per)
        self.base, self.n = self.before + rounds * self.per, 0


def at_least(engine, sem, value):
    if not isinstance(value, int) or value > 0:
        engine.wait_ge(sem, value)


def nodes_of(quarter):
    return min(QN, N - quarter * QN)


def build(nc, x, src, dst, ew, eps, We, be, W1, b1, gamma, beta, W2, b2,
          gate_w, xw1, xw3, xw2, sw1, sw3, sw2, out, scratch):
    xb_dram, rec_dram, xn_dram, tok_dram, y_dram = scratch
    with ExitStack() as ctx:
        def sb(name, shape, dt=F32):
            return ctx.enter_context(nc.sbuf_tensor(name, shape, dt))

        def sem(name):
            return ctx.enter_context(nc.semaphore(name))

        def inside(buffer, layout):
            at, views = 0, []
            for parts, dims, dt in layout:
                n = 1
                for d in dims:
                    n *= d
                v = buffer[0:parts, at:at + n]
                at += n
                if dt is not F32:
                    v = v.bitcast(dt)
                if len(dims) > 1:
                    names = "abcd"[:len(dims)]
                    v = v.rearrange(f"p ({' '.join(names)}) -> p {' '.join(names)}", **dict(zip(names, dims)))
                views.append(v)
            return views

        turned = sb("turned", [P, KC * NP])
        hidden_ = sb("hidden_", [P, KC * NP])
        flight = sb("flight", [P, RING * D])
        rows = sb("rows", [P, 3 * D])
        mixed = sb("mixed", [P, KC * D])
        [hinT] = inside(turned, [(P, (KC, NP), F32)])
        [h1T] = inside(hidden_, [(P, (KC, NP), F32)])
        [ring] = inside(flight, [(P, (RING, D), F32)])
        web, beb, b2b = inside(rows, [(P, (D,), F32)] * 3)
        [oneh] = inside(mixed, [(P, (RING, P), F32)])
        [xres] = inside(turned, [(P, (NT, D), F32)])
        [w3s] = inside(mixed, [(P, (KC, D), F32)])
        [cmpx] = inside(rows, [(P, (XOVER, NX), F32)])
        srcE, ewE, slotF, slotT, slotI, recE, memb, cumu = inside(
            turned, [(EP, (EC,), t) for t in (I32, F32, F32, F32, U32)]
            + [(EP, (EC, REC), F32), (EP, (NT + 1, EC), F32), (EP, (NT, EC), F32)])
        vrow, brow, tmpc, padrec = inside(
            hidden_, [(P, (COLS,), F32)] * 3 + [(PADP, (PADS // PADP, REC), F32)])
        dstE, buckI, buckE = inside(rows, [(EP, (EC + 1,), t) for t in (I32, I32, F32)])
        lg, both, run, pos, slotm, oh0 = inside(
            flight, [(P, (NT, NX), F32), (P, (NT, NX), F32), (P, (NT + 1, NX), F32)] + [(P, (NT, NX), F32)] * 3)
        oh = [oh0, sb("oh1", [P, NT, NX])]
        xeT, sg, hh, hT, ysb = inside(
            turned, [(P, (2, KC, P), F32), (P, (2, HX), F32), (P, (2, HX), F32), (P, (2, XC, P), F32), (P, (WR, D), F32)])
        ident = sb("ident", [P, P])
        below = sb("below", [P, P])
        ones = sb("ones", [P, P])
        zeros_h = sb("zeros_h", [P, D], BF16)
        lane = sb("lane", [P, P])
        vrows = sb("vrows", [3 * L * KC, P])
        vecs = sb("vecs", [P, 3, L, KC])
        zrow = sb("zrow", [P, EC])
        rowtot = sb("rowtot", [EP, NT + 1])
        prior = sb("prior", [EP, NT])
        cnt = sb("cnt", [P, NT + 1])
        upto = sb("upto", [P, NT])
        start = sb("start", [P, NT])
        rowI = sb("rowI", [P, 2, NT], I32)
        row01 = sb("row01", [P, 2, NT])
        unsI = sb("unsI", [1, 1], I32)
        tiles = sb("tiles", [P, NT])
        TS = sb("TS", [P, NT])
        Dd = sb("Dd", [P, NT + 1])
        DD = sb("DD", [P, NT])
        bankI = sb("bankI", [P, COLS], I32)
        NCH = -(-COLS // P)
        rowsel = sb("rowsel", [P, NCH], U32)
        colid = sb("colid", [P, NCH])
        vcol = sb("vcol", [P, NCH])
        tcol = sb("tcol", [P, NCH])
        ccol = sb("ccol", [P, NCH, NT])
        idxT = sb("idxT", [P, COLS], U32)
        wT = sb("wT", [P, COLS])
        dloc = sb("dloc", [P, COLS])
        rec4 = sb("rec4", [EP, 4, REC])
        idx4 = sb("idx4", [EP, 4], U32)
        xs = sb("xs", [P, NT, D])
        hin = sb("hin", [P, NT, D])
        w1s = sb("w1s", [P, KC, D])
        w2s = sb("w2s", [P, KC, D])
        vec = sb("vec", [P, 3, KC])
        epsb = sb("epsb", [P, L])
        cur = sb("cur", [P, RING], U32)
        st = sb("st", [P, NT, 6])
        mv = sb("mv", [P, NT, 2])
        t0 = sb("t0", [P, NT])
        t1 = sb("t1", [P, NT])
        t2 = sb("t2", [P, NT])
        bst = sb("bst", [P, KC, 4, 6])
        bmv = sb("bmv", [P, KC, 2])
        bve = sb("bve", [P, KC])
        bsq = sb("bsq", [P, KC])
        brs = sb("brs", [P, KC])
        bt = sb("bt", [P, KC])
        bscale = sb("bscale", [P, KC])
        bshift = sb("bshift", [P, KC])
        ovx = sb("ovx", [P, D])
        ovh = sb("ovh", [P, P])
        ovi = sb("ovi", [P, 1], U32)
        flagI = sb("flagI", [1, 2], I32)

        gw = sb("gw", [NX, D])
        gT = sb("gT", [P, KC, NX])
        valid = sb("valid", [P, 1])
        m8 = sb("m8", [P, NT, 8])
        i8 = sb("i8", [P, NT, 8], U32)
        i8f = sb("i8f", [P, NT, 8])
        cntx = sb("cntx", [P, NX])
        ovn = sb("ovn", [P, NX])
        ovnI = sb("ovnI", [P, NX], I32)
        ovs = sb("ovs", [P, NX])
        b128 = sb("b128", [P, NX])
        bdif = sb("bdif", [P, NX])
        sel = sb("sel", [P, KX, NT])
        selp = sb("selp", [P, KX, NT])
        selI = sb("selI", [P, KX, NT], I32)
        hiI = sb("hiI", [P, KX, NT], I32)
        slotx = sb("slotx", [P, KX, NT], U32)
        tabx = sb("tabx", [P, KX, NT], U32)
        tokid = sb("tokid", [P, NT], I32)
        tokT = sb("tokT", [P, XT], I32)
        ztab = sb("ztab", [P, XT], I32)
        sgm = sb("sgm", [P, NT, KX])
        gden = sb("gden", [P, NT])
        gate = sb("gate", [P, KX, NT])
        eovF = sb("eovF", [P, XOVER])
        eovI = sb("eovI", [P, XOVER], I32)
        nov = sb("nov", [P, 1], I32)
        shsig = sb("shsig", [P, 2, QN])
        w13 = sb("w13", [P, WR, KC, 2, HX])
        w2e = sb("w2e", [P, WR, XC, D])
        icur = sb("icur", [P, WR], I32)
        xe = ring[:, 0:WR, :]

        ps = ctx.enter_context(nc.psum_tensor("ps", [P, 8, D], F32))

        s_idle = sem("idle")
        s_const = sem("constants")
        s_colid = sem("column_numbers")
        s_zro = sem("zero_bf16")
        s_ldx = sem("x_loaded")
        s_ldd = sem("destinations_loaded")
        s_lde = sem("edges_loaded")
        s_padm = sem("pad_records_made")
        s_rec = sem("records_made")
        s_recw = sem("records_stored")
        s_slot = sem("slots_known")
        s_rot = sem("row_totals_known")
        s_cntp = sem("counts_summed")
        s_uns = sem("order_known")
        s_rsel = sem("row_numbers_ready")
        s_pc = sem("pool_constants")
        s_c4 = sem("pool_copies")
        s_gen = sem("dve_slots_chain")
        s_scat = sem("records_scattered")
        s_rowg = sem("record_rows_gathered")
        s_plane = sem("record_planes_turned")
        s_idx = sem("sources_ready")
        s_brow = sem("overflow_buckets")
        s_tab = sem("tile_tables_ready")
        s_dve = sem("dve_chain")
        s_res = sem("residual_added")
        s_ln = sem("layernorm_sums")
        s_lnq = sem("layernorm_roots")
        s_lwe = sem("We_loaded")
        s_lw1 = sem("W1_loaded")
        s_lw2 = sem("W2_b2_loaded")
        s_lbe = sem("be_loaded")
        s_ldv = sem("vectors_loaded")
        s_vt = sem("vectors_turned")
        s_vec = sem("layer_vectors_ready")
        s_sg = sem("staged")
        s_st = sem("x_be_stored")
        s_first = sem("first_indices")
        s_g = [sem(f"gathered{k}") for k in range(RING)]
        s_y = sem("messages_summed")
        s_m = sem("messages_ready")
        s_free = sem("ring_slots_free")
        s_hin = sem("aggregate_read")
        s_tr = sem("bank_filled")
        s_ra = sem("bank_read_by_act")
        s_rd = sem("bank_read_by_dve")
        s_var = sem("bn_variance")
        s_root = sem("bn_root")
        s_bn = sem("bn_ready")
        s_gt = sem("hidden_ready")
        s_xs = sem("x_relu")
        s_og = [sem(f"over_gathered{h}") for h in range(2)]
        s_oi = [sem(f"over_index{h}") for h in range(2)]
        s_oy = [sem(f"over_summed{h}") for h in range(2)]
        s_om = [sem(f"over_message{h}") for h in range(2)]
        s_ou = [sem(f"over_used{h}") for h in range(2)]
        s_gw = sem("gate_loaded")
        s_gt4 = sem("gate_turned")
        s_ztab = sem("token_table_zero")
        s_ztw = sem("token_table_cleared")
        s_swl = sem("shared_weights_loaded")
        s_xn0 = sem("x_normed")
        s_xn = sem("tokens_normed")
        s_xnw = sem("tokens_stored")
        s_tr2 = sem("tokens_turned")
        s_ra2 = sem("turned_tokens_read")
        s_lg = sem("logits")
        s_gat = sem("top_scores")
        s_sgm = sem("top_sigmoids")
        s_run = sem("expert_members")
        s_pos = sem("expert_ranks")
        s_tabx = sem("token_slots")
        s_scx = sem("tokens_scattered")
        s_tok = sem("token_table_loaded")
        s_xrt = sem("expert_tables_ready")
        s_sp = sem("shared_products")
        s_ssg = sem("shared_sigmoids")
        s_shh = sem("shared_hidden")
        s_so = sem("shared_out")
        s_sod = sem("shared_added")
        s_ic = sem("expert_indices")
        s_w = [sem(f"expert_weights{k}") for k in range(WR)]
        s_xg = [sem(f"tokens_gathered{k}") for k in range(WR)]
        s_tx = sem("x_turned")
        s_xt = sem("xT_ready")
        s_g1 = sem("up_products")
        s_sig = sem("sigmoids")
        s_hh = sem("hidden")
        s_hm = sem("hidden_half")
        s_th = sem("hidden_turned")
        s_ht = sem("hiddenT_ready")
        s_g2 = sem("down_products")
        s_yc = sem("y_copied")
        s_ys = [sem(f"y_stored{k}") for k in range(WR)]
        s_yz = sem("over_rows_cleared")
        s_vw = sem("over_weights")
        s_vg = sem("over_tokens")
        s_vi = sem("over_token_index")
        s_vp = sem("over_pe")
        s_va = sem("over_act")
        s_vd = sem("over_dve")
        s_vs = sem("over_y_stored")
        s_yg = [sem(f"y_gathered{k}") for k in range(RING)]
        s_fa = sem("combined")
        s_fa2 = sem("y_added")
        s_out = sem("out_stored")

        def hold(engine, s, value):
            engine.wait_ge(s, value)
            engine.sem_inc(s_idle, 1)

        block = ctx.enter_context(nc.Block())

        @block.sync
        def _(sp):
            xr = x[0:(NT - 1) * P, :].rearrange("(t p) d -> p t d", p=P)
            sp.dma_start(dstE[:, 0:EC], dst.rearrange("(p c) -> p c", p=EP)).then_inc(s_ldd, 16)
            sp.wait_ge(s_const, 1)
            sp.dma_start(dstE[0:EP - 1, EC:EC + 1], dst.rearrange("(p c) -> p c", p=EP)[1:EP, 0:1],
                         allow_slow_non_contiguous=True).then_inc(s_ldd, 16)
            sp.dma_start(srcE[:, :], src.rearrange("(p c) -> p c", p=EP)).then_inc(s_lde, 16)
            sp.dma_start(ewE[:, :], ew.rearrange("(p c) o -> p (c o)", p=EP)).then_inc(s_lde, 16)
            sp.wait_ge(s_const, 2)
            sp.dma_start(hin[:, 0:NT - 1, :], xr).then_inc(s_ldx, 16)
            sp.dma_start(hin[0:LAST, NT - 1, :], x[(NT - 1) * P:N, :]).then_inc(s_ldx, 16)
            sp.dma_start(epsb[:, :], eps.partition_broadcast(P)).then_inc(s_ldx, 16)
            sp.dma_start(beb[:, :], be[0, :].partition_broadcast(P)).then_inc(s_lbe, 16)
            flat = rec_dram.rearrange("r c -> (r c)")
            sp.wait_ge(s_padm, 1)
            sp.dma_start(flat[E * REC:RROWS * P * REC].rearrange("(p c) -> p c", p=PADP),
                         padrec[:, :, :].rearrange("p a b -> p (a b)")).then_inc(s_recw, 16)
            sp.wait_ge(s_rec, 4)
            sp.dma_start(flat[0:E * REC].rearrange("(p c) -> p c", p=EP),
                         recE[:, :, :].rearrange("p a b -> p (a b)")).then_inc(s_recw, 16)
            for v, a in enumerate((b1, gamma, beta)):
                sp.dma_start(vrows[v * L * KC:(v + 1) * L * KC, :], a.rearrange("l (c p) -> (l c) p", p=P)).then_inc(s_ldv, 16)
            sp.dma_start(gw[:, :], gate_w).then_inc(s_gw, 16)
            sp.wait_ge(s_ztab, 1)
            sp.dma_start(tok_dram.rearrange("(p j) o -> p (j o)", p=P), ztab[:, :]).then_inc(s_ztw, 16)

            def load_expert(e, k, done):
                sp.dma_start(w13[:, k, :, 0, :], xw1[bass.ds(e, 1), :, :].rearrange("o (p k) n -> (o p) k n", k=KC)).then_inc(done, 16)
                sp.dma_start(w13[:, k, :, 1, :], xw3[bass.ds(e, 1), :, :].rearrange("o (p k) n -> (o p) k n", k=KC)).then_inc(done, 16)
                sp.dma_start(w2e[:, k, :, :], xw2[bass.ds(e, 1), :, :].rearrange("o (p k) n -> (o p) k n", k=XC)).then_inc(done, 16)

            sp.wait_ge(s_rot, 1)
            with sp.Fori(0, L) as l:
                hold(sp, s_hin, 1 + l * NT)
                sp.dma_start(web[:, :], We[bass.ds(l, 1), 0, :].rearrange("o d -> (o d)").partition_broadcast(P)).then_inc(s_lwe, 16)
                hold(sp, s_var, 1 + l)
                sp.dma_start(w1s[:, :, :], W1[bass.ds(l, 1), :, :].rearrange("o (p k) n -> (o p) k n", k=KC)).then_inc(s_lw1, 16)
                for t in range(NT):
                    hold(sp, s_sg, l * NT + t + 1)
                    sp.dma_start(xb_dram[t * P:(t + 1) * P, :], hin[:, t, :]).then_inc(s_st, 16)
                hold(sp, s_rd, 10 + l * NT)
                sp.dma_start(w2s[:, :, :], W2[bass.ds(l, 1), :, :].rearrange("o (k p) n -> p (o k) n", p=P)).then_inc(s_lw2, 16)
                sp.dma_start(b2b[:, :], b2[bass.ds(l, 1), :].rearrange("o d -> (o d)").partition_broadcast(P)).then_inc(s_lw2, 16)
                with sp.If(l < L - 1):
                    after = nc.s_assert_within(l + 1, 1, L - 1, skip_runtime_bounds_check_because="l < L - 1 here")
                    sp.dma_start(beb[:, :], be[bass.ds(after, 1), :].rearrange("o d -> (o d)").partition_broadcast(P)).then_inc(s_lbe, 16)
            sp.wait_ge(s_var, 1 + L)
            sp.dma_start(xres[:, 0:NT - 1, :], xr).then_inc(s_ldx, 16)
            sp.dma_start(xres[0:LAST, NT - 1, :], x[(NT - 1) * P:N, :]).then_inc(s_ldx, 16)
            sp.wait_ge(s_rd, 10 + L * NT)
            sp.dma_start(w1s[:, :, :], sw1.rearrange("(p k) n -> p k n", k=KC)).then_inc(s_swl, 16)
            sp.dma_start(w3s[:, :, :], sw3.rearrange("(p k) n -> p k n", k=KC)).then_inc(s_swl, 16)
            sp.dma_start(w2s[:, :, :], sw2.rearrange("(k p) n -> p k n", p=P)).then_inc(s_swl, 16)
            for t in range(NT):
                sp.wait_ge(s_xn, t + 1)
                sp.dma_start(xn_dram[t * P:(t + 1) * P, :], hin[:, t, :]).then_inc(s_xnw, 16)
            for e in range(WR):
                load_expert(e, e, s_w[e])
            sp.wait_ge(s_zro, 1)
            sp.dma_start(y_dram[NX * P:XT * P, :].rearrange("(p t) (a c) -> p (t a) c", p=P, a=2),
                         zeros_h[:, :].bitcast(F32).unsqueeze(1).broadcast_to([P, XOVER * 2, D // 2])).then_inc(s_yz, 16)
            sp.wait_ge(s_scx, 16 * KX * NT)
            sp.dma_start(tokT[:, :], tok_dram.rearrange("(p j) o -> p (j o)", p=P)).then_inc(s_tok, 16)

            def store_y(j, k):
                at_least(sp, s_yc, j + 1)
                sp.dma_start(y_dram[bass.ds(j * P, P), :], ysb[:, k, :]).then_inc(s_ys[k], 16)

            def expert_traffic(j, k):
                sp.wait_ge(s_g2, j - WR + 1)
                load_expert(j, k, s_w[k])
                if not isinstance(j, int) or j > WR:
                    store_y(j - WR - 1, (k - 1) % WR)

            for k in range(WR):
                expert_traffic(WR + k, k)
            with sp.Fori(2, NX // WR) as g:
                for k in range(WR):
                    expert_traffic(g * WR + k, k)
            for j in range(NX - WR - 1, NX):
                store_y(j, j % WR)
            sp.wait_ge(s_xrt, 1)
            sp.wait_ge(s_yz, 16)
            over = sp.value_load(nov[0:1, 0:1], min_val=0, max_val=XOVER)
            with sp.If(over > 0):
                def traffic(o):
                    at_least(sp, s_va, o * 3)
                    e = sp.value_load(eovI[0:1, bass.ds(o, 1)], min_val=0, max_val=NX - 1)
                    load_expert(e, 0, s_vw)
                    sp.wait_ge(s_va, o * 3 + 3)
                    sp.dma_start(y_dram[bass.ds((o + NX) * P, P), :], ysb[:, 0, :]).then_inc(s_vs, 16)

                traffic(0)
                with sp.Fori(1, XOVER) as o:
                    traffic(o)
            for t in range(NT):
                sp.wait_ge(s_fa, t + 1)
                n = min(P, N - t * P)
                sp.dma_start(out[t * P:t * P + n, :], xs[0:n, t, :]).then_inc(s_out, 16)
            sp.wait_ge(s_out, 16 * NT)

        @block.gpsimd
        def _(pool):
            nc.gpsimd.memset(dstE[:, EC:EC + 1], 1 << 20).then_inc(s_const, 1)
            nc.gpsimd.memset(hin[:, NT - 1, :], 0.0).then_inc(s_const, 1)
            nc.gpsimd.memset(h1T[:, :, N:NP], 0.0).then_inc(s_const, 1)
            nc.gpsimd.memset(padrec[:, :, :], 0.0).then_inc(s_pc, 1)
            nc.gpsimd.memset(recE[:, :, 3], 0.0).then_inc(s_rec, 1)
            nc.gpsimd.memset(ones[:, :], 1.0).then_inc(s_pc, 1)
            nc.gpsimd.memset(ident[:, :], 0.0).then_inc(s_pc, 1)
            pool.wait_ge(s_pc, 3)
            nc.gpsimd.memset(padrec[:, :, 1], 65536.0).then_inc(s_padm, 1)
            nc.gpsimd.iota(colid[:, :], [[P, NCH]], base=0, channel_multiplier=1,
                           allow_small_or_imprecise_dtypes=True).then_inc(s_colid, 1)
            nc.gpsimd.affine_select(out=below[:, :], in_=ones[:, :], compare_op=ALU.is_gt, fill=0.0, base=0,
                                    pattern=[[1, P]], channel_multiplier=-1).then_inc(s_const, 1)
            nc.gpsimd.affine_select(out=ident[:, :], in_=ident[:, :], compare_op=ALU.not_equal, fill=1.0, base=0,
                                    pattern=[[-1, P]], channel_multiplier=1).then_inc(s_const, 1)
            nc.gpsimd.iota(lane[:, :], [[1, P]], base=0, channel_multiplier=0,
                           allow_small_or_imprecise_dtypes=True).then_inc(s_const, 1)
            for a, n, v in ((0, MAIN[0], 0), (MAIN[0], MAIN[1], B_AT), (MT, RING, 0),
                            (OV0[0], OVER[0], MAIN[0]), (OV0[1], OVER[1], B_AT + MAIN[1])):
                nc.gpsimd.iota(vrow[:, a:a + n], [[1, n]], base=v, channel_multiplier=0,
                               allow_small_or_imprecise_dtypes=True).then_inc(s_const, 1)
            nc.gpsimd.affine_select(out=valid[:, :], in_=ones[:, 0:1], compare_op=ALU.is_gt, fill=0.0, base=LAST,
                                    pattern=[[0, 1]], channel_multiplier=-1).then_inc(s_const, 1)
            nc.gpsimd.iota(tokid[:, :], [[P, NT]], base=0, channel_multiplier=1).then_inc(s_const, 1)
            pool.wait_ge(s_uns, 1)
            pool.wait_ge(s_recw, 32)
            recs = rec_dram.rearrange("r (e c) -> (r e) c", c=REC)
            unsorted = pool.value_load(unsI[0:1, 0:1], min_val=0, max_val=E)

            def scatter(i):
                nc.gpsimd.tensor_copy(rec4[:, :, :], recE[:, bass.ds(i * 4, 4), :]).then_inc(s_c4, 1)
                nc.gpsimd.tensor_copy(idx4[:, :], slotI[:, bass.ds(i * 4, 4)]).then_inc(s_c4, 1)
                hold(pool, s_c4, i * 2 + 2)
                for k in range(4):
                    pool.indirect_dma_start(recs, bass.IndirectOffsetOnAxis(ap=idx4[:, k:k + 1], axis=0),
                                            rec4[:, k, :], None).then_inc(s_scat, 16)

            with pool.If(unsorted > 0):
                pool.wait_ge(s_slot, 1)
                scatter(0)
                with pool.Fori(1, EC // 4) as i:
                    hold(pool, s_scat, 64 * i)
                    scatter(i)
                pool.wait_ge(s_scat, 64 * (EC // 4))
            pool.wait_ge(s_rsel, 1)
            for c in range(NCH):
                n = min(P, COLS - c * P)
                pool.indirect_dma_start(ring[0:n, c, :], None, rec_dram,
                                        bass.IndirectOffsetOnAxis(ap=rowsel[0:n, c:c + 1], axis=0)).then_inc(s_rowg, 16)
            pool.wait_ge(s_const, 13)
            v, w, x1 = vrow[:, OV0[0]:COLS], brow[:, OV0[0]:COLS], tmpc[:, OV0[0]:COLS]
            nc.gpsimd.tensor_scalar(w, v, 0.0, -1.0, ALU.mult, ALU.add).then_inc(s_brow, 1)
            for b in range(NT):
                pool.wait_ge(s_brow, b * 2 + 1)
                nc.gpsimd.tensor_scalar(x1, v, TS[:, b:b + 1], None, ALU.is_ge).then_inc(s_brow, 1)
                pool.wait_ge(s_brow, b * 2 + 2)
                nc.gpsimd.tensor_tensor(w, w, x1, ALU.add).then_inc(s_brow, 1)
            pool.wait_ge(s_brow, NT * 2 + 1)
            nc.gpsimd.tensor_scalar(x1, v, float(B_AT), float(-HB), ALU.is_ge, ALU.mult).then_inc(s_brow, 1)
            pool.wait_ge(s_brow, NT * 2 + 2)
            nc.gpsimd.tensor_tensor(x1, x1, w, ALU.add).then_inc(s_brow, 1)
            pool.wait_ge(s_brow, NT * 2 + 3)
            nc.gpsimd.tensor_copy(bankI[:, OV0[0]:COLS], x1).then_inc(s_brow, 1)
            needed = [pool.value_load(flagI[0:1, h:h + 1], min_val=0, max_val=HALF_MAX) for h in range(2)]
            with pool.Fori(0, L) as l:
                hold(pool, s_st, (l + 1) * NT * 16)

                def gather(t, k):
                    hold(pool, s_free, l * MT + t + 1)
                    pool.indirect_dma_start(ring[:, k, :], None, xb_dram,
                                            bass.IndirectOffsetOnAxis(ap=cur[:, k:k + 1], axis=0)).then_inc(s_g[k], 16)

                for h, first in enumerate((0, MAIN[0])):
                    groups, rest = divmod(MAIN[h], RING)
                    with pool.Fori(0, groups) as g:
                        for k in range(RING):
                            gather(first + g * RING + k, (first + k) % RING)
                    for k in range(rest):
                        gather(first + groups * RING + k, (first + k) % RING)
                    with pool.If(needed[h] > MAIN[h]):
                        with pool.Fori(0, OVER[h]) as o:
                            hold(pool, s_ou[h], l * OVER[h] + o + 1)
                            nc.gpsimd.tensor_copy(ovi[:, :], idxT[:, bass.ds(o + OV0[h], 1)]).then_inc(s_oi[h], 1)
                            hold(pool, s_oi[h], l * OVER[h] + o + 1)
                            pool.indirect_dma_start(ovx[:, :], None, xb_dram,
                                                    bass.IndirectOffsetOnAxis(ap=ovi[:, :], axis=0)).then_inc(s_og[h], 16)
            pool.wait_ge(s_const, 13)
            pool.wait_ge(s_ztw, 16)
            pool.wait_ge(s_tabx, 1)
            for k in range(KX):
                for t in range(NT):
                    n = min(P, N - t * P)
                    pool.indirect_dma_start(tok_dram, bass.IndirectOffsetOnAxis(ap=tabx[0:n, k, t:t + 1], axis=0),
                                            tokid[0:n, t:t + 1], None).then_inc(s_scx, 16)
            pool.wait_ge(s_tok, 16)
            pool.wait_ge(s_xnw, 16 * NT)

            def tokens(g, k):
                if not isinstance(g, int):
                    hold(pool, s_tx, (g - 1) * WR + k + 1)
                nc.gpsimd.tensor_copy(icur[:, k:k + 1], tokT[:, bass.ds(g * WR + k, 1)]).then_inc(s_ic, 1)
                hold(pool, s_ic, g * WR + k + 1)
                pool.indirect_dma_start(xe[:, k, :], None, xn_dram,
                                        bass.IndirectOffsetOnAxis(ap=icur[:, k:k + 1], axis=0)).then_inc(s_xg[k], 16)

            for k in range(WR):
                tokens(0, k)
            with pool.Fori(1, NX // WR) as g:
                for k in range(WR):
                    tokens(g, k)
            pool.wait_ge(s_xrt, 1)
            over = pool.value_load(nov[0:1, 0:1], min_val=0, max_val=XOVER)
            with pool.If(over > 0):
                pool.wait_ge(s_tx, NX)

                def over_tokens(o):
                    if not isinstance(o, int):
                        hold(pool, s_vp, o * 4)
                    nc.gpsimd.tensor_copy(icur[:, 0:1], tokT[:, bass.ds(o + NX, 1)]).then_inc(s_vi, 1)
                    hold(pool, s_vi, o + 1)
                    pool.indirect_dma_start(xe[:, 0, :], None, xn_dram,
                                            bass.IndirectOffsetOnAxis(ap=icur[:, 0:1], axis=0)).then_inc(s_vg, 16)

                over_tokens(0)
                with pool.Fori(1, XOVER) as o:
                    over_tokens(o)
                pool.wait_ge(s_vs, 16 * XOVER)
            pool.wait_ge(s_tx, NX)
            for k in range(WR):
                pool.wait_ge(s_ys[k], 16 * (NX // WR))
            for u in range(KX * NT):
                at_least(pool, s_fa2, u - RING + 1)
                n = min(P, N - u // KX * P)
                pool.indirect_dma_start(ring[0:n, u % RING, :], None, y_dram,
                                        bass.IndirectOffsetOnAxis(ap=slotx[0:n, u % KX, u // KX:u // KX + 1], axis=0)
                                        ).then_inc(s_yg[u % RING], 16)

        @block.scalar
        def _(act):
            act.wait_ge(s_ldd, 32)
            nc.scalar.copy(recE[:, :, 1], dstE[:, 0:EC]).then_inc(s_rec, 1)
            act.wait_ge(s_lde, 32)
            nc.scalar.copy(recE[:, :, 0], srcE[:, :]).then_inc(s_rec, 1)
            nc.scalar.copy(recE[:, :, 2], ewE[:, :]).then_inc(s_rec, 1)
            act.wait_ge(s_rsel, 1)
            needed = [act.value_load(flagI[0:1, h:h + 1], min_val=0, max_val=HALF_MAX) for h in range(2)]
            act.wait_ge(s_ln, 1)
            nc.scalar.activation(t1[:, :], t0[:, :], ACT.Sqrt).then_inc(s_lnq, 1)
            act.wait_ge(s_ln, 2)
            for t in range(NT):
                nc.scalar.activation(xs[:, t, :], hin[:, t, :], ACT.Identity, bias=t2[:, t:t + 1],
                                     scale=t1[:, t:t + 1]).then_inc(s_xn0, 1)
            act.wait_ge(s_idx, 1)
            nc.scalar.copy(cur[:, :], idxT[:, 0:RING]).then_inc(s_first, 1)
            act.wait_ge(s_first, 1)
            act.sem_inc(s_free, RING)
            act.sem_inc(s_xs, NT)
            with act.Fori(0, L) as l:
                def message(t, k):
                    act.wait_ge(s_y, (l * MT + t + 1) * 2)
                    nc.scalar.activation(ring[:, k, :], ring[:, k, :], ACT.Relu).then_inc(s_m, 1)
                    nc.scalar.copy(cur[:, k:k + 1], idxT[:, bass.ds(t + RING, 1)]).then_inc(s_m, 1)

                def turned_in(t, bank):
                    act.wait_ge(s_tr, l * FILLS + (t if t < HB else t - HB + FILL_HALF) + 1)
                    nc.scalar.copy(hinT[:, :, t * P:(t + 1) * P],
                                   ps[:, bank, :].rearrange("p (k n) -> p k n", k=KC)).then_inc(s_ra, 1)

                def product(h, q, c, bank):
                    n = nodes_of(h * 2 + q) if h else QN
                    act.wait_ge(s_tr, l * FILLS + h * FILL_HALF + HB + q * KC + c + 1)
                    nc.scalar.activation(h1T[:, c, bass.ds(q * QN + h * HB * P, n)], ps[:, bank, 0:n], ACT.Identity,
                                         bias=vec[:, 0, c:c + 1]).then_inc(s_ra, 1)

                with act.Fori(0, MAIN[0] // RING) as g:
                    for k in range(RING):
                        message(g * RING + k, k)
                for t in range(MAIN[0] // RING * RING, MAIN[0]):
                    message(t, t % RING)

                def overflow(h):
                    with act.If(needed[h] > MAIN[h]):
                        with act.Fori(0, OVER[h]) as o:
                            act.wait_ge(s_oy[h], (l * OVER[h] + o + 1) * 2)
                            nc.scalar.activation(ovx[:, :], ovx[:, :], ACT.Relu).then_inc(s_om[h], 1)

                overflow(0)
                hold(act, s_vec, l + 1)
                for t in range(PRE):
                    message(MAIN[0] + t, (MAIN[0] + t) % RING)
                    if t % RING == RING - 1:
                        for b in range(3) if t < RING else range(3, HB):
                            turned_in(b, 5 + b % 3)
                with act.Fori(0, 2) as q:
                    for c in range(KC):
                        for k in range(RING):
                            message(MAIN[0] + PRE + (q * KC + c) * RING + k, (MAIN[0] + k) % RING)
                        product(0, q, c, 6 + c % 2)
                for t in range(MAIN[0] + PRE + BODY, MT):
                    message(t, t % RING)
                overflow(1)
                for b in range(HB):
                    turned_in(HB + b, 5 + (FILL_HALF + b) % 3)
                for q in range(2):
                    for c in range(KC):
                        product(1, q, c, 5 + (FILL_HALF + HB + q * KC + c) % 3)
                act.wait_ge(s_var, 1 + l + 1)
                nc.scalar.activation(bsq[:, :], bve[:, :], ACT.Sqrt).then_inc(s_root, 1)
                act.wait_ge(s_bn, l + 1)
                for q in range(4):
                    for c in range(KC):
                        v = h1T[:, c, PARTS[q]:PARTS[q + 1]]
                        nc.scalar.activation(v, v, ACT.Relu, bias=bshift[:, c:c + 1],
                                             scale=bscale[:, c:c + 1]).then_inc(s_gt, 1)
                with act.If(l < L - 1):
                    for t in range(NT):
                        act.wait_ge(s_sg, (l + 1) * NT + t + 1)
                        nc.scalar.activation(xs[:, t, :], xs[:, t, :], ACT.Relu).then_inc(s_xs, 1)
            act.wait_ge(s_ln, 3)
            nc.scalar.activation(t1[:, :], t0[:, :], ACT.Sqrt).then_inc(s_lnq, 1)
            for t in range(NT):
                act.wait_ge(s_tr2, t + 1)
                nc.scalar.copy(hinT[:, :, t * P:(t + 1) * P],
                               ps[:, 5 + t % 3, :].rearrange("p (k n) -> p k n", k=KC)).then_inc(s_ra2, 1)
            act.wait_ge(s_gat, 1)
            nc.scalar.activation(sgm[:, :, :], m8[:, :, 0:KX], ACT.Sigmoid).then_inc(s_sgm, 1)
            for u in range(16):
                act.wait_ge(s_sp, u + 1)
                at_least(act, s_shh, u - 1)
                n = nodes_of(u // KC)
                nc.scalar.activation(shsig[:, u % 2, 0:n], ps[:, 4 + u % 2 * 2, 0:n], ACT.Sigmoid).then_inc(s_ssg, 1)

            def turned(j, k):
                act.wait_ge(s_tx, j + 1)
                at_least(act, s_g1, j - 1)
                nc.scalar.copy(xeT[:, k % 2, :, :].rearrange("p k n -> p (k n)"), ps[:, k % 2, :]).then_inc(s_xt, 1)

            def sigmoid(j, k):
                act.wait_ge(s_g1, j + 1)
                at_least(act, s_hh, j - 1)
                nc.scalar.activation(sg[:, k % 2, :], ps[:, 2 + k % 2, 0:HX], ACT.Sigmoid).then_inc(s_sig, 1)

            def result(j, k, turn):
                act.wait_ge(s_g2, j + 1)
                at_least(act, s_ys[k], turn * 16)
                nc.scalar.copy(ysb[:, k, :], ps[:, 6 + k % 2, :]).then_inc(s_yc, 1)

            def step(g, k):
                j = g * WR + k
                static = isinstance(j, int)
                if not static or j < NX:
                    sigmoid(j, k)
                if not static or j + 1 < NX:
                    turned(j + 1, (k + 1) % WR)
                if not static or j >= 1:
                    result(j - 1, (k - 1) % WR, g + (k - 1) // WR)

            turned(0, 0)
            for k in range(WR):
                step(0, k)
            with act.Fori(1, NX // WR - 1) as g:
                for k in range(WR):
                    step(g, k)
            for k in range(WR + 1):
                step(NX // WR - 1 + k // WR, k % WR)
            act.wait_ge(s_xrt, 1)
            over = act.value_load(nov[0:1, 0:1], min_val=0, max_val=XOVER)
            with act.If(over > 0):
                act.wait_ge(s_ys[0], 16 * (NX // WR))

                def over_act(o):
                    act.wait_ge(s_vp, o * 4 + 1)
                    nc.scalar.copy(xeT[:, 0, :, :].rearrange("p k n -> p (k n)"), ps[:, 0, :]).then_inc(s_va, 1)
                    act.wait_ge(s_vp, o * 4 + 2)
                    nc.scalar.activation(sg[:, 0, :], ps[:, 2, 0:HX], ACT.Sigmoid).then_inc(s_va, 1)
                    act.wait_ge(s_vp, o * 4 + 4)
                    at_least(act, s_vs, o * 16)
                    nc.scalar.copy(ysb[:, 0, :], ps[:, 6, :]).then_inc(s_va, 1)

                over_act(0)
                with act.Fori(1, XOVER) as o:
                    over_act(o)

        @block.vector
        def _(dve):
            chain = Chain(dve, s_dve)
            V = nc.vector

            def rsqrt_step():
                chain(V.reciprocal(t1[:, :], t1[:, :]))
                chain(V.tensor_tensor(t2[:, :], t1[:, :], t0[:, :], ALU.mult))
                chain(V.scalar_tensor_tensor(t2[:, :], t2[:, :], -0.5, t1[:, :], ALU.mult, ALU.mult))
                chain(V.scalar_tensor_tensor(t1[:, :], t2[:, :], 1.5, t1[:, :], ALU.add, ALU.mult))

            dve.sem_inc(s_rd, 10)
            dve.sem_inc(s_hin, 1)
            dve.sem_inc(s_var, 1)
            V.memset(zeros_h[:, :], 0.0).then_inc(s_zro, 1)
            V.memset(ztab[:, :], 0).then_inc(s_ztab, 1)
            chain(V.memset(zrow[:, :], 0.0))
            dve.wait_ge(s_colid, 1)
            chain(V.tensor_copy(vcol[:, :], colid[:, :]))
            shift = 0
            for a, v in ((MAIN[0], B_AT), (MT, 0), (OV0[0], MAIN[0]), (OV0[1], B_AT + MAIN[1])):
                chain(V.tensor_scalar(tcol[:, :], colid[:, :], float(a), float(v - a - shift), ALU.is_ge, ALU.mult))
                chain(V.tensor_tensor(vcol[:, :], vcol[:, :], tcol[:, :], ALU.add))
                shift = v - a
            dve.wait_ge(s_ldd, 32)
            chain(V.tensor_scalar(buckI[:, :], dstE[:, :], 7, None, ALU.arith_shift_right))
            chain(V.tensor_copy(buckE[:, :], buckI[:, :]))
            for b in range(NT):
                chain.mark(V.tensor_scalar(memb[:, b, :], buckE[:, 0:EC], float(b), None, ALU.is_equal))
            chain(V.tensor_tensor(memb[:, NT, :], buckE[:, 0:EC], buckE[:, 1:EC + 1], ALU.is_gt))
            V.tensor_reduce(rowtot[:, :], memb[:, :, :], AX.X, ALU.add).then_inc(s_rot, 1)
            dve.wait_ge(s_cntp, 2)
            chain(V.tensor_copy(cnt[:, :], ps[:, 1, 0:NT + 1]))
            V.tensor_copy(unsI[:, :], cnt[0:1, NT:NT + 1]).then_inc(s_uns, 1)
            chain(V.tensor_tensor_scan(upto[:, :], cnt[:, 0:NT], zrow[:, 0:NT], 0.0, ALU.add, ALU.add))
            chain(V.tensor_tensor(start[:, :], upto[:, :], cnt[:, 0:NT], ALU.subtract))
            chain.mark(V.tensor_copy(rowI[:, 0, :], start[:, :]))
            chain(V.tensor_scalar(rowI[:, 1, :], upto[:, :], -1.0, None, ALU.add))
            chain(V.tensor_scalar(rowI[:, :, :], rowI[:, :, :], 7, None, ALU.arith_shift_right))
            chain(V.tensor_copy(row01[:, :, :], rowI[:, :, :]))
            chain(V.scalar_tensor_tensor(tiles[:, :], row01[:, 1, :], 1.0, row01[:, 0, :], ALU.add, ALU.subtract))
            for h in range(2):
                s = slice(h * HB, (h + 1) * HB)
                chain(V.tensor_tensor_scan(TS[:, s], tiles[:, s], zrow[:, 0:HB], float(h * B_AT), ALU.add, ALU.add))
            chain.mark(V.tensor_scalar(flagI[0:1, 0:1], TS[0:1, HB - 1:HB], 0.0, None, ALU.add))
            chain(V.tensor_scalar(flagI[0:1, 1:2], TS[0:1, NT - 1:NT], float(-B_AT), None, ALU.add))
            chain.mark(V.memset(Dd[:, 0:1], 0.0))
            chain(V.tensor_tensor(TS[:, :], TS[:, :], tiles[:, :], ALU.subtract))
            chain(V.tensor_tensor(Dd[:, 1:NT + 1], row01[:, 0, :], TS[:, :], ALU.subtract))
            chain(V.tensor_tensor(DD[:, :], Dd[:, 1:NT + 1], Dd[:, 0:NT], ALU.subtract))
            cols = [P, NCH, NT]
            chain(V.tensor_tensor(ccol[:, :, :], vcol[:, :].unsqueeze(2).broadcast_to(cols),
                                  TS[:, :].unsqueeze(1).broadcast_to(cols), ALU.is_ge))
            chain(V.tensor_tensor(ccol[:, :, :], ccol[:, :, :], DD[:, :].unsqueeze(1).broadcast_to(cols), ALU.mult))
            chain(V.tensor_reduce(tcol[:, :], ccol[:, :, :], AX.X, ALU.add))
            chain(V.tensor_tensor(tcol[:, :], tcol[:, :], vcol[:, :], ALU.add))
            V.tensor_scalar(rowsel[:, :], tcol[:, :], float(FULL), None, ALU.min).then_inc(s_rsel, 1)
            needed = [dve.value_load(flagI[0:1, h:h + 1], min_val=0, max_val=HALF_MAX) for h in range(2)]
            unsorted = dve.value_load(unsI[0:1, 0:1], min_val=0, max_val=E)
            with dve.If(unsorted > 0):
                slots = Chain(dve, s_gen)
                slots(V.tensor_tensor(prior[:, :], ps[0:EP, 0, 0:NT], start[0:EP, :], ALU.add))
                for b in range(NT):
                    slots(V.tensor_tensor_scan(cumu[:, b, :], memb[:, b, :], zrow[0:EP, :], 0.0, ALU.add, ALU.add))
                    slots(V.tensor_scalar(slotT[:, :], cumu[:, b, :], prior[:, b:b + 1], -1.0, ALU.add, ALU.add))
                    slots(V.tensor_tensor(slotT[:, :], slotT[:, :], memb[:, b, :], ALU.mult))
                    if b == 0:
                        slots(V.tensor_copy(slotF[:, :], slotT[:, :]))
                    else:
                        slots(V.tensor_tensor(slotF[:, :], slotF[:, :], slotT[:, :], ALU.add))
                V.tensor_copy(slotI[:, :], slotF[:, :]).then_inc(s_slot, 1)
            dve.wait_ge(s_ldx, 48)
            for t in range(NT):
                chain.mark(V.bn_stats(st[:, t, :], hin[:, t, :]))
            chain.wait()
            for t in range(NT):
                chain.mark(V.bn_aggr(mv[:, t, :], st[:, t, :]))
            chain.wait()
            V.tensor_scalar(t0[:, :], mv[:, :, 1], LN_EPS, None, ALU.add).then_inc(s_ln, 1)
            dve.wait_ge(s_lnq, 1)
            rsqrt_step()
            V.scalar_tensor_tensor(t2[:, :], mv[:, :, 0], -1.0, t1[:, :], ALU.mult, ALU.mult).then_inc(s_ln, 1)
            dve.wait_ge(s_lbe, 16)
            for t in range(NT):
                dve.wait_ge(s_xn0, t + 1)
                V.tensor_tensor(hin[:, t, :], xs[:, t, :], beb[:, :], ALU.add).then_inc(s_sg, 1)
            dve.wait_ge(s_plane, 1)
            V.tensor_copy(idxT[:, :], ps[:, 0, 0:COLS]).then_inc(s_idx, 1)
            chain(V.tensor_copy(wT[:, :], ps[:, 2, 0:COLS]))
            chain(V.tensor_scalar(epsb[:, :], epsb[:, :], 1.0, None, ALU.add))
            dve.wait_ge(s_const, 12)
            a = OV0[0]
            chain(V.tensor_scalar(brow[:, 0:a], vrow[:, 0:a], 0.0, -1.0, ALU.mult, ALU.add))
            for b in range(NT):
                chain(V.scalar_tensor_tensor(brow[:, 0:a], vrow[:, 0:a], TS[:, b:b + 1], brow[:, 0:a], ALU.is_ge, ALU.add))
            dve.wait_ge(s_brow, NT * 2 + 4)
            V.scalar_tensor_tensor(dloc[:, :], brow[:, :], float(-P), ps[:, 1, 0:COLS], ALU.mult, ALU.add).then_inc(s_tab, 1)
            chain(V.tensor_scalar(tmpc[:, 0:a], vrow[:, 0:a], float(B_AT), float(-HB), ALU.is_ge, ALU.mult))
            V.tensor_tensor(bankI[:, 0:a], tmpc[:, 0:a], brow[:, 0:a], ALU.add).then_inc(s_tab, 1)
            dve.wait_ge(s_tab, 2)
            dve.wait_ge(s_vt, 1)
            chain(V.tensor_copy(vecs[:, :, :, :].rearrange("p v l c -> p (v l c)"), ps[:, 7, 0:3 * L * KC]))
            dve.wait_ge(s_gt4, 1)
            chain(V.tensor_copy(gT[:, :, :].rearrange("p k e -> p (k e)"), ps[:, 6, 0:KC * NX]))
            with dve.Fori(0, L) as l:
                chain.enter(l, CH_LAYER)
                V.tensor_copy(vec[:, :, :], vecs[:, :, bass.ds(l, 1), :].rearrange("p v o c -> p v (o c)")).then_inc(s_vec, 1)
                hold(dve, s_lwe, (l + 1) * 16)

                def edges(t, k, turn):
                    dve.wait_ge(s_g[k], (l * (MT // RING) + turn + 1) * 16)
                    V.tensor_scalar(oneh[:, k, :], lane[:, :], dloc[:, bass.ds(t, 1)], None, ALU.is_equal).then_inc(s_y, 1)
                    V.scalar_tensor_tensor(ring[:, k, :], web[:, :], wT[:, bass.ds(t, 1)], ring[:, k, :],
                                           ALU.mult, ALU.add).then_inc(s_y, 1)

                for h in range(2):
                    first = (0, MAIN[0] + LEAD)[h]
                    groups, rest = divmod(sum(MAIN[:h + 1]) - first, RING)
                    with dve.Fori(0, groups) as g:
                        for k in range(RING):
                            edges(first + g * RING + k, (first + k) % RING, g + (first + k) // RING)
                    for k in range(rest):
                        edges(first + groups * RING + k, (first + k) % RING, groups + (first + k) // RING)
                    with dve.If(needed[h] > MAIN[h]):
                        with dve.Fori(0, OVER[h]) as o:
                            dve.wait_ge(s_og[h], (l * OVER[h] + o + 1) * 16)
                            V.tensor_scalar(ovh[:, :], lane[:, :], dloc[:, bass.ds(o + OV0[h], 1)], None,
                                            ALU.is_equal).then_inc(s_oy[h], 1)
                            V.scalar_tensor_tensor(ovx[:, :], web[:, :], wT[:, bass.ds(o + OV0[h], 1)], ovx[:, :],
                                                   ALU.mult, ALU.add).then_inc(s_oy[h], 1)
                        hold(dve, s_ou[h], (l + 1) * OVER[h] + 1)
                    if h == 0:
                        for t in range(MAIN[0], MAIN[0] + LEAD):
                            edges(t, t % RING, t // RING)
                    dve.wait_ge(s_free, RING + l * MT + sum(MAIN[:h + 1]))
                    for b in range(HB):
                        t = h * HB + b
                        if h == 0:
                            dve.wait_ge(s_xs, l * NT + NT)
                        V.scalar_tensor_tensor(hin[:, t, :], xs[:, t, :], epsb[:, bass.ds(l, 1)], ps[:, b, :],
                                               ALU.mult, ALU.add).then_inc(s_hin, 1)
                for h in range(2):
                    for q in range(2):
                        for c in range(KC):
                            a, n = (h * 2 + q) * QN, nodes_of(h * 2 + q)
                            dve.wait_ge(s_ra, l * FILL_ACT + h * FILL_HALF + HB + q * KC + c + 1)
                            chain.mark(V.bn_stats(bst[:, c, h * 2 + q, :], h1T[:, c, a:a + n]))
                            if (h, q) == (1, 1):
                                hold(dve, s_dve, chain.count())
                                chain.mark(V.bn_aggr(bmv[:, c, :], bst[:, c, :, :].rearrange("p a b -> p (a b)")))
                chain.wait()
                V.tensor_scalar(bve[:, :], bmv[:, :, 1], BN_EPS, None, ALU.add).then_inc(s_var, 1)
                dve.wait_ge(s_root, l + 1)
                chain(V.reciprocal(brs[:, :], bsq[:, :]))
                chain(V.tensor_tensor(bt[:, :], brs[:, :], bve[:, :], ALU.mult))
                chain(V.scalar_tensor_tensor(bt[:, :], bt[:, :], -0.5, brs[:, :], ALU.mult, ALU.mult))
                chain(V.scalar_tensor_tensor(brs[:, :], bt[:, :], 1.5, brs[:, :], ALU.add, ALU.mult))
                dve.wait_ge(s_vec, l + 1)
                chain(V.tensor_tensor(bscale[:, :], brs[:, :], vec[:, 1, :], ALU.mult))
                chain(V.tensor_tensor(bt[:, :], bmv[:, :, 0], bscale[:, :], ALU.mult))
                V.tensor_tensor(bshift[:, :], vec[:, 2, :], bt[:, :], ALU.subtract).then_inc(s_bn, 1)
                hold(dve, s_lw2, (l + 1) * 32)
                def second(t):
                    dve.wait_ge(s_tr, l * FILLS + FILL_ACT + t + 1)
                    return V.tensor_tensor(xs[:, t, :], ps[:, 5 + (FILL_ACT + t) % 3, :], b2b[:, :], ALU.add).then_inc(s_rd, 1)

                with dve.If(l < L - 1):
                    hold(dve, s_lbe, (l + 2) * 16)
                    for t in range(NT):
                        second(t)
                        dve.wait_ge(s_rd, 10 + l * NT + t + 1)
                        V.scalar_tensor_tensor(hin[:, t, :], xs[:, t, :], 0.0, beb[:, :], ALU.max, ALU.add).then_inc(s_sg, 1)
                with dve.If(l > L - 2):
                    dve.wait_ge(s_ldx, 80)
                    for t in range(NT):
                        second(t)
                        dve.wait_ge(s_rd, 10 + (L - 1) * NT + t + 1)
                        V.scalar_tensor_tensor(xs[:, t, :], xs[:, t, :], 0.0, xres[:, t, :], ALU.max, ALU.add).then_inc(s_res, 1)
                        dve.wait_ge(s_res, t * 3 + 1)
                        V.bn_stats(st[:, t, :], xs[:, t, :]).then_inc(s_res, 1)
                        dve.wait_ge(s_res, t * 3 + 2)
                        V.bn_aggr(mv[:, t, :], st[:, t, :]).then_inc(s_res, 1)
                chain.leave(L)
            dve.wait_ge(s_res, 3 * NT)
            V.tensor_scalar(t0[:, :], mv[:, :, 1], LN_EPS, None, ALU.add).then_inc(s_ln, 1)
            dve.wait_ge(s_lnq, 2)
            rsqrt_step()
            for t in range(NT):
                V.tensor_scalar(hin[:, t, :], xs[:, t, :], mv[:, t, 0:1], t1[:, t:t + 1], ALU.subtract, ALU.mult).then_inc(s_xn, 1)
            dve.wait_ge(s_lg, 1)
            chain(V.tensor_copy(lg[:, :, :].rearrange("p t e -> p (t e)")[:, 0:D], ps[:, 0, :]))
            chain(V.tensor_copy(lg[:, :, :].rearrange("p t e -> p (t e)")[:, D:NT * NX], ps[:, 1, 0:NT * NX - D]))
            for t in range(NT):
                chain.mark(V.max(m8[:, t, :], lg[:, t, :]))
            chain.wait()
            dve.sem_inc(s_gat, 1)
            for t in range(NT):
                chain.mark(V.max_index(i8[:, t, :], m8[:, t, :], lg[:, t, :]))
            chain.wait()
            chain(V.tensor_copy(i8f[:, :, :], i8[:, :, :]))
            def shared(u):
                q, c = divmod(u, KC)
                n = nodes_of(q)
                v = h1T[:, c, q * QN:q * QN + n]
                dve.wait_ge(s_ssg, u + 1)
                chain(V.tensor_tensor(v, shsig[:, u % 2, 0:n], ps[:, 4 + u % 2 * 2, 0:n], ALU.mult))
                V.tensor_tensor(v, v, ps[:, 5 + u % 2 * 2, 0:n], ALU.mult).then_inc(s_shh, 1)

            shared(0)
            every = [P, NT, NX]
            for k in range(KX):
                chain(V.tensor_tensor(oh[k][:, :, :], lane[:, 0:NX].unsqueeze(1).broadcast_to(every),
                                      i8f[:, :, k:k + 1].broadcast_to(every), ALU.is_equal))
                chain(V.tensor_scalar(oh[k][:, NT - 1, :], oh[k][:, NT - 1, :], valid[:, :], None, ALU.mult))
            chain(V.tensor_tensor(both[:, :, :], oh[0][:, :, :], oh[1][:, :, :], ALU.add))
            chain(V.memset(run[:, 0, :], 0.0))
            for t in range(NT):
                chain(V.tensor_tensor(run[:, t + 1, :], run[:, t, :], both[:, t, :], ALU.add))
            V.tensor_scalar(b128[:, :], lane[:, 0:NX], float(P), None, ALU.mult).then_inc(s_run, 1)

            shared(1)
            shared(2)
            dve.wait_ge(s_pos, 1)
            flat = pos[:, :, :].rearrange("p t e -> p (t e)")
            chain.mark(V.tensor_copy(flat[:, 0:D], ps[:, 2, :]))
            chain.mark(V.tensor_copy(flat[:, D:NT * NX], ps[:, 3, 0:NT * NX - D]))
            chain(V.tensor_copy(cntx[:, :], ps[:, 3, 256:256 + NX]))
            chain(V.tensor_scalar(ovn[:, :], cntx[:, :], float(P - 1), None, ALU.add))
            chain(V.tensor_copy(ovnI[:, :], ovn[:, :]))
            chain(V.tensor_scalar(ovnI[:, :], ovnI[:, :], 7, None, ALU.arith_shift_right))
            chain(V.tensor_copy(ovn[:, :], ovnI[:, :]))
            chain(V.tensor_scalar(ovn[:, :], ovn[:, :], -1.0, 0.0, ALU.add, ALU.max))
            chain(V.tensor_tensor_scan(ovs[:, :], ovn[:, :], zrow[:, 0:NX], 0.0, ALU.add, ALU.add))
            chain(V.tensor_copy(nov[:, :], ovs[:, NX - 1:NX]))
            chain(V.tensor_tensor(bdif[:, :], ovs[:, :], ovn[:, :], ALU.subtract))
            chain(V.tensor_scalar(bdif[:, :], bdif[:, :], float(NX - 1), float(P), ALU.add, ALU.mult))
            chain(V.tensor_tensor(bdif[:, :], bdif[:, :], b128[:, :], ALU.subtract))
            shared(3)
            chain(V.tensor_scalar(slotm[:, :, :], pos[:, :, :], float(P), None, ALU.is_ge))
            chain(V.tensor_tensor(slotm[:, :, :], slotm[:, :, :], bdif[:, :].unsqueeze(1).broadcast_to(every), ALU.mult))
            chain(V.tensor_tensor(slotm[:, :, :], slotm[:, :, :], b128[:, :].unsqueeze(1).broadcast_to(every), ALU.add))
            chain(V.tensor_tensor(slotm[:, :, :], slotm[:, :, :], pos[:, :, :], ALU.add))
            for k in range(KX):
                shared(4 + k)
                chain(V.tensor_tensor(lg[:, :, :], oh[k][:, :, :], slotm[:, :, :], ALU.mult))
                chain(V.tensor_reduce(sel[:, k, :], lg[:, :, :], AX.X, ALU.add))
                chain(V.tensor_tensor(lg[:, :, :], oh[k][:, :, :], pos[:, :, :], ALU.mult))
                chain(V.tensor_reduce(selp[:, k, :], lg[:, :, :], AX.X, ALU.add))
            chain.mark(V.tensor_copy(slotx[:, :, :], sel[:, :, :]))
            chain(V.tensor_copy(selI[:, :, :], sel[:, :, :]))
            chain(V.tensor_scalar(hiI[:, :, :], selI[:, :, :], 7, None, ALU.arith_shift_right))
            chain(V.tensor_scalar(selI[:, :, :], selI[:, :, :], P - 1, None, ALU.bitwise_and))
            V.scalar_tensor_tensor(tabx[:, :, :], selI[:, :, :], float(XT), hiI[:, :, :], ALU.mult, ALU.add).then_inc(s_tabx, 1)
            dve.wait_ge(s_sgm, 1)
            chain(V.tensor_tensor(gden[:, :], sgm[:, :, 0], sgm[:, :, 1], ALU.add))
            chain(V.tensor_scalar(gden[:, :], gden[:, :], 1e-20, None, ALU.add))
            chain(V.reciprocal(gden[:, :], gden[:, :]))
            chain(V.tensor_scalar(selp[:, :, :], selp[:, :, :], float(CAP), SCALE, ALU.is_lt, ALU.mult))
            for k in range(KX):
                chain(V.tensor_tensor(gate[:, k, :], sgm[:, :, k], gden[:, :], ALU.mult))
                chain(V.tensor_tensor(gate[:, k, :], gate[:, k, :], selp[:, k, :], ALU.mult))
            shared(4 + KX)
            ovall = [P, XOVER, NX]
            chain(V.tensor_tensor(cmpx[:, :, :], lane[:, 0:XOVER].unsqueeze(2).broadcast_to(ovall),
                                  ovs[:, :].unsqueeze(1).broadcast_to(ovall), ALU.is_ge))
            chain(V.tensor_reduce(eovF[:, :], cmpx[:, :, :], AX.X, ALU.add))
            chain(V.tensor_scalar(eovF[:, :], eovF[:, :], float(NX - 1), None, ALU.min))
            V.tensor_copy(eovI[:, :], eovF[:, :]).then_inc(s_xrt, 1)
            for u in range(5 + KX, 16):
                shared(u)

            def shared_sum(t):
                dve.wait_ge(s_so, t + 1)
                V.tensor_tensor(xs[:, t, :], xs[:, t, :], ps[:, 2 + t % 2, :], ALU.add).then_inc(s_sod, 1)

            for t in range(EARLY):
                shared_sum(t)

            def hidden(j, k):
                dve.wait_ge(s_sig, j + 1)
                at_least(dve, s_th, j - 1)
                V.tensor_tensor(hh[:, k % 2, :], sg[:, k % 2, :], ps[:, 2 + k % 2, 0:HX], ALU.mult).then_inc(s_hm, 1)
                dve.wait_ge(s_hm, j + 1)
                V.tensor_tensor(hh[:, k % 2, :], hh[:, k % 2, :], ps[:, 2 + k % 2, HX:2 * HX], ALU.mult).then_inc(s_hh, 1)

            def hidden_turned(j, k):
                dve.wait_ge(s_th, j + 1)
                at_least(dve, s_g2, j - 1)
                hold(dve, s_th, j + 1)
                V.tensor_copy(hT[:, k % 2, :, :].rearrange("p k n -> p (k n)"), ps[:, 4 + k % 2, 0:XC * P]).then_inc(s_ht, 1)

            def step(g, k):
                j = g * WR + k
                static = isinstance(j, int)
                if not static or j < NX:
                    hidden(j, k)
                    hidden_turned(j, k)

            for k in range(WR):
                step(0, k)
            with dve.Fori(1, NX // WR) as g:
                for k in range(WR):
                    step(g, k)
            over = dve.value_load(nov[0:1, 0:1], min_val=0, max_val=XOVER)
            with dve.If(over > 0):
                with dve.Fori(0, XOVER) as o:
                    dve.wait_ge(s_va, o * 3 + 2)
                    V.tensor_tensor(hh[:, 0, :], sg[:, 0, :], ps[:, 2, 0:HX], ALU.mult).then_inc(s_vd, 1)
                    dve.wait_ge(s_vd, o * 3 + 1)
                    V.tensor_tensor(hh[:, 0, :], hh[:, 0, :], ps[:, 2, HX:2 * HX], ALU.mult).then_inc(s_vd, 1)
                    hold(dve, s_vp, o * 4 + 3)
                    V.tensor_copy(hT[:, 0, :, :].rearrange("p k n -> p (k n)"), ps[:, 4, 0:XC * P]).then_inc(s_vd, 1)
            for u in range(KX * NT):
                t, k = u // KX, u % KX
                n = min(P, N - t * P)
                if k == 0:
                    for late in range(EARLY, NT):
                        if t == max(0, 5 * (late - EARLY) // 3 - 2):
                            shared_sum(late)
                    dve.wait_ge(s_sod, t + 1)
                dve.wait_ge(s_yg[u % RING], 16 * (u // RING + 1))
                if k:
                    dve.wait_ge(s_fa2, u)
                last = V.scalar_tensor_tensor(xs[0:n, t, :], ring[0:n, u % RING, :], gate[0:n, k, t:t + 1], xs[0:n, t, :],
                                              ALU.mult, ALU.add)
                last.then_inc(s_fa2, 1)
                if k:
                    dve.wait_ge(s_fa2, u + 1)
                    dve.sem_inc(s_fa, 1)

        @block.tensor
        def _(pe):
            T = nc.tensor
            pe.wait_ge(s_rot, 1)
            pe.wait_ge(s_const, 6)
            T.matmul(ps[0:EP, 0, 0:NT], below[0:EP, 0:EP], rowtot[:, 0:NT], start=True, stop=True).then_inc(s_cntp, 1)
            T.matmul(ps[:, 1, 0:NT + 1], ones[0:EP, :], rowtot[:, :], start=True, stop=True).then_inc(s_cntp, 1)
            pe.wait_ge(s_rsel, 1)
            needed = [pe.value_load(flagI[0:1, h:h + 1], min_val=0, max_val=HALF_MAX) for h in range(2)]
            pe.wait_ge(s_rowg, 16 * NCH)
            for f in range(3):
                for c in range(NCH):
                    n = min(P, COLS - c * P)
                    last = T.transpose(ps[:, f, c * P:c * P + n], ring[0:n, c, :].rearrange("p (e f) -> p f e", f=REC)[:, f, :],
                                       ident[0:n, 0:n])
            last.then_inc(s_plane, 1)
            pe.wait_ge(s_ldv, 48)
            T.transpose(ps[:, 7, 0:3 * L * KC], vrows[:, :], ident[0:3 * L * KC, 0:3 * L * KC]).then_inc(s_vt, 1)
            pe.wait_ge(s_gw, 16)
            for k in range(KC):
                last = T.transpose(ps[:, 6, k * NX:(k + 1) * NX], gw[:, :].rearrange("e (p k) -> e k p", k=KC)[:, k, :], ident[0:NX, 0:NX])
            last.then_inc(s_gt4, 1)
            pe.wait_ge(s_tab, 2)
            pe.wait_ge(s_zro, 1)
            pe.sem_inc(s_ou[0], 1)
            pe.sem_inc(s_ou[1], 1)

            def warm():
                for i in range(WARM):
                    T.matmul(ps[:, i % 2, :], zeros_h[:, 0:P], zeros_h[:, :], start=True, stop=True, skip_group_check=True)

            with pe.Fori(0, L) as l:
                def clear(h):
                    for b in range(HB):
                        if h == 1:
                            pe.wait_ge(s_hin, 1 + l * NT + b + 1)
                        T.matmul(ps[:, b, :], zeros_h[:, 0:P], zeros_h[:, :], start=True, stop=False, skip_group_check=True)
                        if h == 1 and b < 3:
                            turn_in(b, b)

                def add(t, k):
                    bank = pe.value_load(bankI[0:1, bass.ds(t, 1)], min_val=0, max_val=HB - 1)
                    pe.wait_ge(s_m, (l * MT + t + 1) * 2)
                    T.matmul(ps[:, bass.ds(bank, 1), :], oneh[:, k, :], ring[:, k, :], start=False, stop=False,
                             skip_group_check=True).then_inc(s_free, 1)

                def freed(u):
                    if u < 3:
                        pe.wait_ge(s_rd, 10 + l * NT + u - 3 + 1)
                    elif u - 3 < FILL_ACT:
                        pe.wait_ge(s_ra, l * FILL_ACT + u - 3 + 1)
                    else:
                        pe.wait_ge(s_rd, 10 + l * NT + u - 3 - FILL_ACT + 1)

                def overflow(h):
                    with pe.If(needed[h] > MAIN[h]):
                        with pe.Fori(0, OVER[h]) as o:
                            bank = pe.value_load(bankI[0:1, bass.ds(o + OV0[h], 1)], min_val=0, max_val=HB - 1)
                            pe.wait_ge(s_om[h], l * OVER[h] + o + 1)
                            T.matmul(ps[:, bass.ds(bank, 1), :], ovh[:, :], ovx[:, :], start=False, stop=False,
                                     skip_group_check=True).then_inc(s_ou[h], 1)

                def turn_in(t, use):
                    pe.wait_ge(s_hin, 1 + l * NT + t + 1)
                    freed(use)
                    for k in range(KC):
                        last = T.transpose(ps[:, 5 + use % 3, k * P:(k + 1) * P],
                                           hin[:, t, :].rearrange("p (d k) -> p k d", k=KC)[:, k, :], ident[:, :])
                    last.then_inc(s_tr, 1)

                def product(h, q, c, bank):
                    n = nodes_of(h * 2 + q) if h else QN
                    for k in range(KC):
                        last = T.matmul(ps[:, bank, 0:n], w1s[:, k, c * P:(c + 1) * P],
                                        hinT[:, k, bass.ds(q * QN + h * HB * P, n)], start=k == 0, stop=k == KC - 1)
                    last.then_inc(s_tr, 1)

                clear(0)
                with pe.Fori(0, MAIN[0] // RING) as g:
                    for k in range(RING):
                        add(g * RING + k, k)
                for t in range(MAIN[0] // RING * RING, MAIN[0]):
                    add(t, t % RING)
                overflow(0)
                clear(1)
                for t in range(PRE):
                    add(MAIN[0] + t, (MAIN[0] + t) % RING)
                    if t == RING // 2 + RING - 1:
                        for b in range(3, HB):
                            turn_in(b, b)
                hold(pe, s_lw1, (l + 1) * 16)
                with pe.Fori(0, 2) as q:
                    for c in range(KC):
                        for k in range(RING):
                            add(MAIN[0] + PRE + (q * KC + c) * RING + k, (MAIN[0] + k) % RING)
                            if k == RING // 2 - 1:
                                pe.wait_ge(s_ra, l * FILL_ACT + q * KC + c + HB + (0 if c < 1 else -1))
                                product(0, q, c, 6 + c % 2)
                for t in range(MAIN[0] + PRE + BODY, MT):
                    add(t, t % RING)
                overflow(1)
                pe.wait_ge(s_ra, l * FILL_ACT + FILL_HALF)
                for b in range(HB):
                    turn_in(HB + b, FILL_HALF + b)
                for q in range(2):
                    pe.wait_ge(s_ra, l * FILL_ACT + FILL_HALF + (3 if q == 0 else HB))
                    for c in range(KC):
                        use = FILL_HALF + HB + q * KC + c
                        freed(use)
                        product(1, q, c, 5 + use % 3)
                warm()
                pe.wait_ge(s_lw2, (l + 1) * 32)
                use = FILL_ACT
                for t in range(NT):
                    part = [a >= min(N, (t + 1) * P) for a in PARTS[1:]].index(True)
                    pe.wait_ge(s_gt, l * 16 + KC * (part + 1))
                    freed(use)
                    for k in range(KC):
                        last = T.matmul(ps[:, 5 + use % 3, :], h1T[:, k, t * P:(t + 1) * P], w2s[:, k, :],
                                        start=k == 0, stop=k == KC - 1)
                    last.then_inc(s_tr, 1)
                    use += 1
            warm()
            for t in range(NT):
                pe.wait_ge(s_xn, t + 1)
                at_least(pe, s_ra2, t - 2)
                for k in range(KC):
                    last = T.transpose(ps[:, 5 + t % 3, k * P:(k + 1) * P],
                                       hin[:, t, :].rearrange("p (d k) -> p k d", k=KC)[:, k, :], ident[:, :])
                last.then_inc(s_tr2, 1)
            for t in range(NT):
                pe.wait_ge(s_ra2, t + 1)
                for k in range(KC):
                    last = T.matmul(ps[:, t // 8, t % 8 * NX:(t % 8 + 1) * NX], hinT[:, k, t * P:(t + 1) * P], gT[:, k, :],
                                    start=k == 0, stop=k == KC - 1)
            last.then_inc(s_lg, 1)
            pe.wait_ge(s_swl, 48)

            def shared_up(u):
                q, c = divmod(u, KC)
                n = nodes_of(q)
                at_least(pe, s_shh, u - 1)
                for v, w in ((4, w1s), (5, w3s)):
                    for k in range(KC):
                        last = T.matmul(ps[:, v + u % 2 * 2, 0:n], w[:, k, c * P:(c + 1) * P], hinT[:, k, q * QN:q * QN + n],
                                        start=k == 0, stop=k == KC - 1)
                last.then_inc(s_sp, 1)

            for u in range(3):
                shared_up(u)
            pe.wait_ge(s_run, 1)
            for t in range(NT):
                o = ps[:, 2 + t // 8, t % 8 * NX:(t % 8 + 1) * NX]
                T.matmul(o, below[:, :], both[:, t, :], start=True, stop=False)
                T.matmul(o, ones[:, :], run[:, t, :], start=False, stop=True)
            T.matmul(ps[:, 3, 256:256 + NX], ones[:, :], run[:, NT, :], start=True, stop=True).then_inc(s_pos, 1)
            for u in range(3, 16):
                shared_up(u)
            def shared_down(t):
                pe.wait_ge(s_shh, KC * (((t + 1) * P - 1) // QN + 1))
                at_least(pe, s_sod, t - 1)
                for k in range(KC):
                    last = T.matmul(ps[:, 2 + t % 2, :], h1T[:, k, t * P:(t + 1) * P], w2s[:, k, :], start=k == 0, stop=k == KC - 1)
                last.then_inc(s_so, 1)


            def turn_x(k):
                for c in range(KC):
                    last = T.transpose(ps[:, k % 2, c * P:(c + 1) * P],
                                       xe[:, k, :].rearrange("p (d k) -> p k d", k=KC)[:, c, :], ident[:, :])
                return last

            def up(k):
                for c in range(KC):
                    last = T.matmul(ps[:, 2 + k % 2, :], xeT[:, k % 2, c, :], w13[:, k, c, :, :].rearrange("p a n -> p (a n)"),
                                    start=c == 0, stop=c == KC - 1)
                return last

            def turn_h(k):
                for c in range(XC):
                    last = T.transpose(ps[:, 4 + k % 2, c * P:(c + 1) * P],
                                       hh[:, k % 2, :].rearrange("p (d k) -> p k d", k=XC)[:, c, :], ident[:, :])
                return last

            def down(k):
                for c in range(XC):
                    last = T.matmul(ps[:, 6 + k % 2, :], hT[:, k % 2, c, :], w2e[:, k, c, :], start=c == 0, stop=c == XC - 1)
                return last

            def turned(j, k, turn):
                pe.wait_ge(s_xg[k], (turn + 1) * 16)
                at_least(pe, s_xt, j - 1)
                turn_x(k).then_inc(s_tx, 1)

            def step(g, k):
                j = g * WR + k
                static = isinstance(j, int)
                if not static or j < NX:
                    pe.wait_ge(s_xt, j + 1)
                    pe.wait_ge(s_w[k], (g + 1) * 48)
                    at_least(pe, s_hh, j - 1)
                    up(k).then_inc(s_g1, 1)
                if not static or j + 1 < NX:
                    turned(j + 1, (k + 1) % WR, g + (k + 1) // WR)
                if not static or j >= 1:
                    at_least(pe, s_ht, j)
                    at_least(pe, s_yc, j - 2)
                    down((k - 1) % WR).then_inc(s_g2, 1)
                if not static or j < NX:
                    pe.wait_ge(s_hh, j + 1)
                    at_least(pe, s_ht, j - 1)
                    turn_h(k).then_inc(s_th, 1)

            for t in range(EARLY):
                if t == EARLY - 1:
                    turned(0, 0, 0)
                shared_down(t)
            for k in range(WR):
                if k < 2:
                    pe.wait_ge(s_sod, EARLY - 1 + k)
                step(0, k)
            with pe.Fori(1, NX // WR - 1) as g:
                for k in range(WR):
                    step(g, k)
            for k in range(WR + 1):
                step(NX // WR - 1 + k // WR, k % WR)
            pe.wait_ge(s_xrt, 1)
            over = pe.value_load(nov[0:1, 0:1], min_val=0, max_val=XOVER)
            with pe.If(over > 0):
                with pe.Fori(0, XOVER) as o:
                    pe.wait_ge(s_vg, o * 16 + 16)
                    turn_x(0).then_inc(s_vp, 1)
                    pe.wait_ge(s_va, o * 3 + 1)
                    pe.wait_ge(s_vw, o * 48 + 48)
                    up(0).then_inc(s_vp, 1)
                    pe.wait_ge(s_vd, o * 3 + 2)
                    turn_h(0).then_inc(s_vp, 1)
                    pe.wait_ge(s_vd, o * 3 + 3)
                    down(0).then_inc(s_vp, 1)
            pe.wait_ge(s_hh, NX)
            with pe.If(over > 0):
                pe.wait_ge(s_va, 3 * XOVER)
            for t in range(EARLY, NT):
                shared_down(t)


CH_LAYER = 16 + 4 + 6

_INS = ["x", "src", "dst", "edge_weight1", "L0_gnn_eps", "L0_gnn_We", "L0_gnn_be", "L0_gnn_W1", "L0_gnn_b1",
        "L0_gnn_gamma", "L0_gnn_beta", "L0_gnn_W2", "L0_gnn_b2", "L0_ffn_gate_w", "L0_ffn_w1", "L0_ffn_w3",
        "L0_ffn_w2", "L0_ffn_sw1", "L0_ffn_sw3", "L0_ffn_sw2"]


def kernel(**inputs):
    import numpy as np
    import concourse.bacc as bacc
    from concourse.bass_utils import run_bass_kernel_spmd as run

    nc = bacc.Bacc("TRN2", target_bir_lowering=False, num_devices=1)
    arrays, args = {}, []
    for name in _INS:
        a = np.ascontiguousarray(inputs[name])
        arrays[f"in_{name}"] = a
        args.append(nc.dram_tensor(f"in_{name}", a.shape, mybir.dt.from_np(a.dtype), kind="ExternalInput").ap())
    out = nc.dram_tensor("out", (N, D), F32, kind="ExternalOutput").ap()
    scratch = [nc.dram_tensor("x_rows", (NP, D), F32).ap(), nc.dram_tensor("records", (RROWS, P * REC), F32).ap(),
               nc.dram_tensor("token_rows", (NP, D), F32).ap(), nc.dram_tensor("token_table", (P * XT, 1), I32).ap(),
               nc.dram_tensor("expert_rows", (XT * P, D), F32).ap()]
    build(nc, *args, out, scratch)
    return run(nc, [arrays], core_ids=[0]).results[0]["out"]
```
